# Optimizing a Trainium2 kernel written in Bass

```python
import numpy as np
import jax
import jax.numpy as jnp

def _softmax(x, axis=-1):
    return jax.nn.softmax(x, axis=axis)

def _gelu(x):
    return jax.nn.gelu(x, approximate=True)

def _silu(x):
    return jax.nn.silu(x)

def _sigmoid(x):
    return jax.nn.sigmoid(x)

def _layernorm(x, axis=-1, eps=1e-05):
    m = jnp.mean(x, axis=axis, keepdims=True)
    v = jnp.var(x, axis=axis, keepdims=True)
    return (x - m) / jnp.sqrt(v + eps)

def _scatter_add(tgt, idx, src, axis=0):
    return tgt.at[idx].add(src)

def _segment_sum(src, seg, n):
    return jax.ops.segment_sum(src, seg, n)
kernel_name = 'mk_recurrent_d4_jaxref_r8_cc080b'

def setup_inputs(seed: int=0):
    np.random.seed(seed)
    _w = jnp.asarray

    def _L0_attn_setup():
        import jax, jax.numpy as jnp
        import numpy as np
        CHUNK = 32
        NUM_HEADS = 4
        HEAD_K = 32
        HEAD_V = 32
        EPS = 1e-05

        def l2norm(x, eps=1e-06):
            return x * jax.lax.rsqrt(jnp.sum(x * x, axis=-1, keepdims=True) + eps)

        def causal_depthwise_conv(x, w):
            K = w.shape[1]
            l = x.shape[1]
            xp = jnp.pad(x, ((0, 0), (K - 1, 0), (0, 0)))
            return sum((w[:, k] * xp[:, k:k + l, :] for k in range(K)))

        def delta_rule_chunkwise(q, k, v, beta):
            b, h, l, dk = q.shape
            dv = v.shape[-1]
            c = CHUNK
            n = l // c
            q = l2norm(q)
            k = l2norm(k)
            v = v * beta[..., None]
            k_beta = k * beta[..., None]
            resh = lambda x: x.reshape(b, h, n, c, x.shape[-1])
            q, k, v, k_beta = map(resh, (q, k, v, k_beta))
            tri_strict = jnp.tril(jnp.ones((c, c), dtype=q.dtype), -1)
            attn = -(k_beta @ jnp.swapaxes(k, -1, -2)) * tri_strict

            def body(i, a):
                row = a[..., i, :]
                upd = jnp.einsum('bhnj,bhnjk->bhnk', row, a)
                return a.at[..., i, :].add(upd)
            attn = jax.lax.fori_loop(1, c, body, attn)
            attn = attn + jnp.eye(c, dtype=attn.dtype)
            u = attn @ v
            w = attn @ k_beta
            mask_causal = jnp.tril(jnp.ones((c, c), dtype=q.dtype), 0)
            S0 = jnp.zeros((b, h, dk, dv), dtype=q.dtype)
            to_front = lambda x: jnp.moveaxis(x, 2, 0)

            def step(S, inp):
                q_i, k_i, u_i, w_i = inp
                attn_i = q_i @ jnp.swapaxes(k_i, -1, -2) * mask_causal
                u_new = u_i - w_i @ S
                o_i = q_i @ S + attn_i @ u_new
                S = S + jnp.swapaxes(k_i, -1, -2) @ u_new
                return (S, o_i)
            S, o = jax.lax.scan(step, S0, (to_front(q), to_front(k), to_front(u), to_front(w)))
            o = jnp.moveaxis(o, 0, 2).reshape(b, h, l, dv)
            return (o, S)
        key = jax.random.key(seed)
        ks = jax.random.split(key, 12)
        b, l, d = (4, 512, 128)
        sc = 0.02
        return {'hidden_states': jax.random.normal(ks[0], (b, l, d), jnp.float32), 'Wq': jax.random.normal(ks[1], (128, 128), jnp.float32) * sc, 'Wk': jax.random.normal(ks[2], (128, 128), jnp.float32) * sc, 'Wv': jax.random.normal(ks[3], (128, 128), jnp.float32) * sc, 'conv_q': jax.random.normal(ks[4], (128, 4), jnp.float32) * 0.1, 'conv_k': jax.random.normal(ks[5], (128, 4), jnp.float32) * 0.1, 'conv_v': jax.random.normal(ks[6], (128, 4), jnp.float32) * 0.1, 'Wb': jax.random.normal(ks[7], (4, 128), jnp.float32) * sc, 'Wmix': jax.random.normal(ks[8], (4, 128), jnp.float32) * sc, 'norm_w': jnp.ones((32,), jnp.float32), 'Wo': jax.random.normal(ks[9], (128, 128), jnp.float32) * sc}
    _L0_attn_in = _L0_attn_setup()

    def _L0_ffn_setup():
        import jax, jax.numpy as jnp
        import numpy as np
        D_MODEL = 128
        NHEAD = 16
        HEAD_DIM = D_MODEL // NHEAD
        FF = 256
        NUM_EXPERTS = 8
        EPS = 1e-05

        def _ln(x, g, b):
            m = x.mean(-1, keepdims=True)
            v = ((x - m) ** 2).mean(-1, keepdims=True)
            return (x - m) / jnp.sqrt(v + EPS) * g + b

        def _attention(src, Wq, bq, Wk, bk, Wv, bv, Wo, bo):
            B, T, d = src.shape
            scale = HEAD_DIM ** (-0.5)
            q = (src @ Wq + bq).reshape(B, T, NHEAD, HEAD_DIM)
            k = (src @ Wk + bk).reshape(B, T, NHEAD, HEAD_DIM)
            v = (src @ Wv + bv).reshape(B, T, NHEAD, HEAD_DIM)
            scores = jnp.einsum('bqhd,bkhd->bhqk', q, k) * scale
            probs = jax.nn.softmax(scores, axis=-1)
            out = jnp.einsum('bhqk,bkhd->bqhd', probs, v).reshape(B, T, d)
            return out @ Wo + bo

        def _moe(x, gW, gb, W1, b1, W2, b2):
            B, T, d = x.shape
            xf = x.reshape(-1, d)
            gates = jax.nn.softmax(xf @ gW + gb, axis=-1)
            top2_scores, top2_idx = jax.lax.top_k(gates, 2)
            w = (jax.nn.one_hot(top2_idx, NUM_EXPERTS, dtype=xf.dtype) * top2_scores[..., None]).sum(1)
            h = jax.nn.relu(jnp.einsum('nd,edf->enf', xf, W1) + b1[:, None, :])
            y = jnp.einsum('enf,efd->end', h, W2) + b2[:, None, :]
            out = jnp.einsum('ne,end->nd', w, y)
            return out.reshape(B, T, d)
        key = jax.random.key(seed)
        ks = jax.random.split(key, 12)
        s = 0.02
        d, f, E = (D_MODEL, FF, NUM_EXPERTS)
        return {'src': jax.random.normal(ks[0], (8, 64, d), dtype=jnp.float32), 'Wq': jax.random.normal(ks[1], (d, d), dtype=jnp.float32) * s, 'bq': jnp.zeros((d,), jnp.float32), 'Wk': jax.random.normal(ks[2], (d, d), dtype=jnp.float32) * s, 'bk': jnp.zeros((d,), jnp.float32), 'Wv': jax.random.normal(ks[3], (d, d), dtype=jnp.float32) * s, 'bv': jnp.zeros((d,), jnp.float32), 'Wo': jax.random.normal(ks[4], (d, d), dtype=jnp.float32) * s, 'bo': jnp.zeros((d,), jnp.float32), 'gW': jax.random.normal(ks[5], (d, E), dtype=jnp.float32) * s, 'gb': jnp.zeros((E,), jnp.float32), 'W1': jax.random.normal(ks[6], (E, d, f), dtype=jnp.float32) * s, 'b1': jnp.zeros((E, f), jnp.float32), 'W2': jax.random.normal(ks[7], (E, f, d), dtype=jnp.float32) * s, 'b2': jnp.zeros((E, d), jnp.float32), 'ln1_g': jnp.ones((d,), jnp.float32), 'ln1_b': jnp.zeros((d,), jnp.float32), 'ln2_g': jnp.ones((d,), jnp.float32), 'ln2_b': jnp.zeros((d,), jnp.float32)}
    _L0_ffn_in = _L0_ffn_setup()

    def _L1_attn_setup():
        import jax, jax.numpy as jnp
        from jax import lax
        import numpy as np
        B, S, D = (4, 256, 128)
        D_INNER, D_STATE, D_CONV = (256, 16, 4)

        def silu(v):
            return v * jax.nn.sigmoid(v)
        key = jax.random.key(seed)
        ks = jax.random.split(key, 7)
        return {'x': jax.random.normal(ks[0], (B, S, D), jnp.float32), 'w_in': jax.random.normal(ks[1], (D, 2 * D_INNER), jnp.float32) * 0.02, 'conv_w': jax.random.normal(ks[2], (D_INNER, 1, D_CONV), jnp.float32) * 0.1, 'conv_b': jax.random.normal(ks[3], (D_INNER,), jnp.float32) * 0.01, 'w_B': jax.random.normal(ks[4], (D_INNER, D_STATE), jnp.float32) * 0.02, 'w_C': jax.random.normal(ks[5], (D_STATE, D_INNER), jnp.float32) * 0.02, 'w_out': jax.random.normal(ks[6], (D_INNER, D), jnp.float32) * 0.02}
    _L1_attn_in = _L1_attn_setup()

    def _L1_ffn_setup():
        import jax, jax.numpy as jnp
        import numpy as np
        B, T, C, H, E = (4, 256, 128, 256, 8)
        CAPACITY_FACTOR = 1.0
        key = jax.random.key(seed)
        ks = jax.random.split(key, 5)
        scale = 0.02
        return {'x': jax.random.normal(ks[0], (B, T, C), dtype=jnp.float32), 'Wg': jax.random.normal(ks[1], (E, C), dtype=jnp.float32) * scale, 'W1': jax.random.normal(ks[2], (E, H, C), dtype=jnp.float32) * scale, 'W2': jax.random.normal(ks[3], (E, C, H), dtype=jnp.float32) * scale, 'W3': jax.random.normal(ks[4], (E, H, C), dtype=jnp.float32) * scale}
    _L1_ffn_in = _L1_ffn_setup()

    def _L2_attn_setup():
        import jax, jax.numpy as jnp
        import numpy as np
        KERNEL_SIZE = 16

        def _pad_amounts(kernel_size):
            side = (kernel_size - 1) // 2
            if (kernel_size - 1) % 2:
                return (side, side + 1)
            return (side, side)
        key = jax.random.key(seed)
        k1, k2, k3, k4 = jax.random.split(key, 4)
        B, T, H = (4, 256, 128)
        inputs = jax.random.normal(k1, (B, T, H), dtype=jnp.float32)
        w1 = jax.random.normal(k2, (H, H), dtype=jnp.float32) / np.sqrt(H)
        w2 = jax.random.normal(k3, (H, H), dtype=jnp.float32) / np.sqrt(H)
        v = jax.random.normal(k4, (H, 1), dtype=jnp.float32) / np.sqrt(H)
        return {'inputs': inputs, 'w1': w1, 'w2': w2, 'v': v}
    _L2_attn_in = _L2_attn_setup()

    def _L2_ffn_setup():
        import jax, jax.numpy as jnp
        import numpy as np
        LN_EPS = 1e-05

        def layer_norm(x, g, b):
            mu = jnp.mean(x, axis=-1, keepdims=True)
            var = jnp.var(x, axis=-1, keepdims=True)
            return (x - mu) / jnp.sqrt(var + LN_EPS) * g + b

        def balanced_assignment(scores):
            T, E = scores.shape
            C = T // E
            taken = jnp.zeros((T,), dtype=bool)
            parts = []
            for e in range(E):
                s = jnp.where(taken, -jnp.inf, scores[:, e])
                _, idx = jax.lax.top_k(s, C)
                parts.append(idx)
                taken = taken.at[idx].set(True)
            return jnp.concatenate(parts)
        key = jax.random.key(seed)
        ks = jax.random.split(key, 4)
        B, S, D, F, E = (4, 256, 128, 512, 8)
        return {'x': jax.random.normal(ks[0], (B, S, D), dtype=jnp.float32), 'centroids': jax.random.normal(ks[1], (E, D), dtype=jnp.float32) * 0.1, 'ln_g': jnp.ones((D,), dtype=jnp.float32), 'ln_b': jnp.zeros((D,), dtype=jnp.float32), 'w1': jax.random.normal(ks[2], (E, D, F), dtype=jnp.float32) * 0.02, 'b1': jnp.zeros((E, F), dtype=jnp.float32), 'w2': jax.random.normal(ks[3], (E, F, D), dtype=jnp.float32) * 0.02, 'b2': jnp.zeros((E, D), dtype=jnp.float32)}
    _L2_ffn_in = _L2_ffn_setup()

    def _L3_attn_setup():
        import jax, jax.numpy as jnp
        import numpy as np
        N_HEADS = 16
        D_MODEL = 128
        D_HEAD = 64
        BATCH = 4
        SEQ = 256
        IGNORE = -100000.0
        key = jax.random.key(seed)
        ks = jax.random.split(key, 10)
        s = 1.0 / np.sqrt(D_MODEL)
        return {'x': jax.random.normal(ks[0], (BATCH, SEQ, D_MODEL), jnp.float32), 'pos_embed': jax.random.normal(ks[1], (BATCH, SEQ, D_MODEL), jnp.float32), 'W_Q': jax.random.normal(ks[2], (N_HEADS, D_MODEL, D_HEAD), jnp.float32) * s, 'b_Q': jnp.zeros((N_HEADS, D_HEAD), jnp.float32), 'W_K': jax.random.normal(ks[3], (N_HEADS, D_MODEL, D_HEAD), jnp.float32) * s, 'b_K': jnp.zeros((N_HEADS, D_HEAD), jnp.float32), 'W_V': jax.random.normal(ks[4], (N_HEADS, D_MODEL, D_HEAD), jnp.float32) * s, 'b_V': jnp.zeros((N_HEADS, D_HEAD), jnp.float32), 'W_O': jax.random.normal(ks[5], (N_HEADS, D_HEAD, D_MODEL), jnp.float32) * (1.0 / np.sqrt(D_HEAD)), 'b_O': jnp.zeros((D_MODEL,), jnp.float32)}
    _L3_attn_in = _L3_attn_setup()

    def _L3_ffn_setup():
        import jax, jax.numpy as jnp
        import numpy as np
        DIM = 128
        MOE_INTER = 128
        SHARED_INTER = 128
        N_EXPERTS = 6
        TOP_K = 2
        ROUTE_SCALE = 1.0
        B, S = (8, 512)
        STD = 0.02 / np.sqrt(DIM)
        STD_I = 0.02 / np.sqrt(MOE_INTER)
        key = jax.random.key(seed)
        ks = jax.random.split(key, 10)
        inp = {'x': jax.random.normal(ks[0], (B, S, DIM), dtype=jnp.float32), 'gate_w': jax.random.normal(ks[1], (N_EXPERTS, DIM), dtype=jnp.float32) * STD, 'gate_b': jnp.zeros((N_EXPERTS,), dtype=jnp.float32), 'ew1': jax.random.normal(ks[2], (N_EXPERTS, MOE_INTER, DIM), dtype=jnp.float32) * STD, 'ew2': jax.random.normal(ks[3], (N_EXPERTS, DIM, MOE_INTER), dtype=jnp.float32) * STD_I, 'ew3': jax.random.normal(ks[4], (N_EXPERTS, MOE_INTER, DIM), dtype=jnp.float32) * STD, 'fc1': jax.random.normal(ks[5], (SHARED_INTER, DIM), dtype=jnp.float32) * STD, 'fc2': jax.random.normal(ks[6], (SHARED_INTER, DIM), dtype=jnp.float32) * STD, 'fc3': jax.random.normal(ks[7], (DIM, SHARED_INTER), dtype=jnp.float32) * STD_I}
        return inp
    _L3_ffn_in = _L3_ffn_setup()
    _d = {'L0_attn_hidden_states': _L0_attn_in['hidden_states'], 'L0_attn_Wq': _L0_attn_in['Wq'], 'L0_attn_Wk': _L0_attn_in['Wk'], 'L0_attn_Wv': _L0_attn_in['Wv'], 'L0_attn_conv_q': _L0_attn_in['conv_q'], 'L0_attn_conv_k': _L0_attn_in['conv_k'], 'L0_attn_conv_v': _L0_attn_in['conv_v'], 'L0_attn_Wb': _L0_attn_in['Wb'], 'L0_attn_Wmix': _L0_attn_in['Wmix'], 'L0_attn_norm_w': _L0_attn_in['norm_w'], 'L0_attn_Wo': _L0_attn_in['Wo'], 'L0_ffn_Wq': _L0_ffn_in['Wq'], 'L0_ffn_bq': _L0_ffn_in['bq'], 'L0_ffn_Wk': _L0_ffn_in['Wk'], 'L0_ffn_bk': _L0_ffn_in['bk'], 'L0_ffn_Wv': _L0_ffn_in['Wv'], 'L0_ffn_bv': _L0_ffn_in['bv'], 'L0_ffn_Wo': _L0_ffn_in['Wo'], 'L0_ffn_bo': _L0_ffn_in['bo'], 'L0_ffn_gW': _L0_ffn_in['gW'], 'L0_ffn_gb': _L0_ffn_in['gb'], 'L0_ffn_W1': _L0_ffn_in['W1'], 'L0_ffn_b1': _L0_ffn_in['b1'], 'L0_ffn_W2': _L0_ffn_in['W2'], 'L0_ffn_b2': _L0_ffn_in['b2'], 'L0_ffn_ln1_g': _L0_ffn_in['ln1_g'], 'L0_ffn_ln1_b': _L0_ffn_in['ln1_b'], 'L0_ffn_ln2_g': _L0_ffn_in['ln2_g'], 'L0_ffn_ln2_b': _L0_ffn_in['ln2_b'], 'L1_attn_w_in': _L1_attn_in['w_in'], 'L1_attn_conv_w': _L1_attn_in['conv_w'], 'L1_attn_conv_b': _L1_attn_in['conv_b'], 'L1_attn_w_B': _L1_attn_in['w_B'], 'L1_attn_w_C': _L1_attn_in['w_C'], 'L1_attn_w_out': _L1_attn_in['w_out'], 'L1_ffn_Wg': _L1_ffn_in['Wg'], 'L1_ffn_W1': _L1_ffn_in['W1'], 'L1_ffn_W2': _L1_ffn_in['W2'], 'L1_ffn_W3': _L1_ffn_in['W3'], 'L2_attn_w1': _L2_attn_in['w1'], 'L2_attn_w2': _L2_attn_in['w2'], 'L2_attn_v': _L2_attn_in['v'], 'L2_ffn_centroids': _L2_ffn_in['centroids'], 'L2_ffn_ln_g': _L2_ffn_in['ln_g'], 'L2_ffn_ln_b': _L2_ffn_in['ln_b'], 'L2_ffn_w1': _L2_ffn_in['w1'], 'L2_ffn_b1': _L2_ffn_in['b1'], 'L2_ffn_w2': _L2_ffn_in['w2'], 'L2_ffn_b2': _L2_ffn_in['b2'], 'L3_attn_pos_embed': _L3_attn_in['pos_embed'], 'L3_attn_W_Q': _L3_attn_in['W_Q'], 'L3_attn_b_Q': _L3_attn_in['b_Q'], 'L3_attn_W_K': _L3_attn_in['W_K'], 'L3_attn_b_K': _L3_attn_in['b_K'], 'L3_attn_W_V': _L3_attn_in['W_V'], 'L3_attn_b_V': _L3_attn_in['b_V'], 'L3_attn_W_O': _L3_attn_in['W_O'], 'L3_attn_b_O': _L3_attn_in['b_O'], 'L3_ffn_gate_w': _L3_ffn_in['gate_w'], 'L3_ffn_gate_b': _L3_ffn_in['gate_b'], 'L3_ffn_ew1': _L3_ffn_in['ew1'], 'L3_ffn_ew2': _L3_ffn_in['ew2'], 'L3_ffn_ew3': _L3_ffn_in['ew3'], 'L3_ffn_fc1': _L3_ffn_in['fc1'], 'L3_ffn_fc2': _L3_ffn_in['fc2'], 'L3_ffn_fc3': _L3_ffn_in['fc3']}
    _x0 = _d['L0_attn_hidden_states']
    _d['L0_attn_hidden_states'] = jax.random.normal(jax.random.fold_in(jax.random.key(seed), 1), (16, 256, 128), dtype=_x0.dtype)
    del _x0
    return _d

def reference(L0_attn_hidden_states, L0_attn_Wq, L0_attn_Wk, L0_attn_Wv, L0_attn_conv_q, L0_attn_conv_k, L0_attn_conv_v, L0_attn_Wb, L0_attn_Wmix, L0_attn_norm_w, L0_attn_Wo, L0_ffn_Wq, L0_ffn_bq, L0_ffn_Wk, L0_ffn_bk, L0_ffn_Wv, L0_ffn_bv, L0_ffn_Wo, L0_ffn_bo, L0_ffn_gW, L0_ffn_gb, L0_ffn_W1, L0_ffn_b1, L0_ffn_W2, L0_ffn_b2, L0_ffn_ln1_g, L0_ffn_ln1_b, L0_ffn_ln2_g, L0_ffn_ln2_b, L1_attn_w_in, L1_attn_conv_w, L1_attn_conv_b, L1_attn_w_B, L1_attn_w_C, L1_attn_w_out, L1_ffn_Wg, L1_ffn_W1, L1_ffn_W2, L1_ffn_W3, L2_attn_w1, L2_attn_w2, L2_attn_v, L2_ffn_centroids, L2_ffn_ln_g, L2_ffn_ln_b, L2_ffn_w1, L2_ffn_b1, L2_ffn_w2, L2_ffn_b2, L3_attn_pos_embed, L3_attn_W_Q, L3_attn_b_Q, L3_attn_W_K, L3_attn_b_K, L3_attn_W_V, L3_attn_b_V, L3_attn_W_O, L3_attn_b_O, L3_ffn_gate_w, L3_ffn_gate_b, L3_ffn_ew1, L3_ffn_ew2, L3_ffn_ew3, L3_ffn_fc1, L3_ffn_fc2, L3_ffn_fc3):

    def _L0_attn_ref(hidden_states, Wq, Wk, Wv, conv_q, conv_k, conv_v, Wb, Wmix, norm_w, Wo):
        import jax, jax.numpy as jnp
        import numpy as np
        CHUNK = 32
        NUM_HEADS = 4
        HEAD_K = 32
        HEAD_V = 32
        EPS = 1e-05

        def l2norm(x, eps=1e-06):
            return x * jax.lax.rsqrt(jnp.sum(x * x, axis=-1, keepdims=True) + eps)

        def causal_depthwise_conv(x, w):
            K = w.shape[1]
            l = x.shape[1]
            xp = jnp.pad(x, ((0, 0), (K - 1, 0), (0, 0)))
            return sum((w[:, k] * xp[:, k:k + l, :] for k in range(K)))

        def delta_rule_chunkwise(q, k, v, beta):
            b, h, l, dk = q.shape
            dv = v.shape[-1]
            c = CHUNK
            n = l // c
            q = l2norm(q)
            k = l2norm(k)
            v = v * beta[..., None]
            k_beta = k * beta[..., None]
            resh = lambda x: x.reshape(b, h, n, c, x.shape[-1])
            q, k, v, k_beta = map(resh, (q, k, v, k_beta))
            tri_strict = jnp.tril(jnp.ones((c, c), dtype=q.dtype), -1)
            attn = -(k_beta @ jnp.swapaxes(k, -1, -2)) * tri_strict

            def body(i, a):
                row = a[..., i, :]
                upd = jnp.einsum('bhnj,bhnjk->bhnk', row, a)
                return a.at[..., i, :].add(upd)
            attn = jax.lax.fori_loop(1, c, body, attn)
            attn = attn + jnp.eye(c, dtype=attn.dtype)
            u = attn @ v
            w = attn @ k_beta
            mask_causal = jnp.tril(jnp.ones((c, c), dtype=q.dtype), 0)
            S0 = jnp.zeros((b, h, dk, dv), dtype=q.dtype)
            to_front = lambda x: jnp.moveaxis(x, 2, 0)

            def step(S, inp):
                q_i, k_i, u_i, w_i = inp
                attn_i = q_i @ jnp.swapaxes(k_i, -1, -2) * mask_causal
                u_new = u_i - w_i @ S
                o_i = q_i @ S + attn_i @ u_new
                S = S + jnp.swapaxes(k_i, -1, -2) @ u_new
                return (S, o_i)
            S, o = jax.lax.scan(step, S0, (to_front(q), to_front(k), to_front(u), to_front(w)))
            o = jnp.moveaxis(o, 0, 2).reshape(b, h, l, dv)
            return (o, S)
        x = hidden_states
        b, l, d = x.shape
        h, dk, dv = (NUM_HEADS, HEAD_K, HEAD_V)
        q = jax.nn.silu(causal_depthwise_conv(x @ Wq.T, conv_q))
        k = jax.nn.silu(causal_depthwise_conv(x @ Wk.T, conv_k))
        v = jax.nn.silu(causal_depthwise_conv(x @ Wv.T, conv_v))
        v_token = v.reshape(b, l, h, dv)
        qh = q.reshape(b, l, h, dk).transpose(0, 2, 1, 3)
        kh = k.reshape(b, l, h, dk).transpose(0, 2, 1, 3)
        vh = v_token.transpose(0, 2, 1, 3)
        beta = jax.nn.sigmoid(x @ Wb.T).transpose(0, 2, 1)
        o, S = delta_rule_chunkwise(qh, kh, vh, beta)
        o = o.transpose(0, 2, 1, 3)
        mix = jax.nn.sigmoid(x @ Wmix.T)[..., None]
        o = mix * o + (1.0 - mix) * v_token
        o = o * jax.lax.rsqrt(jnp.mean(o * o, axis=-1, keepdims=True) + EPS) * norm_w
        o = o.reshape(b, l, h * dv) @ Wo.T
        return o

    def _L0_ffn_ref(src, Wq, bq, Wk, bk, Wv, bv, Wo, bo, gW, gb, W1, b1, W2, b2, ln1_g, ln1_b, ln2_g, ln2_b):
        import jax, jax.numpy as jnp
        import numpy as np
        D_MODEL = 128
        NHEAD = 16
        HEAD_DIM = D_MODEL // NHEAD
        FF = 256
        NUM_EXPERTS = 8
        EPS = 1e-05

        def _ln(x, g, b):
            m = x.mean(-1, keepdims=True)
            v = ((x - m) ** 2).mean(-1, keepdims=True)
            return (x - m) / jnp.sqrt(v + EPS) * g + b

        def _attention(src, Wq, bq, Wk, bk, Wv, bv, Wo, bo):
            B, T, d = src.shape
            scale = HEAD_DIM ** (-0.5)
            q = (src @ Wq + bq).reshape(B, T, NHEAD, HEAD_DIM)
            k = (src @ Wk + bk).reshape(B, T, NHEAD, HEAD_DIM)
            v = (src @ Wv + bv).reshape(B, T, NHEAD, HEAD_DIM)
            scores = jnp.einsum('bqhd,bkhd->bhqk', q, k) * scale
            probs = jax.nn.softmax(scores, axis=-1)
            out = jnp.einsum('bhqk,bkhd->bqhd', probs, v).reshape(B, T, d)
            return out @ Wo + bo

        def _moe(x, gW, gb, W1, b1, W2, b2):
            B, T, d = x.shape
            xf = x.reshape(-1, d)
            gates = jax.nn.softmax(xf @ gW + gb, axis=-1)
            top2_scores, top2_idx = jax.lax.top_k(gates, 2)
            w = (jax.nn.one_hot(top2_idx, NUM_EXPERTS, dtype=xf.dtype) * top2_scores[..., None]).sum(1)
            h = jax.nn.relu(jnp.einsum('nd,edf->enf', xf, W1) + b1[:, None, :])
            y = jnp.einsum('enf,efd->end', h, W2) + b2[:, None, :]
            out = jnp.einsum('ne,end->nd', w, y)
            return out.reshape(B, T, d)
        attn_out = _attention(src, Wq, bq, Wk, bk, Wv, bv, Wo, bo)
        x = _ln(src + attn_out, ln1_g, ln1_b)
        ff = _moe(x, gW, gb, W1, b1, W2, b2)
        return _ln(x + ff, ln2_g, ln2_b)

    def _L1_attn_ref(x, w_in, conv_w, conv_b, w_B, w_C, w_out):
        import jax, jax.numpy as jnp
        from jax import lax
        import numpy as np
        B, S, D = (4, 256, 128)
        D_INNER, D_STATE, D_CONV = (256, 16, 4)

        def silu(v):
            return v * jax.nn.sigmoid(v)
        d_inner = conv_w.shape[0]
        d_conv = conv_w.shape[2]
        xz = x @ w_in
        xp, z = jnp.split(xz, 2, axis=-1)
        xc = lax.conv_general_dilated(xp.transpose(0, 2, 1), conv_w, window_strides=(1,), padding=[(d_conv - 1, 0)], dimension_numbers=('NCH', 'OIH', 'NCH'), feature_group_count=d_inner)
        xc = (xc + conv_b[None, :, None]).transpose(0, 2, 1)
        xc = silu(xc)
        h0 = jnp.zeros((xc.shape[0], w_B.shape[1]), xc.dtype)

        def step(h, xt):
            h = h * 0.9 + 0.1 * (xt @ w_B)
            return (h, h @ w_C)
        _, ys = lax.scan(step, h0, xc.transpose(1, 0, 2))
        y = ys.transpose(1, 0, 2) * silu(z)
        return y @ w_out

    def _L1_ffn_ref(x, Wg, W1, W2, W3):
        import jax, jax.numpy as jnp
        import numpy as np
        B, T, C, H, E = (4, 256, 128, 256, 8)
        CAPACITY_FACTOR = 1.0
        b, t, c = x.shape
        e = Wg.shape[0]
        n = b * t
        capacity = max(1, int(CAPACITY_FACTOR * n / e))
        x_flat = x.reshape(n, c)
        scores = (x_flat @ Wg.T).T
        top_vals, token_idx = jax.lax.top_k(scores, capacity)
        token_w = jax.nn.softmax(top_vals, axis=-1)
        xg = x_flat[token_idx]
        h = jax.nn.silu(jnp.einsum('eic,ehc->eih', xg, W1)) * jnp.einsum('eic,ehc->eih', xg, W3)
        y = jnp.einsum('eih,ech->eic', h, W2) * token_w[..., None]
        out = jnp.zeros_like(x_flat).at[token_idx.reshape(-1)].add(y.reshape(-1, c))
        return out.reshape(b, t, c)

    def _L2_attn_ref(inputs, w1, w2, v):
        import jax, jax.numpy as jnp
        import numpy as np
        KERNEL_SIZE = 16

        def _pad_amounts(kernel_size):
            side = (kernel_size - 1) // 2
            if (kernel_size - 1) % 2:
                return (side, side + 1)
            return (side, side)
        B, T, H = inputs.shape
        K = KERNEL_SIZE
        pl, pr = _pad_amounts(K)
        x_pad = jnp.pad(inputs, ((0, 0), (pl, pr), (0, 0)))
        idx = jnp.arange(T)[:, None] + jnp.arange(K)[None, :]
        proj = x_pad @ w2
        local_proj = proj[:, idx]
        q = inputs @ w1
        score = jnp.squeeze(jnp.tanh(local_proj + q[:, :, None, :]) @ v, -1)
        weight = jax.nn.softmax(score, axis=-1)
        local = x_pad[:, idx]
        output = jnp.einsum('btk,btkh->bth', weight, local)
        return output

    def _L2_ffn_ref(x, centroids, ln_g, ln_b, w1, b1, w2, b2):
        import jax, jax.numpy as jnp
        import numpy as np
        LN_EPS = 1e-05

        def layer_norm(x, g, b):
            mu = jnp.mean(x, axis=-1, keepdims=True)
            var = jnp.var(x, axis=-1, keepdims=True)
            return (x - mu) / jnp.sqrt(var + LN_EPS) * g + b

        def balanced_assignment(scores):
            T, E = scores.shape
            C = T // E
            taken = jnp.zeros((T,), dtype=bool)
            parts = []
            for e in range(E):
                s = jnp.where(taken, -jnp.inf, scores[:, e])
                _, idx = jax.lax.top_k(s, C)
                parts.append(idx)
                taken = taken.at[idx].set(True)
            return jnp.concatenate(parts)
        D = x.shape[-1]
        feat = x.reshape(-1, D)
        T = feat.shape[0]
        E = centroids.shape[0]
        C = T // E
        norm = layer_norm(feat, ln_g, ln_b)
        scores = jax.lax.stop_gradient(norm @ centroids.T)
        sort_by_expert = balanced_assignment(scores)
        routed = feat[sort_by_expert].reshape(E, C, D)
        h = layer_norm(routed, ln_g, ln_b)
        h = jax.nn.gelu(jnp.einsum('ecd,edf->ecf', h, w1) + b1[:, None, :])
        h = jnp.einsum('ecf,efd->ecd', h, w2) + b2[:, None, :]
        out = routed + h
        inv = jnp.zeros((T,), dtype=jnp.int32).at[sort_by_expert].set(jnp.arange(T, dtype=jnp.int32))
        return out.reshape(T, D)[inv].reshape(x.shape)

    def _L3_attn_ref(x, pos_embed, W_Q, b_Q, W_K, b_K, W_V, b_V, W_O, b_O):
        import jax, jax.numpy as jnp
        import numpy as np
        N_HEADS = 16
        D_MODEL = 128
        D_HEAD = 64
        BATCH = 4
        SEQ = 256
        IGNORE = -100000.0
        q = jnp.einsum('bpm,imh->bpih', x, W_Q) + b_Q
        k = jnp.einsum('bpm,imh->bpih', x, W_K) + b_K
        v = jnp.einsum('bpm,imh->bpih', x, W_V) + b_V
        attn_scale = np.sqrt(D_HEAD).astype(np.float32)
        scores = jnp.einsum('bpih,bqih->bipq', q, k) / attn_scale
        S = x.shape[1]
        causal = jnp.tril(jnp.ones((S, S), dtype=bool))
        scores = jnp.where(causal, scores, jnp.float32(IGNORE))
        attn = jax.nn.softmax(scores, axis=-1)
        z = jnp.einsum('bpih,biqp->bqih', v, attn)
        out = jnp.einsum('bqih,ihm->bqm', z, W_O) + b_O
        return out

    def _L3_ffn_ref(x, gate_w, gate_b, ew1, ew2, ew3, fc1, fc2, fc3):
        import jax, jax.numpy as jnp
        import numpy as np
        DIM = 128
        MOE_INTER = 128
        SHARED_INTER = 128
        N_EXPERTS = 6
        TOP_K = 2
        ROUTE_SCALE = 1.0
        B, S = (8, 512)
        STD = 0.02 / np.sqrt(DIM)
        STD_I = 0.02 / np.sqrt(MOE_INTER)
        orig_shape = x.shape
        xt = x.reshape(-1, DIM)
        logits = xt @ gate_w.T + gate_b
        probs = jax.nn.sigmoid(logits)
        w, idx = jax.lax.top_k(probs, TOP_K)
        w = w / (jnp.sum(w, axis=-1, keepdims=True) + 1e-08)
        w = w * ROUTE_SCALE
        ge = jnp.sum(jax.nn.one_hot(idx, N_EXPERTS, dtype=w.dtype) * w[..., None], axis=1)
        y = jnp.zeros_like(xt)
        for e in range(N_EXPERTS):
            h = jax.nn.silu(xt @ ew1[e].T) * (xt @ ew3[e].T)
            y = y + ge[:, e:e + 1] * (h @ ew2[e].T)
        z = jax.nn.silu(xt @ fc1.T) * (xt @ fc2.T) @ fc3.T
        return (y + z).reshape(orig_shape)
    x = L0_attn_hidden_states
    xn = _layernorm(x, axis=-1)
    s = _L0_attn_ref(xn, L0_attn_Wq, L0_attn_Wk, L0_attn_Wv, L0_attn_conv_q, L0_attn_conv_k, L0_attn_conv_v, L0_attn_Wb, L0_attn_Wmix, L0_attn_norm_w, L0_attn_Wo)
    g = _silu(_L0_ffn_ref(xn, L0_ffn_Wq, L0_ffn_bq, L0_ffn_Wk, L0_ffn_bk, L0_ffn_Wv, L0_ffn_bv, L0_ffn_Wo, L0_ffn_bo, L0_ffn_gW, L0_ffn_gb, L0_ffn_W1, L0_ffn_b1, L0_ffn_W2, L0_ffn_b2, L0_ffn_ln1_g, L0_ffn_ln1_b, L0_ffn_ln2_g, L0_ffn_ln2_b))
    x = x + s * g
    xn = _layernorm(x, axis=-1)
    s = _L1_attn_ref(xn, L1_attn_w_in, L1_attn_conv_w, L1_attn_conv_b, L1_attn_w_B, L1_attn_w_C, L1_attn_w_out)
    g = _silu(_L1_ffn_ref(xn, L1_ffn_Wg, L1_ffn_W1, L1_ffn_W2, L1_ffn_W3))
    x = x + s * g
    xn = _layernorm(x, axis=-1)
    s = _L2_attn_ref(xn, L2_attn_w1, L2_attn_w2, L2_attn_v)
    g = _silu(_L2_ffn_ref(xn, L2_ffn_centroids, L2_ffn_ln_g, L2_ffn_ln_b, L2_ffn_w1, L2_ffn_b1, L2_ffn_w2, L2_ffn_b2))
    x = x + s * g
    xn = _layernorm(x, axis=-1)
    s = _L3_attn_ref(xn, L3_attn_pos_embed, L3_attn_W_Q, L3_attn_b_Q, L3_attn_W_K, L3_attn_b_K, L3_attn_W_V, L3_attn_b_V, L3_attn_W_O, L3_attn_b_O)
    g = _silu(_L3_ffn_ref(xn, L3_ffn_gate_w, L3_ffn_gate_b, L3_ffn_ew1, L3_ffn_ew2, L3_ffn_ew3, L3_ffn_fc1, L3_ffn_fc2, L3_ffn_fc3))
    x = x + s * g
    return x

_drawn_inputs = setup_inputs


def setup_inputs(seed=0):
    import zlib

    import numpy as np

    out = dict(_drawn_inputs(seed))
    spreads = {'L0_attn_norm_w': (1.0, 0.2),
     'L0_ffn_bq': (0.0, 0.8),
     'L0_ffn_bk': (0.0, 2.0),
     'L0_ffn_bv': (0.0, 0.8),
     'L0_ffn_bo': (0.0, 0.492),
     'L0_ffn_gb': (0.0, 0.8),
     'L0_ffn_b1': (0.0, 0.8),
     'L0_ffn_b2': (0.0, 0.8),
     'L0_ffn_ln1_g': (1.0, 0.2),
     'L0_ffn_ln1_b': (0.0, 0.507),
     'L0_ffn_ln2_g': (1.0, 0.2),
     'L0_ffn_ln2_b': (0.0, 0.545),
     'L2_ffn_ln_g': (1.0, 0.6),
     'L2_ffn_ln_b': (0.0, 0.8),
     'L2_ffn_b1': (0.0, 0.8),
     'L2_ffn_b2': (0.0, 0.48),
     'L3_attn_b_Q': (0.0, 0.8),
     'L3_attn_b_K': (0.0, 0.8),
     'L3_attn_b_V': (0.0, 2.0),
     'L3_attn_b_O': (0.0, 2.0),
     'L3_ffn_gate_b': (0.0, 0.8)}
    factors = {'L0_attn_Wb': 5.983,
     'L0_attn_Wmix': 3.714,
     'L0_ffn_Wq': 8.0,
     'L0_ffn_Wk': 8.0,
     'L0_ffn_Wv': 8.0,
     'L0_ffn_Wo': 8.0,
     'L0_ffn_gW': 8.0,
     'L0_ffn_W1': 8.0,
     'L0_ffn_W2': 8.0,
     'L2_ffn_centroids': 3.097,
     'L2_ffn_w1': 5.962,
     'L2_ffn_w2': 5.484,
     'L3_attn_W_Q': 8.0,
     'L3_attn_W_K': 8.0,
     'L3_attn_W_V': 8.0,
     'L3_attn_W_O': 8.0,
     'L3_ffn_gate_w': 8.0,
     'L3_ffn_ew1': 8.0,
     'L3_ffn_ew2': 8.0,
     'L3_ffn_ew3': 8.0,
     'L3_ffn_fc1': 8.0,
     'L3_ffn_fc2': 8.0,
     'L3_ffn_fc3': 8.0,
     'L1_attn_w_in': 8.0,
     'L1_attn_conv_w': 8.0,
     'L1_attn_conv_b': 8.0,
     'L1_attn_w_B': 8.0,
     'L1_attn_w_C': 8.0,
     'L1_attn_w_out': 8.0,
     'L1_ffn_Wg': 8.0,
     'L1_ffn_W1': 8.0,
     'L1_ffn_W2': 8.0,
     'L1_ffn_W3': 8.0}
    for name, (base, spread) in spreads.items():
        noise = np.random.default_rng([zlib.crc32(name.encode()), seed]).standard_normal(out[name].shape)
        drawn = base * np.exp(spread * noise) if base else spread * noise
        out[name] = jnp.asarray(drawn.astype(out[name].dtype))
    for name, factor in factors.items():
        out[name] = (out[name] * factor).astype(out[name].dtype)
    return out
```

```python
from contextlib import ExitStack, contextmanager

import concourse.bass as bass
import numpy as np
from concourse import mybir

F32 = mybir.dt.float32
BF16 = mybir.dt.bfloat16
I32 = mybir.dt.int32
ALU = mybir.AluOpType
ACT = mybir.ActivationFunctionType
AX = mybir.AxisListType

P = 128
D = 128
BATCH = 16
SEQ = 256
TOK = BATCH * SEQ
BLK = TOK // P
GB = 4
GT = GB * P
GRP = TOK // GT
LN_EPS = 1e-5


@contextmanager
def phase(nc, names, steps=1):
    with ExitStack() as ctx:
        sems = [ctx.enter_context(nc.semaphore(n)) for n in names]
        step = ctx.enter_context(nc.Fori(0, steps)) if steps > 1 else 0
        with nc.Block() as block:
            yield block, step, sems
        numbers = sorted(s.num for s in sems)
        while numbers:
            run = 1
            while run < len(numbers) and numbers[run] == numbers[0] + run:
                run += 1
            nc.sync.sem_clear(range(numbers[0], numbers[0] + run))
            numbers = numbers[run:]
        nc.all_engine_barrier()


class Chain:

    def __init__(self, engine, sem):
        self.engine, self.sem, self.count = engine, sem, 0

    def __call__(self, instruction):
        self.count += 1
        instruction.then_inc(self.sem, 1)
        self.engine.wait_ge(self.sem, self.count)


class Memory:

    def __init__(self, nc, ctx):
        self.nc, self.ctx = nc, ctx

    def sb(self, name, shape, dt=F32):
        return self.ctx.enter_context(self.nc.sbuf_tensor(name, shape, dt))

    def psum(self, name, shape, dt=F32):
        return self.ctx.enter_context(self.nc.psum_tensor(name, shape, dt))


def load(nc, pairs):
    with phase(nc, ["loaded_sp", "loaded_act"]) as (block, _, (loaded_sp, loaded_act)):
        @block.sync
        def _(sp):
            mine = pairs[0::2]
            for dst, src in mine:
                sp.dma_start(dst, src).then_inc(loaded_sp, 16)
            sp.wait_ge(loaded_sp, 16 * len(mine))

        @block.scalar
        def _(act):
            mine = pairs[1::2]
            for dst, src in mine:
                act.dma_start(dst, src).then_inc(loaded_act, 16)
            if mine:
                act.wait_ge(loaded_act, 16 * len(mine))


def constants(nc, c):
    with phase(nc, ["filled", "cut"]) as (block, _, (filled, cut)):
        @block.gpsimd
        def _(pool):
            pool.memset(c.ident[:, :], 0.0).then_inc(filled, 1)
            pool.memset(c.ones[:, :], 1.0).then_inc(filled, 1)
            pool.memset(c.minus_half[:, :], -0.5).then_inc(filled, 1)
            pool.memset(c.triu[:, :], 1.0).then_inc(filled, 1)
            pool.memset(c.ident_bf[:, :], 0.0).then_inc(filled, 1)
            pool.memset(c.future[:, :], 0.0).then_inc(filled, 1)
            pool.wait_ge(filled, 6)
            pool.affine_select(out=c.ident[:, :], in_=c.ident[:, :], compare_op=ALU.not_equal, fill=1.0,
                               base=0, pattern=[[-1, P]], channel_multiplier=1).then_inc(cut, 1)
            pool.affine_select(out=c.ident_bf[:, :], in_=c.ident_bf[:, :], compare_op=ALU.not_equal, fill=1.0,
                               base=0, pattern=[[-1, P]], channel_multiplier=1).then_inc(cut, 1)
            pool.affine_select(out=c.triu[:, :], in_=c.triu[:, :], compare_op=ALU.is_gt, fill=0.0,
                               base=0, pattern=[[1, P]], channel_multiplier=-1).then_inc(cut, 1)
            pool.affine_select(out=c.future[:, :], in_=c.future[:, :], compare_op=ALU.is_ge, fill=-1e5,
                               base=0, pattern=[[-1, P]], channel_multiplier=1).then_inc(cut, 1)
            pool.wait_ge(cut, 4)


class Constants:
    def __init__(self, mem):
        self.ident = mem.sb("ident", [P, P])
        self.ones = mem.sb("ones", [P, P])
        self.triu = mem.sb("triu", [P, P])
        self.minus_half = mem.sb("minus_half", [P, GB])
        self.ident_bf = mem.sb("ident_bf", [P, P], BF16)
        self.future = mem.sb("future", [P, P], BF16)


class State:

    def __init__(self, mem):
        self.x = mem.sb("x_tok", [P, BLK, D])
        self.xn = mem.sb("xn_tok", [P, BLK, D])
        self.xnt = mem.sb("xn_ch", [P, TOK])
        self.s = mem.sb("mixer_out", [P, BLK, D])
        self.g = mem.sb("ffn_out", [P, BLK, D])


def combine(nc, st, layer):
    with nc.sbuf_tensor(f"gate{layer}", [P, GB, D], F32) as gate, \
            phase(nc, ["gate_ready", "dve_step"], GRP) as (block, i, (gate_ready, dve_step)):
        rows = bass.ds(i * GB, GB)

        @block.scalar
        def _(act):
            act.activation(gate[:, :, :], st.g[:, rows, :], ACT.Silu).then_inc(gate_ready, 1)

        @block.vector
        def _(dve):
            link = Chain(dve, dve_step)
            dve.wait_ge(gate_ready, 1)
            link(dve.tensor_tensor(gate[:, :, :], gate[:, :, :], st.s[:, rows, :], ALU.mult))
            link(dve.tensor_tensor(st.x[:, rows, :], st.x[:, rows, :], gate[:, :, :], ALU.add))


def layer_norm(nc, c, name, src, dst, dst_ch=None, gain=None, shift=None):
    with ExitStack() as ctx:
        mem = Memory(nc, ctx)
        stats = mem.sb(name + "_stats", [P, GB, 6])
        mv = mem.sb(name + "_mv", [P, GB, 2])
        rstd = mem.sb(name + "_rstd", [P, GB])
        norm = mem.sb(name + "_norm", [P, GB, D])
        pt = mem.psum(name + "_pt", [P, GB, P])
        names = ["stats_ready", "dve_step", "rstd_ready", "pool_step", "norm_ready", "turned", "stored"]
        with phase(nc, names, GRP) as (block, i, sems):
            stats_ready, dve_step, rstd_ready, pool_step, norm_ready, turned, stored = sems
            rows = bass.ds(i * GB, GB)

            @block.vector
            def _(dve):
                link = Chain(dve, dve_step)
                for j in range(GB):
                    link(dve.bn_stats(stats[:, j, :], src[:, i * GB + j, :]))
                for j in range(GB):
                    dve.bn_aggr(mv[:, j, :], stats[:, j, :]).then_inc(stats_ready, 1)
                dve.wait_ge(rstd_ready, 1)
                for j in range(GB):
                    ins = dve.tensor_scalar(norm[:, j, :], src[:, i * GB + j, :], mv[:, j, 0:1], rstd[:, j:j + 1],
                                            ALU.subtract, ALU.mult)
                    if gain is None:
                        ins.then_inc(norm_ready, 1)
                    else:
                        link(ins)
                if gain is not None:
                    link(dve.tensor_tensor(norm[:, :, :], norm[:, :, :],
                                           gain.unsqueeze(1).to_broadcast([P, GB, D]), ALU.mult))
                    dve.tensor_tensor(norm[:, :, :], norm[:, :, :],
                                      shift.unsqueeze(1).to_broadcast([P, GB, D]), ALU.add).then_inc(norm_ready, GB)

            @block.gpsimd
            def _(pool):
                link = Chain(pool, pool_step)
                pool.wait_ge(stats_ready, GB)
                link(pool.tensor_scalar(rstd[:, :], mv[:, :, 1], LN_EPS, None, ALU.add))
                pool.tensor_tensor(rstd[:, :], rstd[:, :], c.minus_half[:, :], ALU.pow).then_inc(rstd_ready, 1)
                pool.wait_ge(norm_ready, GB)
                if dst is None:
                    return
                pool.tensor_copy(dst[:, rows, :], norm[:, :, :]).then_inc(stored, 1)

            if dst_ch is not None:
                @block.tensor
                def _(pe):
                    for j in range(GB):
                        pe.wait_ge(norm_ready, GB if gain is not None else j + 1)
                        pe.transpose(pt[:, j, :], norm[:, j, :], c.ident[:, :]).then_inc(turned, 1)

                @block.scalar
                def _(act):
                    act.wait_ge(turned, GB)
                    act.activation(dst_ch[:, bass.ds(i * GT, GT)], pt[:, :, :].rearrange("p a b -> p (a b)"), ACT.Copy)\
                       .then_inc(stored, 1)


WAYS = 16
ROUNDS = 6
EXPONENT = 0x7F800000
GONE = 1e30


def token_scores(nc, name, src_ch, w, n_exp, score):
    with nc.psum_tensor(name + "_ps", [P, BLK, n_exp], F32) as ps, \
            phase(nc, [name + "_scores_ready"]) as (block, _, (scores_ready,)):
        @block.tensor
        def _(pe):
            for b in range(BLK):
                ins = pe.matmul(ps[:, b, :], src_ch[:, b * P:(b + 1) * P], w[:, :], start=True, stop=True)
            ins.then_inc(scores_ready, 1)

        @block.vector
        def _(dve):
            dve.wait_ge(scores_ready, 1)
            dve.tensor_copy(score[:, :, :], ps[:, :, :].rearrange("p b e -> p e b"))


def choose(nc, c, name, score, chosen, n_exp, count, in_turn=False):
    with ExitStack() as ctx:
        mem = Memory(nc, ctx)
        E = 1 if in_turn else n_exp
        T = WAYS - 1
        biggest = mem.sb(name + "_biggest", [P, 1])
        bound = mem.sb(name + "_bound", [P, 1])
        index = mem.sb(name + "_index", [P, T])
        width = mem.sb(name + "_width", [P, ROUNDS])
        offsets = mem.sb(name + "_offsets", [P, ROUNDS, T])
        low = mem.sb(name + "_low", [P, E])
        thr = mem.sb(name + "_thr", [P, E, T])
        reached = mem.sb(name + "_reached", [P, E, T, BLK])
        part = mem.sb(name + "_part", [P, E, T])
        over = mem.sb(name + "_over", [P, E, T])
        kept = mem.sb(name + "_kept", [P, E])
        tie = mem.sb(name + "_tie", [P, E, BLK])
        before = mem.sb(name + "_before", [P, E, BLK + 1])
        one = mem.sb(name + "_one", [P, BLK])
        need = mem.sb(name + "_need", [P, E])
        p_count = mem.psum(name + "_count", [P, E, T])
        p_before = mem.psum(name + "_p_before", [P, E, BLK])

        names = [name + "_" + n for n in ("dve_step", "set", "biggest_ready", "bound_ready")]
        with phase(nc, names) as (block, _, (dve_step, set_, biggest_ready, bound_ready)):
            @block.gpsimd
            def _(pool):
                pool.iota(index[:, :], pattern=[[1, T]], base=1, channel_multiplier=0, allow_small_or_imprecise_dtypes=True)\
                    .then_inc(set_, 1)
                pool.memset(one[:, :], 1.0).then_inc(set_, 1)
                pool.memset(before[:, :, :], 0.0).then_inc(set_, 1)
                pool.wait_ge(biggest_ready, 1)
                pool.partition_all_reduce(bound[:, :], biggest[:, :], P, bass.bass_isa.ReduceOp.max).then_inc(bound_ready, 1)

            @block.vector
            def _(dve):
                link = Chain(dve, dve_step)
                link(dve.tensor_reduce(biggest[:, :], score[:, :, :], AX.XY, ALU.max, apply_absolute_value=True))
                dve.tensor_scalar(biggest[:, :], biggest[:, :], 1e-30, None, ALU.max).then_inc(biggest_ready, 1)
                dve.wait_ge(bound_ready, 1)
                link(dve.tensor_scalar(bound[:, :].bitcast(I32), bound[:, :].bitcast(I32), EXPONENT, None, ALU.bitwise_and))
                link(dve.tensor_scalar(bound[:, :], bound[:, :], 2.0, None, ALU.mult))
                dve.wait_ge(set_, 3)
                for r in range(ROUNDS):
                    link(dve.tensor_scalar(width[:, r:r + 1], bound[:, :], 2.0 / WAYS ** (r + 1), None, ALU.mult))
                    link(dve.tensor_scalar(offsets[:, r, :], index[:, :], width[:, r:r + 1], None, ALU.mult))

        for turn in range(n_exp if in_turn else 1):
            s = score[:, turn:turn + 1, :] if in_turn else score[:, :, :]
            got = chosen[:, turn:turn + 1, :] if in_turn else chosen[:, :, :]
            wide = [P, E, T, BLK]
            names = [name + "_" + n for n in ("dve_step", "part_ready", "count_ready", "tie_ready", "before_ready")]
            with phase(nc, names) as (block, _, (dve_step, part_ready, count_ready, tie_ready, before_ready)):
                @block.tensor
                def _(pe):
                    for r in range(ROUNDS):
                        pe.wait_ge(part_ready, r + 1)
                        pe.matmul(p_count[:, :, :], c.ones[:, :], part[:, :, :], start=True, stop=True).then_inc(count_ready, 1)
                    pe.wait_ge(part_ready, ROUNDS + 1)
                    pe.matmul(p_count[:, :, 0], c.ones[:, :], part[:, :, 0], start=True, stop=True).then_inc(count_ready, 1)
                    pe.wait_ge(tie_ready, 1)
                    pe.matmul(p_before[:, :, :], c.ones[:, :], before[:, :, 0:BLK], start=True, stop=False)
                    pe.matmul(p_before[:, :, :], c.triu[:, :], tie[:, :, :], start=False, stop=True).then_inc(before_ready, 1)

                @block.vector
                def _(dve):
                    link = Chain(dve, dve_step)
                    link(dve.tensor_scalar(low[:, :], bound[:, 0:1].to_broadcast([P, E]), -1.0, None, ALU.mult))
                    for r in range(ROUNDS):
                        link(dve.tensor_tensor(thr[:, :, :], low[:, :].unsqueeze(2).to_broadcast([P, E, T]),
                                               offsets[:, r, :].unsqueeze(1).to_broadcast([P, E, T]), ALU.add))
                        link(dve.tensor_tensor(reached[:, :, :, :], s.unsqueeze(2).to_broadcast(wide),
                                               thr[:, :, :].unsqueeze(3).to_broadcast(wide), ALU.is_ge))
                        dve.tensor_reduce(part[:, :, :], reached[:, :, :, :], AX.X, ALU.add).then_inc(part_ready, 1)
                        dve.wait_ge(count_ready, r + 1)
                        link(dve.tensor_scalar(over[:, :, :], p_count[:, :, :], count - 0.5, None, ALU.is_ge))
                        link(dve.tensor_reduce(kept[:, :], over[:, :, :], AX.X, ALU.add))
                        link(dve.scalar_tensor_tensor(low[:, :], kept[:, :], width[:, r:r + 1], low[:, :], ALU.mult, ALU.add))
                    spread = [P, E, BLK]
                    link(dve.tensor_tensor(tie[:, :, :], s, low[:, :].unsqueeze(2).to_broadcast(spread), ALU.is_ge))
                    link(dve.tensor_scalar(low[:, :], low[:, :], width[:, ROUNDS - 1:ROUNDS], None, ALU.add))
                    link(dve.tensor_tensor(got, s, low[:, :].unsqueeze(2).to_broadcast(spread), ALU.is_ge))
                    dve.tensor_reduce(part[:, :, 0], got, AX.X, ALU.add).then_inc(part_ready, 1)
                    link(dve.tensor_tensor(tie[:, :, :], tie[:, :, :], got, ALU.subtract))
                    for e in range(E):
                        ins = dve.tensor_tensor_scan(before[:, e, 1:], one[:, :], tie[:, e, :], 0.0, ALU.mult, ALU.add)
                        if e < E - 1:
                            link(ins)
                    ins.then_inc(tie_ready, 1)
                    dve.wait_ge(count_ready, ROUNDS + 1)
                    link(dve.tensor_scalar(need[:, :], p_count[:, :, 0], -1.0, float(count), ALU.mult, ALU.add))
                    dve.wait_ge(before_ready, 1)
                    room = reached[:, :, 0, :]
                    link(dve.tensor_tensor(room, p_before[:, :, :], need[:, :].unsqueeze(2).to_broadcast(spread), ALU.is_lt))
                    link(dve.tensor_tensor(room, room, tie[:, :, :], ALU.mult))
                    link(dve.tensor_tensor(got, got, room, ALU.add))
                    if in_turn and turn < n_exp - 1:
                        later = [P, n_exp - turn - 1, BLK]
                        link(dve.tensor_scalar(room, got, -GONE, None, ALU.mult))
                        link(dve.tensor_tensor(score[:, turn + 1:, :], score[:, turn + 1:, :], room.to_broadcast(later), ALU.add))


def experts(nc, c, st, name, src_ch, w_tok, n_exp, chunks, func, w1, w2, b1=None, w3=None, b2=None, residual=None):
    units = n_exp * chunks
    gated = w3 is not None
    with ExitStack() as ctx:
        mem = Memory(nc, ctx)
        act_out = mem.sb(name + "_act", [P, 2, GT]) if gated else None
        hidden = mem.sb(name + "_hidden", [P, 2, chunks, GT])
        acc = mem.sb(name + "_acc", [P, GB, D])
        w_now = mem.sb(name + "_w", [P, GB, n_exp])
        wt = mem.sb(name + "_wt", [n_exp, GB, P]) if b2 is not None else None
        ph1 = [mem.psum(f"{name}_ph1{k}", [P, GT]) for k in range(2)]
        ph3 = [mem.psum(f"{name}_ph3{k}", [P, GT]) for k in range(2)] if gated else None
        py = [mem.psum(f"{name}_py{k}", [P, GB, D]) for k in range(2)]
        names = ["h1_ready", "h3_ready", "act_ready", "hidden_ready", "y_ready", "added", "w_ready", "wt_ready", "wt_saved"]
        with phase(nc, [name + "_" + n for n in names], GRP) as (block, i, sems):
            h1_ready, h3_ready, act_ready, hidden_ready, y_ready, added, w_ready, wt_ready, wt_saved = sems
            tokens = bass.ds(i * GT, GT)

            @block.tensor
            def _(pe):
                def up(u):
                    if u >= 2:
                        pe.wait_ge(hidden_ready, u - 1)
                    pe.matmul(ph1[u % 2][:, :], w1[:, u, :], src_ch[:, tokens], start=True, stop=True).then_inc(h1_ready, 1)
                    if gated:
                        pe.matmul(ph3[u % 2][:, :], w3[:, u, :], src_ch[:, tokens], start=True, stop=True).then_inc(h3_ready, 1)

                def down(e):
                    pe.wait_ge(hidden_ready, chunks * (e + 1))
                    if e >= 2:
                        pe.wait_ge(added, GB * (e - 1))
                    for j in range(GB):
                        for f in range(chunks):
                            ins = pe.matmul(py[e % 2][:, j, :], hidden[:, e % 2, f, j * P:(j + 1) * P],
                                            w2[:, e * chunks + f, :], start=(f == 0), stop=(f == chunks - 1))
                    ins.then_inc(y_ready, 1)

                for e in range(n_exp + 1):
                    if e < n_exp:
                        for f in range(chunks):
                            up(e * chunks + f)
                            if f == 0 and e >= 1:
                                down(e - 1)
                    else:
                        down(e - 1)
                if b2 is not None:
                    e = n_exp
                    pe.wait_ge(w_ready, 1)
                    pe.wait_ge(added, GB * (e - 1))
                    for j in range(GB):
                        pe.transpose(py[e % 2][0:n_exp, j, :], w_now[:, j, :], c.ident[:, :]).then_inc(wt_ready, 1)
                    pe.wait_ge(wt_saved, 1)
                    pe.wait_ge(added, GB * e)
                    for j in range(GB):
                        ins = pe.matmul(py[1 - e % 2][:, j, :], wt[:, j, :], b2[:, :], start=True, stop=True)
                    ins.then_inc(y_ready, 1)

            @block.scalar
            def _(act):
                for u in range(units):
                    act.wait_ge(h1_ready, u + 1)
                    e, f = u // chunks, u % chunks
                    if gated:
                        if u >= 2:
                            act.wait_ge(hidden_ready, u - 1)
                        act.activation(act_out[:, u % 2, :], ph1[u % 2][:, :], func).then_inc(act_ready, 1)
                    else:
                        if f == 0 and e >= 2:
                            act.wait_ge(y_ready, e - 1)
                        act.activation(hidden[:, e % 2, f, :], ph1[u % 2][:, :], func, bias=b1[:, u:u + 1])\
                           .then_inc(hidden_ready, 1)
                if b2 is not None:
                    act.wait_ge(wt_ready, GB)
                    act.activation(wt[:, :, :], py[n_exp % 2][0:n_exp, :, :], ACT.Copy).then_inc(wt_saved, 1)

            @block.vector
            def _(dve):
                def add(e):
                    dve.wait_ge(y_ready, e + 1)
                    for j in range(GB):
                        y = py[e % 2][:, j, :] if e < n_exp else py[1 - e % 2][:, j, :]
                        out = acc[:, j, :] if e < last else st.g[:, i * GB + j, :]
                        if e > 0:
                            dve.wait_ge(added, GB * (e - 1) + j + 1)
                        if e == n_exp:
                            ins = dve.tensor_tensor(out, y, acc[:, j, :], ALU.add)
                        elif e == 0 and residual is None:
                            ins = dve.tensor_scalar(out, y, w_now[:, j, e:e + 1], None, ALU.mult)
                        else:
                            more = acc[:, j, :] if e else residual[:, i * GB + j, :]
                            ins = dve.scalar_tensor_tensor(out, y, w_now[:, j, e:e + 1], more, ALU.mult, ALU.add)
                        ins.then_inc(added, 1)

                last = n_exp if b2 is not None else n_exp - 1
                dve.tensor_copy(w_now[:, :, :], w_tok[:, bass.ds(i * GB, GB), :]).then_inc(w_ready, 1)
                dve.wait_ge(w_ready, 1)
                for e in range(n_exp + 1):
                    if gated and e < n_exp:
                        for f in range(chunks):
                            u = e * chunks + f
                            dve.wait_ge(act_ready, u + 1)
                            dve.wait_ge(h3_ready, u + 1)
                            if f == 0 and e >= 2:
                                dve.wait_ge(y_ready, e - 1)
                            dve.tensor_tensor(hidden[:, e % 2, f, :], ph3[u % 2][:, :], act_out[:, u % 2, :], ALU.mult)\
                               .then_inc(hidden_ready, 1)
                    if e >= 1:
                        add(e - 1)
                if b2 is not None:
                    add(n_exp)


def top_two(nc, c, st, name, src_ch, gate_w, gate_b, n_exp, w_tok, softmax):
    with ExitStack() as ctx:
        mem = Memory(nc, ctx)
        prob = mem.sb(name + "_prob", [P, BLK, n_exp])
        rank = mem.sb(name + "_rank", [P, BLK, n_exp])
        beats = mem.sb(name + "_beats", [P, BLK, n_exp])
        small = mem.sb(name + "_small", [P, BLK])
        pl = mem.psum(name + "_pl", [P, BLK, n_exp])
        wide = [P, BLK, n_exp]
        with phase(nc, [name + "_" + n for n in ("logits_ready", "dve_step", "shifted", "prob_ready")]) as (block, _, sems):
            logits_ready, dve_step, shifted, prob_ready = sems

            @block.tensor
            def _(pe):
                for b in range(BLK):
                    pe.matmul(pl[:, b, :], src_ch[:, b * P:(b + 1) * P], gate_w[:, :], start=True, stop=True)\
                      .then_inc(logits_ready, 1)

            @block.scalar
            def _(act):
                act.wait_ge(shifted, 1)
                act.activation(prob[:, :, :], prob[:, :, :], ACT.Exp if softmax else ACT.Sigmoid).then_inc(prob_ready, 1)

            @block.vector
            def _(dve):
                link = Chain(dve, dve_step)
                spread = small[:, :].unsqueeze(2).to_broadcast(wide)
                dve.wait_ge(logits_ready, BLK)
                ins = dve.tensor_tensor(prob[:, :, :], pl[:, :, :], gate_b[:, :].unsqueeze(1).to_broadcast(wide), ALU.add)
                if softmax:
                    link(ins)
                    link(dve.tensor_reduce(small[:, :], prob[:, :, :], AX.X, ALU.max))
                    ins = dve.tensor_tensor(prob[:, :, :], prob[:, :, :], spread, ALU.subtract)
                ins.then_inc(shifted, 1)
                dve.wait_ge(prob_ready, 1)
                if softmax:
                    link(dve.tensor_reduce(small[:, :], prob[:, :, :], AX.X, ALU.add))
                    link(dve.reciprocal(small[:, :], small[:, :]))
                    link(dve.tensor_tensor(prob[:, :, :], prob[:, :, :], spread, ALU.mult))
                link(dve.memset(rank[:, :, :], 0.0))
                for e in range(n_exp):
                    one = prob[:, :, e:e + 1]
                    if e + 1 < n_exp:
                        rest = [P, BLK, n_exp - e - 1]
                        link(dve.tensor_tensor(beats[:, :, e + 1:], one.to_broadcast(rest), prob[:, :, e + 1:], ALU.is_ge))
                        link(dve.tensor_tensor(rank[:, :, e + 1:], rank[:, :, e + 1:], beats[:, :, e + 1:], ALU.add))
                    if e:
                        rest = [P, BLK, e]
                        link(dve.tensor_tensor(beats[:, :, :e], one.to_broadcast(rest), prob[:, :, :e], ALU.is_gt))
                        link(dve.tensor_tensor(rank[:, :, :e], rank[:, :, :e], beats[:, :, :e], ALU.add))
                link(dve.tensor_scalar(rank[:, :, :], rank[:, :, :], 1.5, None, ALU.is_lt))
                out = w_tok[:, :, 0:n_exp]
                link(dve.tensor_tensor(out, prob[:, :, :], rank[:, :, :], ALU.mult))
                if not softmax:
                    link(dve.tensor_reduce(small[:, :], out, AX.X, ALU.add))
                    link(dve.tensor_scalar(small[:, :], small[:, :], 1e-8, None, ALU.add))
                    link(dve.reciprocal(small[:, :], small[:, :]))
                    link(dve.tensor_tensor(out, out, spread, ALU.mult))


CHUNK = 32
HEADS = 4
HD = 32
CPB = P // CHUNK
MATS = BLK * HEADS * CPB
NSEQ = GT // SEQ


def delta_masks(nc, m):
    with phase(nc, ["gd_zero", "gd_same", "gd_cut"]) as (block, _, (zero, same, cut)):
        @block.gpsimd
        def _(pool):
            for t in (m.same, m.minus_same, m.minus_strict, m.causal):
                pool.memset(t[:, :], 0.0).then_inc(zero, 1)
            pool.wait_ge(zero, 4)
            for t, value in ((m.same, 1.0), (m.minus_same, -1.0), (m.minus_strict, -1.0), (m.causal, 1.0)):
                for n in range(CPB):
                    part = slice(n * CHUNK, (n + 1) * CHUNK)
                    pool.memset(t[part, part], value).then_inc(same, 1)
            pool.wait_ge(same, 4 * CPB)
            pool.affine_select(out=m.minus_strict[:, :], in_=m.minus_strict[:, :], compare_op=ALU.is_gt, fill=0.0,
                               base=0, pattern=[[1, P]], channel_multiplier=-1).then_inc(cut, 1)
            pool.affine_select(out=m.causal[:, :], in_=m.causal[:, :], compare_op=ALU.is_ge, fill=0.0,
                               base=0, pattern=[[1, P]], channel_multiplier=-1).then_inc(cut, 1)
            pool.wait_ge(cut, 2)


class DeltaState:
    def __init__(self, nc, mem):
        self.same = mem.sb("gd_m_same", [P, P])
        self.minus_same = mem.sb("gd_m_minus_same", [P, P])
        self.minus_strict = mem.sb("gd_m_strict", [P, P])
        self.causal = mem.sb("gd_m_causal", [P, P])
        self.beta = mem.sb("gd_beta", [P, BLK, 2 * HEADS])
        self.q_ch = mem.sb("gd_q_ch", [P, TOK])
        self.k_ch = mem.sb("gd_k_ch", [P, TOK])
        self.k_tok = mem.sb("gd_k_tok", [P, BLK, D])
        self.v_tok = mem.sb("gd_v_tok", [P, BLK, D])
        self.tri = nc.dram_tensor("gd_tri", (MATS * CHUNK * CHUNK,), F32, kind="Internal").ap()


def gates(nc, st, m, w_b, w_gates):
    beta_ch = st.g[:, :, :].rearrange("p b d -> p (b d)")
    with ExitStack() as ctx:
        mem = Memory(nc, ctx)
        p_tok = mem.psum("gd_p_tok", [P, BLK, 2 * HEADS])
        p_ch = [mem.psum(f"gd_p_ch{n}", [P, GT]) for n in range(2)]
        with phase(nc, ["gd_tok_ready", "gd_ch_ready", "gd_ch_saved"]) as (block, _, (tok_ready, ch_ready, ch_saved)):
            @block.tensor
            def _(pe):
                for b in range(BLK):
                    ins = pe.matmul(p_tok[:, b, :], st.xnt[:, b * P:(b + 1) * P], w_gates[:, :], start=True, stop=True)
                ins.then_inc(tok_ready, 1)
                for g in range(GRP):
                    if g >= 2:
                        pe.wait_ge(ch_saved, g - 1)
                    pe.matmul(p_ch[g % 2][:, :], w_b[:, :], st.xnt[:, g * GT:(g + 1) * GT], start=True, stop=True)\
                      .then_inc(ch_ready, 1)

            @block.scalar
            def _(act):
                act.wait_ge(tok_ready, 1)
                act.activation(m.beta[:, :, :], p_tok[:, :, :], ACT.Sigmoid)
                for g in range(GRP):
                    act.wait_ge(ch_ready, g + 1)
                    act.activation(beta_ch[:, g * GT:(g + 1) * GT], p_ch[g % 2][:, :], ACT.Sigmoid).then_inc(ch_saved, 1)


def project(nc, c, st, m, w3, taps):
    TAPS = 4
    PAD = TAPS - 1
    beta_ch = st.g[:, :, :].rearrange("p b d -> p (b d)")
    with ExitStack() as ctx:
        mem = Memory(nc, ctx)
        padded = mem.sb("gp_padded", [P, 3, NSEQ, PAD + SEQ])
        y = mem.sb("gp_y", [P, 3, NSEQ, SEQ])
        square = mem.sb("gp_square", [P, 2, GT])
        kb = mem.sb("gp_kb", [P, GT])
        tri = mem.sb("gp_tri", [P, HEADS, GB, P])
        eps = mem.sb("gp_eps", [P, 1])
        bank = [mem.psum(f"gp_bank{n}", [P, 512]) for n in range(8)]
        flat = y[:, :, :, :].rearrange("p a b c -> p a (b c)")
        with phase(nc, ["gp_set"]) as (block, _, (set_,)):
            @block.gpsimd
            def _(pool):
                pool.memset(padded[:, :, :, :], 0.0).then_inc(set_, 1)
                pool.memset(eps[:, :], 1e-6).then_inc(set_, 1)
                pool.wait_ge(set_, 2)
        names = ["gp_" + n for n in ("in_ready", "x_saved", "dve_step", "conv_ready", "silu_ready", "square_ready", "sum_ready",
                                     "root_ready", "unit_ready", "kb_ready", "turn_ready", "v_saved", "tri_ready", "tri_masked",
                                     "tri_stored", "k_saved")]
        with phase(nc, names, GRP) as (block, i, sems):
            (in_ready, x_saved, dve_step, conv_ready, silu_ready, square_ready, sum_ready, root_ready, unit_ready, kb_ready,
             turn_ready, v_saved, tri_ready, tri_masked, tri_stored, k_saved) = sems
            tokens = bass.ds(i * GT, GT)

            @block.tensor
            def _(pe):
                for n in range(3):
                    pe.matmul(bank[n][:, :], w3[:, n, :], st.xnt[:, tokens], start=True, stop=True).then_inc(in_ready, 1)
                for n in range(2):
                    pe.wait_ge(square_ready, n + 1)
                    pe.matmul(bank[3 + n][:, :], m.same[:, :], square[:, n, :], start=True, stop=True).then_inc(sum_ready, 1)
                pe.wait_ge(silu_ready, 3)
                for j in range(GB):
                    ins = pe.transpose(bank[5][:, j * P:(j + 1) * P], flat[:, 2, j * P:(j + 1) * P], c.ident[:, :])
                ins.then_inc(turn_ready, 1)
                pe.wait_ge(unit_ready, 2)
                for j in range(GB):
                    ins = pe.transpose(bank[6][:, j * P:(j + 1) * P], flat[:, 1, j * P:(j + 1) * P], c.ident[:, :])
                ins.then_inc(turn_ready, 1)
                pe.wait_ge(kb_ready, 1)
                for h in range(HEADS):
                    rows = slice(h * HD, (h + 1) * HD)
                    for j in range(GB):
                        cols = slice(j * P, (j + 1) * P)
                        ins = pe.matmul(bank[h][:, cols], flat[rows, 1, cols], kb[rows, cols], start=True, stop=True)
                    ins.then_inc(tri_ready, 1)

            @block.scalar
            def _(act):
                for n in range(3):
                    act.wait_ge(in_ready, n + 1)
                    act.activation(padded[:, n, :, PAD:], bank[n][:, :].rearrange("p (a b) -> p a b", a=NSEQ), ACT.Copy)\
                       .then_inc(x_saved, 1)
                for n in range(3):
                    act.wait_ge(conv_ready, n + 1)
                    act.activation(y[:, n, :, :], y[:, n, :, :], ACT.Silu).then_inc(silu_ready, 1)
                for n in range(2):
                    act.wait_ge(silu_ready, n + 1)
                    act.activation(square[:, n, :], flat[:, n, :], ACT.Square).then_inc(square_ready, 1)
                act.wait_ge(turn_ready, 1)
                act.activation(m.v_tok[:, bass.ds(i * GB, GB), :], bank[5][:, :].rearrange("p (a b) -> p a b", a=GB), ACT.Copy)\
                   .then_inc(v_saved, 1)
                for n in range(2):
                    act.wait_ge(sum_ready, n + 1)
                    act.activation(square[:, n, :], bank[3 + n][:, :], ACT.Sqrt, bias=eps[:, 0:1]).then_inc(root_ready, 1)
                act.wait_ge(turn_ready, 2)
                act.activation(m.k_tok[:, bass.ds(i * GB, GB), :], bank[6][:, :].rearrange("p (a b) -> p a b", a=GB), ACT.Copy)\
                   .then_inc(k_saved, 1)

            @block.vector
            def _(dve):
                link = Chain(dve, dve_step)
                for n in range(3):
                    dve.wait_ge(x_saved, n + 1)
                    out = y[:, n, :, :]
                    for k in range(TAPS):
                        x = padded[:, n, :, k:k + SEQ]
                        if k == 0:
                            link(dve.tensor_scalar(out, x, taps[:, n, k:k + 1], None, ALU.mult))
                        else:
                            ins = dve.scalar_tensor_tensor(out, x, taps[:, n, k:k + 1], out, ALU.mult, ALU.add)
                            if k < TAPS - 1:
                                link(ins)
                    ins.then_inc(conv_ready, 1)
                for n in range(2):
                    dve.wait_ge(root_ready, n + 1)
                    link(dve.reciprocal(square[:, n, :], square[:, n, :]))
                    dve.tensor_tensor(flat[:, n, :], flat[:, n, :], square[:, n, :], ALU.mult).then_inc(unit_ready, 1)
                dve.wait_ge(unit_ready, 2)
                dve.tensor_tensor(kb[:, :], flat[:, 1, :], beta_ch[:, tokens], ALU.mult).then_inc(kb_ready, 1)
                for h in range(HEADS):
                    dve.wait_ge(tri_ready, h + 1)
                    dve.tensor_tensor(tri[:, h, :, :], bank[h][:, :].rearrange("p (a b) -> p a b", a=GB),
                                      m.minus_strict[:, :].unsqueeze(1).to_broadcast([P, GB, P]), ALU.mult).then_inc(tri_masked, 1)

            @block.gpsimd
            def _(pool):
                pool.wait_ge(unit_ready, 2)
                pool.tensor_copy(m.q_ch[:, tokens], flat[:, 0, :])
                pool.tensor_copy(m.k_ch[:, tokens], flat[:, 1, :])

            @block.sync
            def _(sp):
                sp.wait_ge(tri_masked, HEADS)
                size = GB * HEADS * CPB * CHUNK * CHUNK
                mats = m.tri[bass.ds(i * size, size)].rearrange("(b h n j i) -> n j h b i", h=HEADS, n=CPB, j=CHUNK, i=CHUNK)
                for n in range(CPB):
                    part = slice(n * CHUNK, (n + 1) * CHUNK)
                    for h in range(HEADS):
                        sp.dma_start(mats[n, :, h, :, :], tri[part, h, :, part]).then_inc(tri_stored, 16)
                sp.wait_ge(tri_stored, 16 * CPB * HEADS)


def invert(nc, m):
    LM = MATS // P
    with ExitStack() as ctx:
        mem = Memory(nc, ctx)
        at = mem.sb("gi_at", [P, LM, CHUNK, CHUNK])
        prod = mem.sb("gi_prod", [P, LM, CHUNK * CHUNK])
        upd = mem.sb("gi_upd", [P, LM, CHUNK])
        lanes = m.tri.rearrange("(p n) -> p n", p=P)
        flat = at[:, :, :, :].rearrange("p a b c -> p (a b c)")
        with phase(nc, ["gi_loaded", "gi_dve_step", "gi_inverted", "gi_stored"]) as (block, _, sems):
            loaded, dve_step, inverted, stored = sems

            @block.sync
            def _(sp):
                sp.dma_start(flat, lanes).then_inc(loaded, 16)
                sp.wait_ge(inverted, 1)
                sp.dma_start(lanes, flat).then_inc(stored, 16)
                sp.wait_ge(stored, 16)

            @block.vector
            def _(dve):
                link = Chain(dve, dve_step)
                dve.wait_ge(loaded, 16)
                for i in range(2, CHUNK):
                    full = [P, LM, i, i]
                    terms = prod[:, :, 0:i * i].rearrange("p a (k j) -> p a k j", k=i)
                    link(dve.tensor_tensor(terms, at[:, :, 0:i, 0:i], at[:, :, 0:i, i].unsqueeze(2).to_broadcast(full), ALU.mult))
                    link(dve.tensor_reduce(upd[:, :, 0:i], terms, AX.X, ALU.add))
                    link(dve.tensor_tensor(at[:, :, 0:i, i], at[:, :, 0:i, i], upd[:, :, 0:i], ALU.add))
                diag = at[:, :, :, :].rearrange("p a b c -> p a (b c)")[:, :, 0:CHUNK * CHUNK:CHUNK + 1]
                dve.tensor_scalar(diag, diag, 1.0, None, ALU.add).then_inc(inverted, 1)


def recur(nc, c, st, m, w_o, norm_w):
    with ExitStack() as ctx:
        mem = Memory(nc, ctx)
        inv = mem.sb("gr_inv", [P, GB, HEADS, P])
        q = mem.sb("gr_q", [P, GT])
        k = mem.sb("gr_k", [P, GT])
        k_tok = mem.sb("gr_k_tok", [P, GB, D])
        v_tok = mem.sb("gr_v_tok", [P, GB, D])
        beta = mem.sb("gr_beta", [P, GB, 2 * HEADS])
        vk = mem.sb("gr_vk", [P, GB, HEADS, 2 * HD])
        u = mem.sb("gr_u", [P, GB, D])
        w = mem.sb("gr_w", [P, GB, D])
        attn = mem.sb("gr_attn", [P, HEADS, GB, P])
        kv = mem.sb("gr_kv", [P, CPB, GB, P])
        trans = mem.sb("gr_trans", [P, CPB, GB, P])
        q_eff = mem.sb("gr_q_eff", [P, GB, P])
        state = mem.sb("gr_state", [P, 2, NSEQ, P])
        o_ch = mem.sb("gr_o_ch", [P, GB, P])
        o = u
        square = vk[:, 0:2, :, :].rearrange("p b h x -> p (b h x)").rearrange("p (a x) -> p a x", x=HD)
        power = mem.sb("gr_power", [P, GB * HEADS])
        half = mem.sb("gr_half", [P, GB * HEADS])
        bank = [mem.psum(f"gr_bank{n}", [P, 4, P]) for n in range(8)]
        with phase(nc, ["gr_set"]) as (block, _, (set_,)):
            @block.gpsimd
            def _(pool):
                pool.memset(inv[:, :, :, :], 0.0).then_inc(set_, 1)
                pool.memset(half[:, :], -0.5).then_inc(set_, 1)
                pool.wait_ge(set_, 2)
        names = ["gr_" + n for n in ("inv_loaded", "qk_loaded", "tok_loaded", "vk_ready", "uw_ready", "u_saved", "w_saved",
                                     "attn_ready", "attn_masked", "kv_ready", "kv_masked", "wk_ready", "wk_masked", "trans_ready",
                                     "qw_ready", "intra_ready", "q_eff_ready", "s_ready", "s_saved", "o_ready", "o_saved",
                                     "o_turned", "dve_step", "mixed", "squared", "power_sum", "pool_step", "power_ready",
                                     "normed", "n_turned", "n_saved", "out_ready")]
        with phase(nc, names, GRP) as (block, i, sems):
            (inv_loaded, qk_loaded, tok_loaded, vk_ready, uw_ready, u_saved, w_saved, attn_ready, attn_masked, kv_ready,
             kv_masked, wk_ready, wk_masked, trans_ready, qw_ready, intra_ready, q_eff_ready, s_ready, s_saved, o_ready,
             o_saved, o_turned, dve_step, mixed, squared, power_sum, pool_step, power_ready, normed, n_turned, n_saved,
             out_ready) = sems
            tokens, rows = bass.ds(i * GT, GT), bass.ds(i * GB, GB)
            CH = SEQ // CHUNK

            @block.sync
            def _(sp):
                sp.dma_start(k_tok[:, :, :], m.k_tok[:, rows, :]).then_inc(tok_loaded, 16)
                sp.dma_start(v_tok[:, :, :], m.v_tok[:, rows, :]).then_inc(tok_loaded, 16)
                sp.dma_start(beta[:, :, :], m.beta[:, rows, :]).then_inc(tok_loaded, 16)
                sp.dma_start(q[:, :], m.q_ch[:, tokens]).then_inc(qk_loaded, 16)
                sp.dma_start(k[:, :], m.k_ch[:, tokens]).then_inc(qk_loaded, 16)

            @block.scalar
            def _(act):
                size = GB * HEADS * CPB * CHUNK * CHUNK
                mats = m.tri[bass.ds(i * size, size)].rearrange("(b h n j i) -> n j b h i", h=HEADS, n=CPB, j=CHUNK, i=CHUNK)
                for n in range(CPB):
                    part = slice(n * CHUNK, (n + 1) * CHUNK)
                    for b in range(GB):
                        act.dma_start(inv[part, b, :, part], mats[n, :, b, :, :]).then_inc(inv_loaded, 16)
                for t in range(2):
                    act.wait_ge(uw_ready, t + 1)
                    src = bank[4 + t][:, :, :].rearrange("p a b -> p (a b)").rearrange("p (b h x) -> p b h x", b=2, h=HEADS)
                    for dst, part, sem in ((u, slice(0, HD), u_saved), (w, slice(HD, 2 * HD), w_saved)):
                        act.activation(dst[:, 2 * t:2 * t + 2, :].rearrange("p b (h x) -> p b h x", h=HEADS),
                                       src[:, :, :, part], ACT.Copy).then_inc(sem, 1)
                act.wait_ge(o_ready, 1)
                act.activation(o_ch[:, :, :], bank[1][:, :, :], ACT.Copy).then_inc(o_saved, 1)
                act.wait_ge(mixed, 1)
                act.activation(square, o[:, :, :].rearrange("p b (h x) -> p (b h) x", h=HEADS), ACT.Square)\
                   .then_inc(squared, 1)
                act.wait_ge(n_turned, 1)
                act.activation(o_ch[:, :, :], bank[5][:, :, :], ACT.Copy, scale=norm_w[:, 0:1]).then_inc(n_saved, 1)
                act.wait_ge(out_ready, 1)
                act.activation(st.s[:, rows, :], bank[6][:, :, :], ACT.Copy)

            @block.tensor
            def _(pe):
                pe.wait_ge(qk_loaded, 32)
                for h in range(HEADS):
                    part = slice(h * HD, (h + 1) * HD)
                    for b in range(GB):
                        cols = slice(b * P, (b + 1) * P)
                        ins = pe.matmul(bank[h][:, b, :], k[part, cols], q[part, cols], start=True, stop=True)
                    ins.then_inc(attn_ready, 1)
                pe.wait_ge(vk_ready, 2)
                pe.wait_ge(inv_loaded, 16 * CPB * GB)
                for b in range(GB):
                    out = bank[4 + b // 2][:, :, :].rearrange("p a b -> p (a b)").rearrange("p (b h x) -> p b h x", b=2, h=HEADS)
                    for h in range(HEADS):
                        ins = pe.matmul(out[:, b % 2, h, :], inv[:, b, h, :], vk[:, b, h, :], start=True, stop=True)
                    if b % 2:
                        ins.then_inc(uw_ready, 1)
                pe.wait_ge(tok_loaded, 48)
                pe.wait_ge(u_saved, 2)
                for n in range(CPB):
                    part = slice(n * CHUNK, (n + 1) * CHUNK)
                    pe.wait_ge(attn_masked, n + 1)
                    for b in range(GB):
                        ins = pe.matmul(bank[n][:, b, :], k_tok[part, b, :], u[part, b, :], start=True, stop=True)
                    ins.then_inc(kv_ready, 1)
                pe.wait_ge(w_saved, 2)
                for n in range(CPB):
                    part = slice(n * CHUNK, (n + 1) * CHUNK)
                    for b in range(GB):
                        ins = pe.matmul(bank[4 + n][:, b, :], w[part, b, :], k_tok[part, b, :], start=True, stop=True)
                    ins.then_inc(wk_ready, 1)
                for src, n, sem in ((w, 0, qw_ready), (u, 1, intra_ready)):
                    pe.wait_ge(kv_masked, n + 1)
                    for b in range(GB):
                        for h in range(HEADS):
                            part = slice(h * HD, (h + 1) * HD)
                            ins = pe.matmul(bank[n][part, b, :], src[:, b, part], attn[:, h, b, :], start=(b == 0),
                                            stop=(n == 0), skip_group_check=True)
                    ins.then_inc(sem, 1)
                pe.wait_ge(q_eff_ready, 1)
                pe.wait_ge(trans_ready, CPB)
                pe.wait_ge(kv_masked, CPB)
                for t in range(1, CH):
                    for s in range(NSEQ):
                        if t > 1:
                            pe.wait_ge(s_saved, NSEQ * (t - 2) + s + 1)
                        b, n = 2 * s + t // CPB, t % CPB
                        now = kv[:, 0, 2 * s, :] if t == 1 else state[:, t % 2, s, :]
                        if t < CH - 1:
                            pe.matmul(bank[2 + s][:, 0, :], trans[:, n, b, :], now, start=True, stop=True).then_inc(s_ready, 1)
                        cols = slice(n * CHUNK, (n + 1) * CHUNK)
                        ins = pe.matmul(bank[1][:, b, cols], now, q_eff[:, b, cols], start=False, stop=True,
                                        skip_group_check=True)
                ins.then_inc(o_ready, 1)
                pe.wait_ge(o_saved, 1)
                pe.wait_ge(wk_masked, CPB)
                for b in range(GB):
                    ins = pe.transpose(bank[4][:, b, :], o_ch[:, b, :], c.ident[:, :])
                ins.then_inc(o_turned, 1)
                pe.wait_ge(normed, 1)
                for b in range(GB):
                    ins = pe.transpose(bank[5][:, b, :], o[:, b, :], c.ident[:, :])
                ins.then_inc(n_turned, 1)
                pe.wait_ge(n_saved, 1)
                for b in range(GB):
                    ins = pe.matmul(bank[6][:, b, :], o_ch[:, b, :], w_o[:, :], start=True, stop=True)
                ins.then_inc(out_ready, 1)

            @block.vector
            def _(dve):
                link = Chain(dve, dve_step)
                wide = [P, GB, HEADS, HD]
                dve.wait_ge(tok_loaded, 48)
                by_head = lambda t: t[:, :, :].rearrange("p b (h x) -> p b h x", h=HEADS)
                for n, src in enumerate((v_tok, k_tok)):
                    dve.tensor_tensor(vk[:, :, :, n * HD:(n + 1) * HD], by_head(src),
                                      beta[:, :, 0:HEADS].unsqueeze(3).to_broadcast(wide), ALU.mult).then_inc(vk_ready, 1)
                spread = [P, GB, P]
                for h in range(HEADS):
                    dve.wait_ge(attn_ready, h + 1)
                    dve.tensor_tensor(attn[:, h, :, :], bank[h][:, :, :], m.causal[:, :].unsqueeze(1).to_broadcast(spread), ALU.mult)\
                       .then_inc(attn_masked, 1)
                for n in range(CPB):
                    dve.wait_ge(kv_ready, n + 1)
                    dve.tensor_tensor(kv[:, n, :, :], bank[n][:, :, :], m.same[:, :].unsqueeze(1).to_broadcast(spread), ALU.mult)\
                       .then_inc(kv_masked, 1)
                for n in range(CPB):
                    dve.wait_ge(wk_ready, n + 1)
                    dve.tensor_tensor(trans[:, n, :, :], bank[4 + n][:, :, :], m.minus_same[:, :].unsqueeze(1).to_broadcast(spread),
                                      ALU.mult).then_inc(wk_masked, 1)
                dve.wait_ge(qw_ready, 1)
                dve.tensor_tensor(q_eff[:, :, :], q[:, :].rearrange("p (a b) -> p a b", a=GB), bank[0][:, :, :], ALU.subtract)\
                   .then_inc(q_eff_ready, 1)
                for t in range(1, CH - 1):
                    for s in range(NSEQ):
                        b, n = 2 * s + t // CPB, t % CPB
                        dve.wait_ge(s_ready, NSEQ * (t - 1) + s + 1)
                        dve.tensor_tensor(state[:, (t + 1) % 2, s, :], bank[2 + s][:, 0, :], kv[:, n, b, :], ALU.add)\
                           .then_inc(s_saved, 1)
                dve.wait_ge(o_turned, 1)
                link(dve.tensor_tensor(o[:, :, :], bank[4][:, :, :], v_tok[:, :, :], ALU.subtract))
                link(dve.tensor_tensor(by_head(o), by_head(o), beta[:, :, HEADS:].unsqueeze(3).to_broadcast(wide), ALU.mult))
                dve.tensor_tensor(o[:, :, :], o[:, :, :], v_tok[:, :, :], ALU.add).then_inc(mixed, 1)
                dve.wait_ge(squared, 1)
                dve.tensor_reduce(power[:, :], square, AX.X, ALU.add).then_inc(power_sum, 1)
                dve.wait_ge(power_ready, 1)
                heads = o[:, :, :].rearrange("p b (h x) -> p (b h) x", h=HEADS)
                dve.tensor_tensor(heads, heads, power[:, :].unsqueeze(2).to_broadcast([P, GB * HEADS, HD]), ALU.mult)\
                   .then_inc(normed, 1)

            @block.gpsimd
            def _(pool):
                link = Chain(pool, pool_step)
                for n in range(CPB):
                    pool.wait_ge(wk_masked, n + 1)
                    pool.tensor_tensor(trans[:, n, :, :], trans[:, n, :, :], c.ident[:, :].unsqueeze(1).to_broadcast([P, GB, P]),
                                       ALU.add).then_inc(trans_ready, 1)
                pool.wait_ge(power_sum, 1)
                link(pool.tensor_scalar(power[:, :], power[:, :], 1.0 / HD, LN_EPS, ALU.mult, ALU.add))
                pool.tensor_tensor(power[:, :], power[:, :], half[:, :], ALU.pow).then_inc(power_ready, 1)


def layer0_attention(nc, c, st, a):
    with ExitStack() as ctx:
        mem = Memory(nc, ctx)
        w3 = mem.sb("l0_w_qkv", [P, 3, P])
        taps = mem.sb("l0_taps", [P, 3, 4])
        w_b = mem.sb("l0_w_beta", [P, P])
        w_gates = mem.sb("l0_w_gates", [P, 2 * HEADS])
        w_o = mem.sb("l0_w_o", [P, D])
        norm_w = mem.sb("l0_norm_w", [P, 1])
        m = DeltaState(nc, mem)
        load(nc, [(w3[:, 0, :], a["L0_attn_Wq"]), (w3[:, 1, :], a["L0_attn_Wk"]), (w3[:, 2, :], a["L0_attn_Wv"]),
                  (taps[:, 0, :], a["L0_attn_conv_q"]), (taps[:, 1, :], a["L0_attn_conv_k"]), (taps[:, 2, :], a["L0_attn_conv_v"]),
                  (w_b[:, :], a["L0_attn_Wb_wide"]), (w_gates[:, 0:HEADS], a["L0_attn_Wb"]), (w_gates[:, HEADS:], a["L0_attn_Wmix"]),
                  (w_o[:, :], a["L0_attn_Wo"]), (norm_w[:, :], a["L0_attn_norm_w"])])
        delta_masks(nc, m)
        gates(nc, st, m, w_b, w_gates)
        project(nc, c, st, m, w3, taps)
        invert(nc, m)
        recur(nc, c, st, m, w_o, norm_w)


def attention16(nc, c, st, a):
    HEADS, HD, QUAD = 16, 8, 32
    Q = HEADS // 4
    SCALE = HD ** -0.5
    NB = 4
    ALL = NB * HEADS
    PLAN = [("qk", n, 4 * n - 4) for n in range(Q)] + [("v", 0, -3), ("v", 1, -1), ("out", 0, HEADS + 5)]
    jobs = {}
    for b in range(NB):
        for what, n, at in PLAN:
            jobs.setdefault(max(b * HEADS + at, 0), []).append((what, b, n))
    last = max(jobs) + 1
    order = [job for t in sorted(jobs) for job in jobs[t]]
    turn_of = {job: n for n, job in enumerate(order)}
    by_act = [sum(j[0] != "out" for j in order[:n]) for n in range(len(order) + 1)]
    by_dve = [n - m for n, m in enumerate(by_act)]
    with ExitStack() as ctx:
        mem = Memory(nc, ctx)
        wq = mem.sb("l0a_wq", [P, HEADS, QUAD])
        wk = mem.sb("l0a_wk", [P, HEADS, QUAD])
        wv = mem.sb("l0a_wv", [P, HEADS, QUAD])
        wo = mem.sb("l0a_wo", [P, Q, D])
        bq = mem.sb("l0a_bq", [P, Q])
        bk = mem.sb("l0a_bk", [P, Q])
        bv = mem.sb("l0a_bv", [P, Q])
        bo = mem.sb("l0a_bo", [P, D])
        with phase(nc, ["l0a_clear"]) as (block, _, (clear,)):
            @block.gpsimd
            def _(pool):
                for t in (wq, wk, wv, wo):
                    pool.memset(t[:, :, :], 0.0).then_inc(clear, 1)
                for t in (bq, bk, bv):
                    pool.memset(t[:, :], 0.0).then_inc(clear, 1)
                pool.wait_ge(clear, 7)
        pairs = [(wq[:, :, 0:HD], a["L0_ffn_Wq"]), (wk[:, :, 0:HD], a["L0_ffn_Wk"]), (wv[:, :, 0:HD], a["L0_ffn_Wv"]),
                 (bo[:, :], a["L0_ffn_bo"])]
        for s in range(4):
            rows = slice(QUAD * s, QUAD * s + HD)
            pairs += [(bq[rows, :], a["L0_ffn_bq"][s]), (bk[rows, :], a["L0_ffn_bk"][s]), (bv[rows, :], a["L0_ffn_bv"][s]),
                      (wo[rows, :, :], a["L0_ffn_Wo"][s])]
        load(nc, pairs)
        with phase(nc, ["l0a_scaled"]) as (block, _, (scaled,)):
            @block.vector
            def _(dve):
                dve.tensor_scalar(bq[:, :], bq[:, :], SCALE, None, ALU.mult).then_inc(scaled, 1)
        xs = mem.sb("l0a_x", [P, 2, SEQ])
        q = mem.sb("l0a_q", [P, 2, Q, SEQ])
        k = mem.sb("l0a_k", [P, 2, Q, SEQ])
        v = mem.sb("l0a_v", [P, 2, 2, HEADS * QUAD])
        prob = mem.sb("l0a_prob", [P, 3, 2, SEQ])
        turned = mem.sb("l0a_prob_t", [P, 2, 2, SEQ])
        neg_max = mem.sb("l0a_neg_max", [P, 4, 2])
        total = mem.sb("l0a_total", [P, 4, 2])
        z = mem.sb("l0a_z", [P, 2, Q, SEQ])
        ps = [mem.psum(f"l0a_ps{n}", [P, 2, SEQ]) for n in range(3)]
        pt = [mem.psum(f"l0a_pt{n}", [P, 2, SEQ]) for n in range(2)]
        pz = [mem.psum(f"l0a_pz{n}", [P, SEQ]) for n in range(2)]
        px = mem.psum("l0a_px", [P, 512])
        names = ["l0a_" + n for n in ("x_ready", "job_ready", "job_saved", "out_saved", "scores_ready", "max_ready", "exp_ready",
                                      "dve_step", "prob_ready", "turn_ready", "turned_saved", "z_ready", "z_saved")]
        with phase(nc, names, BATCH // NB) as (block, i, sems):
            (x_ready, job_ready, job_saved, out_saved, scores_ready, max_ready, exp_ready, dve_step, prob_ready, turn_ready,
             turned_saved, z_ready, z_saved) = sems

            @block.gpsimd
            def _(pool):
                for b in range(NB):
                    if b >= 2:
                        pool.wait_ge(job_ready, turn_of["qk", b - 2, Q - 1] + 1)
                    pool.tensor_copy(xs[:, b % 2, :], st.xnt[:, bass.ds(i * (NB * SEQ) + b * SEQ, SEQ)]).then_inc(x_ready, 1)

            @block.tensor
            def _(pe):
                def job(what, b, n):
                    m = turn_of[what, b, n]
                    if by_act[m]:
                        pe.wait_ge(job_saved, by_act[m])
                    if by_dve[m]:
                        pe.wait_ge(out_saved, by_dve[m])
                    if what == "out":
                        pe.wait_ge(z_saved, Q * (b + 1))
                        for t in range(2):
                            for g in range(Q):
                                ins = pe.matmul(px[:, t * P:(t + 1) * P], z[:, b % 2, g, t * P:(t + 1) * P], wo[:, g, :],
                                                start=(g == 0), stop=(g == Q - 1))
                    else:
                        pe.wait_ge(x_ready, b + 1)
                        x = xs[:, b % 2, :]
                    if what == "qk":
                        pe.matmul(px[:, 0:SEQ], wq[:, 4 * n:4 * n + 4, :], x, start=True, stop=True)
                        ins = pe.matmul(px[:, SEQ:], wk[:, 4 * n:4 * n + 4, :], x, start=True, stop=True)
                    if what == "v":
                        ins = pe.matmul(px[:, :], x[:, n * P:(n + 1) * P], wv[:, :, :], start=True, stop=True)
                    ins.then_inc(job_ready, 1)

                def scores(m):
                    b, h = m // HEADS, m % HEADS
                    if h % 4 == 0:
                        pe.wait_ge(job_saved, by_act[turn_of["qk", b, h // 4] + 1])
                    if m >= 3:
                        pe.wait_ge(exp_ready, 2 * (m - 2))
                    rows = slice(QUAD * (h % 4), QUAD * (h % 4) + QUAD)
                    for t in range(2):
                        ins = pe.matmul(ps[m % 3][:, t, :], q[rows, b % 2, h // 4, t * P:(t + 1) * P], k[rows, b % 2, h // 4, :],
                                        start=True, stop=True)
                    ins.then_inc(scores_ready, 1)

                def turn(m):
                    pe.wait_ge(prob_ready, 2 * m + 2)
                    if m >= 2:
                        pe.wait_ge(turned_saved, m - 1)
                    for t in range(2):
                        for s in range(2):
                            ins = pe.transpose(pt[m % 2][:, s, t * P:(t + 1) * P], prob[:, m % 3, t, s * P:(s + 1) * P],
                                               c.ident[:, :])
                    ins.then_inc(turn_ready, 1)

                def weigh(m):
                    b, h = m // HEADS, m % HEADS
                    g = m // 4
                    if h == 0:
                        pe.wait_ge(job_saved, by_act[turn_of["v", b, 1] + 1])
                    if h % 4 == 0 and g >= 2:
                        pe.wait_ge(z_saved, g - 1)
                    pe.wait_ge(turned_saved, m + 1)
                    rows = slice(QUAD * (h % 4), QUAD * (h % 4) + QUAD)
                    for s in range(2):
                        ins = pe.matmul(pz[g % 2][rows, :], v[:, b % 2, s, h * QUAD:(h + 1) * QUAD], turned[:, m % 2, s, :],
                                        start=(s == 0), stop=(s == 1))
                    ins.then_inc(z_ready, 1)

                for m in range(max(ALL + 3, last)):
                    for j in jobs.get(m, []):
                        job(*j)
                    if m < ALL:
                        scores(m)
                    if 0 <= m - 2 < ALL:
                        turn(m - 2)
                    if 0 <= m - 3 < ALL:
                        weigh(m - 3)

            @block.scalar
            def _(act):
                def save(what, b, n):
                    act.wait_ge(job_ready, turn_of[what, b, n] + 1)
                    if what == "qk":
                        if b >= 2:
                            act.wait_ge(scores_ready, HEADS * (b - 2) + 4 * n + 4)
                        act.activation(q[:, b % 2, n, :], px[:, 0:SEQ], ACT.Identity, bias=bq[:, n:n + 1], scale=SCALE)
                        act.activation(k[:, b % 2, n, :], px[:, SEQ:], ACT.Identity, bias=bk[:, n:n + 1]).then_inc(job_saved, 1)
                    else:
                        if b >= 2:
                            act.wait_ge(z_ready, HEADS * (b - 1))
                        act.activation(v[:, b % 2, n, :], px[:, :], ACT.Copy).then_inc(job_saved, 1)

                def exp(m):
                    act.wait_ge(max_ready, m + 1)
                    if m >= 3:
                        act.wait_ge(turn_ready, m - 2)
                    for t in range(2):
                        act.activation(prob[:, m % 3, t, :], ps[m % 3][:, t, :], ACT.Exp, bias=neg_max[:, m % 4, t:t + 1],
                                       accum_out=total[:, m % 4, t:t + 1]).then_inc(exp_ready, 1)

                def save_z(g):
                    b = g // Q
                    act.wait_ge(z_ready, 4 * g + 4)
                    if b >= 2 and g % Q == 0:
                        act.wait_ge(job_ready, turn_of["out", b - 2, 0] + 1)
                    act.activation(z[:, b % 2, g % Q, :], pz[g % 2][:, :], ACT.Identity, bias=bv[:, g % Q:g % Q + 1])\
                       .then_inc(z_saved, 1)

                for m in range(max(ALL + 4, last)):
                    for j in jobs.get(m, []):
                        if j[0] != "out":
                            save(*j)
                    if m < ALL:
                        exp(m)
                    if m >= 7 and m % 4 == 3 and m // 4 - 1 < ALL // 4:
                        save_z(m // 4 - 1)

            @block.vector
            def _(dve):
                link = Chain(dve, dve_step)
                for m in range(max(ALL + 2, last)):
                    if m < ALL:
                        dve.wait_ge(scores_ready, m + 1)
                        dve.tensor_reduce(neg_max[:, m % 4, :], ps[m % 3][:, :, :], AX.X, ALU.max, negate=True).then_inc(max_ready, 1)
                    if 1 <= m <= ALL:
                        n = m - 1
                        dve.wait_ge(exp_ready, 2 * n + 2)
                        link(dve.reciprocal(total[:, n % 4, :], total[:, n % 4, :]))
                        for t in range(2):
                            dve.tensor_scalar(prob[:, n % 3, t, :], prob[:, n % 3, t, :], total[:, n % 4, t:t + 1], None, ALU.mult)\
                               .then_inc(prob_ready, 1)
                    if 2 <= m < ALL + 2:
                        n = m - 2
                        dve.wait_ge(turn_ready, n + 1)
                        if n >= 2:
                            dve.wait_ge(z_ready, n - 1)
                        dve.tensor_copy(turned[:, n % 2, :, :], pt[n % 2][:, :, :]).then_inc(turned_saved, 1)
                    for what, b, n in jobs.get(m, []):
                        if what == "out":
                            rows = st.g[:, bass.ds(i * (2 * NB) + 2 * b, 2), :]
                            dve.wait_ge(job_ready, turn_of[what, b, n] + 1)
                            ins = dve.tensor_tensor(rows, px[:, 0:2 * P].rearrange("p (a b) -> p a b", a=2),
                                                    bo[:, :].unsqueeze(1).to_broadcast([P, 2, D]), ALU.add)
                            ins.then_inc(out_saved, 1)
                            dve.wait_ge(out_saved, b + 1)
                            dve.tensor_tensor(rows, rows, st.xn[:, bass.ds(i * (2 * NB) + 2 * b, 2), :], ALU.add)


def layer0_ffn(nc, c, st, a):
    E, F = 8, 256
    U = E * F // P
    attention16(nc, c, st, a)
    with ExitStack() as ctx:
        mem = Memory(nc, ctx)
        w1 = mem.sb("l0f_w1", [P, U, P])
        w2 = mem.sb("l0f_w2", [P, U, D])
        b1 = mem.sb("l0f_b1", [P, U])
        b2 = mem.sb("l0f_b2", [E, D])
        gw = mem.sb("l0f_gw", [P, E])
        gb = mem.sb("l0f_gb", [P, E])
        norms = mem.sb("l0f_norms", [P, 4, D])
        w_tok = mem.sb("l0f_w_tok", [P, BLK, E])
        h_tok = mem.sb("l0f_h_tok", [P, BLK, D])
        h_ch = mem.sb("l0f_h_ch", [P, TOK])
        load(nc, [(w1[:, :, :], a["L0_ffn_W1"]), (w2[:, :, :], a["L0_ffn_W2"]), (b1[:, :], a["L0_ffn_b1"]),
                  (b2[:, :], a["L0_ffn_b2"]), (gw[:, :], a["L0_ffn_gW"]), (gb[:, :], a["L0_ffn_gb"]),
                  (norms[:, 0, :], a["L0_ffn_ln1_g"]), (norms[:, 1, :], a["L0_ffn_ln1_b"]),
                  (norms[:, 2, :], a["L0_ffn_ln2_g"]), (norms[:, 3, :], a["L0_ffn_ln2_b"])])
        layer_norm(nc, c, "l0n1", st.g, h_tok, h_ch, norms[:, 0, :], norms[:, 1, :])
        top_two(nc, c, st, "l0r", h_ch, gw, gb, E, w_tok, softmax=True)
        experts(nc, c, st, "l0e", h_ch, w_tok, E, F // P, ACT.Relu, w1, w2, b1=b1, b2=b2, residual=h_tok)
        layer_norm(nc, c, "l0n2", st.g, st.g, None, norms[:, 2, :], norms[:, 3, :])


def layer1_attention(nc, c, st, a):
    INNER, STATES, TAPS = 256, 16, 4
    CH = INNER // P
    PAD = TAPS - 1
    NSEQ = GT // SEQ
    with ExitStack() as ctx:
        mem = Memory(nc, ctx)
        w_in = mem.sb("l1_w_in", [P, 2 * CH, P])
        conv_w = mem.sb("l1_conv_w", [P, CH, TAPS])
        conv_b = mem.sb("l1_conv_b", [P, CH])
        w_b = mem.sb("l1_w_b", [P, CH, STATES])
        w_c = mem.sb("l1_w_c", [STATES, CH, P])
        w_out = mem.sb("l1_w_out", [P, CH, D])
        load(nc, [(w_in[:, :, :], a["L1_attn_w_in"]), (conv_w[:, :, :], a["L1_attn_conv_w"]), (conv_b[:, :], a["L1_attn_conv_b"]),
                  (w_b[:, :, :], a["L1_attn_w_B"]), (w_c[:, :, :], a["L1_attn_w_C"]), (w_out[:, :, :], a["L1_attn_w_out"])])
        padded = mem.sb("l1_padded", [P, CH, NSEQ, PAD + SEQ])
        conv = mem.sb("l1_conv", [P, CH, NSEQ, SEQ])
        zs = mem.sb("l1_zs", [P, CH, GT])
        decay = mem.sb("l1_decay", [STATES, SEQ])
        drive = mem.sb("l1_drive", [STATES, NSEQ, SEQ])
        state = mem.sb("l1_state", [STATES, NSEQ, SEQ])
        yz = mem.sb("l1_yz", [P, CH, GT])
        p_in = [mem.psum(f"l1_p_in{n}", [P, NSEQ, SEQ]) for n in range(2 * CH)]
        p_b = mem.psum("l1_p_b", [STATES, NSEQ, SEQ])
        p_y = [mem.psum(f"l1_p_y{n}", [P, GT]) for n in range(CH)]
        p_o = mem.psum("l1_p_o", [P, GB, D])
        with phase(nc, ["l1_set"]) as (block, _, (l1_set,)):
            @block.gpsimd
            def _(pool):
                pool.memset(padded[:, :, :, :], 0.0).then_inc(l1_set, 1)
                pool.memset(decay[:, :], 0.9).then_inc(l1_set, 1)
                pool.wait_ge(l1_set, 2)
        names = ["l1_" + n for n in ("in_ready", "x_saved", "z_saved", "dve_step", "conv_ready", "xc_ready", "b_ready",
                                     "drive_ready", "state_ready", "y_ready", "yz_ready", "o_ready")]
        with phase(nc, names, GRP) as (block, i, sems):
            (in_ready, x_saved, z_saved, dve_step, conv_ready, xc_ready, b_ready, drive_ready, state_ready, y_ready,
             yz_ready, o_ready) = sems

            @block.tensor
            def _(pe):
                for n in range(2 * CH):
                    pe.matmul(p_in[n][:, :, :], w_in[:, n, :], st.xnt[:, bass.ds(i * GT, GT)], start=True, stop=True)\
                      .then_inc(in_ready, 1)
                for n in range(CH):
                    pe.wait_ge(xc_ready, n + 1)
                    ins = pe.matmul(p_b[:, :, :], w_b[:, n, :], conv[:, n, :, :], start=(n == 0), stop=(n == CH - 1))
                ins.then_inc(b_ready, 1)
                pe.wait_ge(state_ready, NSEQ)
                for n in range(CH):
                    pe.matmul(p_y[n][:, :], w_c[:, n, :], state[:, :, :], start=True, stop=True).then_inc(y_ready, 1)
                pe.wait_ge(yz_ready, CH)
                for j in range(GB):
                    for n in range(CH):
                        ins = pe.matmul(p_o[:, j, :], yz[:, n, j * P:(j + 1) * P], w_out[:, n, :],
                                        start=(n == 0), stop=(n == CH - 1))
                ins.then_inc(o_ready, 1)

            @block.scalar
            def _(act):
                for n in range(CH):
                    act.wait_ge(in_ready, n + 1)
                    act.activation(padded[:, n, :, PAD:], p_in[n][:, :, :], ACT.Copy).then_inc(x_saved, 1)
                for n in range(CH):
                    act.wait_ge(in_ready, CH + n + 1)
                    act.activation(zs[:, n, :].rearrange("p (a b) -> p a b", a=NSEQ), p_in[CH + n][:, :, :], ACT.Silu)\
                       .then_inc(z_saved, 1)
                for n in range(CH):
                    act.wait_ge(conv_ready, n + 1)
                    act.activation(conv[:, n, :, :], conv[:, n, :, :], ACT.Silu, bias=conv_b[:, n:n + 1]).then_inc(xc_ready, 1)
                act.wait_ge(b_ready, 1)
                act.activation(drive[:, :, :], p_b[:, :, :], ACT.Copy, scale=0.1).then_inc(drive_ready, 1)
                act.wait_ge(o_ready, 1)
                act.activation(st.s[:, bass.ds(i * GB, GB), :], p_o[:, :, :], ACT.Copy)

            @block.vector
            def _(dve):
                link = Chain(dve, dve_step)
                for n in range(CH):
                    dve.wait_ge(x_saved, n + 1)
                    out = conv[:, n, :, :]
                    for k in range(TAPS):
                        x = padded[:, n, :, k:k + SEQ]
                        if k == 0:
                            link(dve.tensor_scalar(out, x, conv_w[:, n, k:k + 1], None, ALU.mult))
                        else:
                            ins = dve.scalar_tensor_tensor(out, x, conv_w[:, n, k:k + 1], out, ALU.mult, ALU.add)
                            if k < TAPS - 1:
                                link(ins)
                    ins.then_inc(conv_ready, 1)
                dve.wait_ge(drive_ready, 1)
                for s in range(NSEQ):
                    dve.tensor_tensor_scan(state[:, s, :], decay[:, :], drive[:, s, :], 0.0, ALU.mult, ALU.add)\
                       .then_inc(state_ready, 1)
                for n in range(CH):
                    dve.wait_ge(y_ready, n + 1)
                    dve.wait_ge(z_saved, n + 1)
                    dve.tensor_tensor(yz[:, n, :], p_y[n][:, :], zs[:, n, :], ALU.mult).then_inc(yz_ready, 1)


def layer1_ffn(nc, c, st, a):
    E, H = 8, 256
    with ExitStack() as ctx:
        mem = Memory(nc, ctx)
        w1 = mem.sb("l1f_w1", [P, E * H // P, P])
        w3 = mem.sb("l1f_w3", [P, E * H // P, P])
        w2 = mem.sb("l1f_w2", [P, E * H // P, D])
        gw = mem.sb("l1f_gw", [P, E])
        w_tok = mem.sb("l1f_w_tok", [P, BLK, E])
        load(nc, [(w1[:, :, :], a["L1_ffn_W1"]), (w3[:, :, :], a["L1_ffn_W3"]), (w2[:, :, :], a["L1_ffn_W2"]),
                  (gw[:, :], a["L1_ffn_Wg"])])
        with ExitStack() as inner:
            mem = Memory(nc, inner)
            score = mem.sb("l1f_score", [P, E, BLK])
            chosen = mem.sb("l1f_chosen", [P, E, BLK])
            token_scores(nc, "l1f", st.xnt, gw, E, score)
            choose(nc, c, "l1c", score, chosen, E, TOK // E)
            softmax_of_chosen(nc, c, score, chosen, w_tok, E)
        experts(nc, c, st, "l1e", st.xnt, w_tok, E, H // P, ACT.Silu, w1, w2, w3=w3)


def softmax_of_chosen(nc, c, score, chosen, w_tok, n_exp):
    with ExitStack() as ctx:
        mem = Memory(nc, ctx)
        best = mem.sb("l1s_best", [P, n_exp])
        top = mem.sb("l1s_top", [P, n_exp])
        part = mem.sb("l1s_part", [P, n_exp])
        recip = mem.sb("l1s_recip", [P, n_exp])
        p_sum = mem.psum("l1s_sum", [P, n_exp])
        wide = [P, n_exp, BLK]
        with phase(nc, ["l1s_dve_step", "l1s_best_ready", "l1s_top_ready", "l1s_shifted", "l1s_exp_ready", "l1s_part_ready",
                        "l1s_sum_ready"]) as (block, _, sems):
            dve_step, best_ready, top_ready, shifted, exp_ready, part_ready, sum_ready = sems

            @block.vector
            def _(dve):
                link = Chain(dve, dve_step)
                dve.tensor_reduce(best[:, :], score[:, :, :], AX.X, ALU.max).then_inc(best_ready, 1)
                dve.wait_ge(top_ready, 1)
                dve.tensor_tensor(score[:, :, :], score[:, :, :], top[:, :].unsqueeze(2).to_broadcast(wide), ALU.subtract)\
                   .then_inc(shifted, 1)
                dve.wait_ge(exp_ready, 1)
                link(dve.tensor_tensor(score[:, :, :], score[:, :, :], chosen[:, :, :], ALU.mult))
                dve.tensor_reduce(part[:, :], score[:, :, :], AX.X, ALU.add).then_inc(part_ready, 1)
                dve.wait_ge(sum_ready, 1)
                link(dve.reciprocal(recip[:, :], p_sum[:, :]))
                link(dve.tensor_tensor(w_tok[:, :, :].rearrange("p b e -> p e b"), score[:, :, :],
                                       recip[:, :].unsqueeze(2).to_broadcast(wide), ALU.mult))

            @block.gpsimd
            def _(pool):
                pool.wait_ge(best_ready, 1)
                pool.partition_all_reduce(top[:, :], best[:, :], P, bass.bass_isa.ReduceOp.max).then_inc(top_ready, 1)

            @block.scalar
            def _(act):
                act.wait_ge(shifted, 1)
                act.activation(score[:, :, :], score[:, :, :], ACT.Exp).then_inc(exp_ready, 1)

            @block.tensor
            def _(pe):
                pe.wait_ge(part_ready, 1)
                pe.matmul(p_sum[:, :], c.ones[:, :], part[:, :], start=True, stop=True).then_inc(sum_ready, 1)


WINDOW = 16
BEFORE = (WINDOW - 1) // 2
PITCH = SEQ + WINDOW


def layer2_attention(nc, c, st, a):
    KG = 4
    with ExitStack() as ctx:
        mem = Memory(nc, ctx)
        band = nc.dram_tensor("l2_band", (BATCH * SEQ * PITCH,), F32, kind="Internal").ap()
        w1 = mem.sb("l2_w1", [P, D])
        w2 = mem.sb("l2_w2", [P, D])
        v = mem.sb("l2_v", [P, 1])
        zero = mem.sb("l2_zero", [P, 2, PITCH])
        padded = mem.sb("l2_padded", [P, WINDOW - 1 + SEQ])
        load(nc, [(w1[:, :], a["L2_attn_w1"]), (w2[:, :], a["L2_attn_w2"]), (v[:, :], a["L2_attn_v"])])
        with phase(nc, ["l2_zero_set", "l2_band_cleared"]) as (block, _, (zero_set, band_cleared)):
            @block.gpsimd
            def _(pool):
                pool.memset(zero[:, :, :], 0.0).then_inc(zero_set, 1)
                pool.memset(padded[:, :], 0.0).then_inc(zero_set, 1)

            @block.sync
            def _(sp):
                sp.wait_ge(zero_set, 2)
                for b in range(BATCH):
                    rows = band[b * SEQ * PITCH:(b + 1) * SEQ * PITCH].rearrange("(t p n) -> p t n", t=2, p=P)
                    sp.dma_start(rows, zero[:, :, :]).then_inc(band_cleared, 16)
                sp.wait_ge(band_cleared, 16 * BATCH)

        with ExitStack() as inner:
            mem = Memory(nc, inner)
            q = mem.sb("l2_q", [P, SEQ])
            th = mem.sb("l2_tanh", [P, WINDOW, SEQ])
            prob = mem.sb("l2_prob", [P, 2, WINDOW])
            small = mem.sb("l2_small", [P, 2])
            pp = mem.psum("l2_pp", [P, SEQ])
            pq = mem.psum("l2_pq", [P, SEQ])
            ps = mem.psum("l2_ps", [P, 2, WINDOW])
            names = ["l2_" + n for n in ("proj_ready", "p_saved", "q_saved", "sum_ready", "tanh_ready", "score_ready", "dve_step",
                                         "shifted", "exp_ready", "weight_ready", "stored")]
            with phase(nc, names, BATCH) as (block, i, sems):
                (proj_ready, p_saved, q_saved, sum_ready, tanh_ready, score_ready, dve_step, shifted, exp_ready, weight_ready,
                 stored) = sems

                @block.tensor
                def _(pe):
                    x = st.xnt[:, bass.ds(i * SEQ, SEQ)]
                    pe.matmul(pp[:, :], w2[:, :], x, start=True, stop=True).then_inc(proj_ready, 1)
                    pe.matmul(pq[:, :], w1[:, :], x, start=True, stop=True).then_inc(proj_ready, 1)
                    for k in range(WINDOW):
                        pe.wait_ge(tanh_ready, k // KG + 1)
                        for t in range(2):
                            ins = pe.matmul(ps[:, t, k:k + 1], th[:, k, t * P:(t + 1) * P], v[:, :], start=True, stop=True)
                    ins.then_inc(score_ready, 1)

                @block.scalar
                def _(act):
                    act.wait_ge(proj_ready, 1)
                    act.activation(padded[:, BEFORE:BEFORE + SEQ], pp[:, :], ACT.Copy).then_inc(p_saved, 1)
                    for n in range(WINDOW // KG):
                        act.wait_ge(sum_ready, KG * (n + 1))
                        part = th[:, n * KG:(n + 1) * KG, :]
                        act.activation(part, part, ACT.Tanh).then_inc(tanh_ready, 1)
                    act.wait_ge(shifted, 1)
                    act.activation(prob[:, :, :], prob[:, :, :], ACT.Exp).then_inc(exp_ready, 1)

                @block.vector
                def _(dve):
                    link = Chain(dve, dve_step)
                    spread = small[:, :].unsqueeze(2).to_broadcast([P, 2, WINDOW])
                    dve.wait_ge(proj_ready, 2)
                    dve.tensor_copy(q[:, :], pq[:, :]).then_inc(q_saved, 1)
                    dve.wait_ge(q_saved, 1)
                    dve.wait_ge(p_saved, 1)
                    for k in range(WINDOW):
                        dve.tensor_tensor(th[:, k, :], padded[:, k:k + SEQ], q[:, :], ALU.add).then_inc(sum_ready, 1)
                    dve.wait_ge(score_ready, 1)
                    link(dve.tensor_reduce(small[:, :], ps[:, :, :], AX.X, ALU.max))
                    dve.tensor_tensor(prob[:, :, :], ps[:, :, :], spread, ALU.subtract).then_inc(shifted, 1)
                    dve.wait_ge(exp_ready, 1)
                    link(dve.tensor_reduce(small[:, :], prob[:, :, :], AX.X, ALU.add))
                    link(dve.reciprocal(small[:, :], small[:, :]))
                    dve.tensor_tensor(prob[:, :, :], prob[:, :, :], spread, ALU.mult).then_inc(weight_ready, 1)

                @block.sync
                def _(sp):
                    sp.wait_ge(weight_ready, 1)
                    rows = band[bass.ds(i * (SEQ * PITCH), SEQ * PITCH)]
                    for t in range(2):
                        dst = bass.AP(rows.tensor, rows.offset + t * P * (PITCH + 1), [[PITCH + 1, P], [1, WINDOW]])
                        sp.dma_start(dst, prob[:, t, :]).then_inc(stored, 16)
                    sp.wait_ge(stored, 32)

        with ExitStack() as inner:
            mem = Memory(nc, inner)
            NB = 2
            rows_sb = mem.sb("l2_rows", [P, 2 * NB, SEQ])
            turned = mem.sb("l2_turned", [P, 4 * NB, P])
            pt = [mem.psum(f"l2_pt{n}", [P, 4, P]) for n in range(NB)]
            po = mem.psum("l2_po", [P, 2 * NB, D])
            with phase(nc, ["l2_loaded", "l2_turn_ready", "l2_turn_saved", "l2_out_ready"], BATCH // NB) as (block, i, sems):
                loaded, turn_ready, turn_saved, out_ready = sems

                @block.sync
                def _(sp):
                    src = band[bass.ds(i * (NB * SEQ * PITCH), NB * SEQ * PITCH)].rearrange("(n p w) -> p n w", p=P, w=PITCH)
                    sp.dma_start(rows_sb[:, :, :], src[:, :, BEFORE:BEFORE + SEQ]).then_inc(loaded, 16)

                @block.tensor
                def _(pe):
                    pe.wait_ge(loaded, 16)
                    for n in range(NB):
                        for t in range(2):
                            for s in range(2):
                                ins = pe.transpose(pt[n][:, 2 * t + s, :], rows_sb[:, 2 * n + t, s * P:(s + 1) * P], c.ident[:, :])
                        ins.then_inc(turn_ready, 1)
                    for n in range(NB):
                        pe.wait_ge(turn_saved, n + 1)
                        for t in range(2):
                            for s in range(2):
                                ins = pe.matmul(po[:, 2 * n + t, :], turned[:, 4 * n + 2 * t + s, :],
                                                st.xn[:, i * (2 * NB) + 2 * n + s, :], start=(s == 0), stop=(s == 1))
                    ins.then_inc(out_ready, 1)

                @block.vector
                def _(dve):
                    for n in range(NB):
                        dve.wait_ge(turn_ready, n + 1)
                        dve.tensor_copy(turned[:, 4 * n:4 * n + 4, :], pt[n][:, :, :]).then_inc(turn_saved, 1)

                @block.scalar
                def _(act):
                    act.wait_ge(out_ready, 1)
                    act.activation(st.s[:, bass.ds(i * (2 * NB), 2 * NB), :], po[:, :, :], ACT.Copy)


def layer2_ffn(nc, c, st, a):
    E, F = 8, 512
    U = E * F // P
    with ExitStack() as ctx:
        mem = Memory(nc, ctx)
        w1 = mem.sb("l2f_w1", [P, U, P])
        w2 = mem.sb("l2f_w2", [P, U, D])
        b1 = mem.sb("l2f_b1", [P, U])
        b2 = mem.sb("l2f_b2", [E, D])
        cent = mem.sb("l2f_cent", [P, E])
        gain = mem.sb("l2f_gain", [P, D])
        shift = mem.sb("l2f_shift", [P, D])
        w_tok = mem.sb("l2f_w_tok", [P, BLK, E])
        norm_ch = mem.sb("l2f_norm_ch", [P, TOK])
        load(nc, [(w1[:, :, :], a["L2_ffn_w1"]), (w2[:, :, :], a["L2_ffn_w2"]), (b1[:, :], a["L2_ffn_b1"]),
                  (b2[:, :], a["L2_ffn_b2"]), (cent[:, :], a["L2_ffn_centroids"]), (gain[:, :], a["L2_ffn_ln_g"]),
                  (shift[:, :], a["L2_ffn_ln_b"])])
        layer_norm(nc, c, "l2n", st.xn, None, norm_ch, gain[:, :], shift[:, :])
        with ExitStack() as inner:
            mem = Memory(nc, inner)
            score = mem.sb("l2f_score", [P, E, BLK])
            chosen = mem.sb("l2f_chosen", [P, E, BLK])
            token_scores(nc, "l2f", norm_ch, cent, E, score)
            choose(nc, c, "l2c", score, chosen, E, TOK // E, in_turn=True)
            with phase(nc, ["l2f_w_ready"]) as (block, _, (w_ready,)):
                @block.vector
                def _(dve):
                    dve.tensor_copy(w_tok[:, :, :], chosen[:, :, :].rearrange("p e b -> p b e")).then_inc(w_ready, 1)
        experts(nc, c, st, "l2e", norm_ch, w_tok, E, F // P, ACT.Gelu_apprx_tanh, w1, w2, b1=b1, b2=b2, residual=st.xn)


def layer3_attention(nc, c, st, a):
    HEADS, HD = 16, 64
    PAIRS = HEADS // 2
    with ExitStack() as ctx:
        mem = Memory(nc, ctx)
        wq = mem.sb("l3_wq", [P, PAIRS, P])
        wk = mem.sb("l3_wk", [P, PAIRS, P])
        wv = mem.sb("l3_wv", [P, HEADS * HD])
        wo = mem.sb("l3_wo", [P, PAIRS, D])
        bq = mem.sb("l3_bq", [P, PAIRS])
        bk = mem.sb("l3_bk", [P, PAIRS])
        bv = mem.sb("l3_bv", [P, PAIRS])
        bo = mem.sb("l3_bo", [P, D])
        load(nc, [(wq[:, :, :], a["L3_attn_W_Q"]), (wk[:, :, :], a["L3_attn_W_K"]), (wv[:, :], a["L3_attn_W_V"]),
                  (wo[:, :, :], a["L3_attn_W_O"]), (bq[:, :], a["L3_attn_b_Q"]), (bk[:, :], a["L3_attn_b_K"]),
                  (bv[:, :], a["L3_attn_b_V"]), (bo[:, :], a["L3_attn_b_O"])])
        bq8 = mem.sb("l3_bq8", [P, PAIRS])
        with phase(nc, ["bias_ready"]) as (block, _, (bias_ready,)):
            @block.vector
            def _(dve):
                dve.tensor_scalar(bq8[:, :], bq[:, :], 1 / 8, None, ALU.mult).then_inc(bias_ready, 1)
        xs = mem.sb("l3_x", [P, SEQ])
        q = mem.sb("l3_q", [P, PAIRS, SEQ])
        k = mem.sb("l3_k", [P, PAIRS, SEQ])
        v = mem.sb("l3_v", [P, 2, HEADS * HD])
        prob = mem.sb("l3_prob", [P, 3, 3 * P])
        turned = mem.sb("l3_prob_t", [P, 2, 3 * P])
        neg_max = mem.sb("l3_neg_max", [P, HEADS, 2])
        total = mem.sb("l3_total", [P, HEADS, 2])
        z = mem.sb("l3_z", [P, PAIRS, SEQ])
        ps = [mem.psum(f"l3_ps{n}", [P, 512]) for n in range(3)]
        pt = [mem.psum(f"l3_pt{n}", [P, 512]) for n in range(2)]
        pz = [mem.psum(f"l3_pz{n}", [P, 512]) for n in range(2)]
        po = mem.psum("l3_po", [P, 2, D])
        names = ["l3_" + n for n in ("x_ready", "proj_ready", "q_saved", "k_saved", "scores_ready", "max_ready", "exp_ready",
                                     "recip_ready", "prob_ready", "turn_ready", "turned_saved", "z_ready", "z_saved",
                                     "out_ready")]
        with phase(nc, names, BATCH) as (block, i, sems):
            (x_ready, proj_ready, q_saved, k_saved, scores_ready, max_ready, exp_ready, recip_ready, prob_ready,
             turn_ready, turned_saved, z_ready, z_saved, out_ready) = sems

            @block.gpsimd
            def _(pool):
                pool.tensor_copy(xs[:, :], st.xnt[:, bass.ds(i * SEQ, SEQ)]).then_inc(x_ready, 1)
                for h in range(HEADS):
                    pool.wait_ge(recip_ready, h + 1)
                    row = prob[:, h % 3, :]
                    pool.tensor_scalar(row[:, 0:P], row[:, 0:P], total[:, h, 0:1], None, ALU.mult).then_inc(prob_ready, 1)
                    pool.tensor_scalar(row[:, P:], row[:, P:], total[:, h, 1:2], None, ALU.mult).then_inc(prob_ready, 1)

            @block.tensor
            def _(pe):
                pe.wait_ge(x_ready, 1)
                for n in range(PAIRS + 4):
                    if n >= 3:
                        pe.wait_ge(q_saved, n - 2)
                        pe.wait_ge(k_saved, min(n - 2, PAIRS))
                    bank = ps[n % 3]
                    if n < PAIRS:
                        pe.matmul(bank[:, 0:SEQ], wq[:, n, :], xs[:, :], start=True, stop=True)
                        pe.matmul(bank[:, SEQ:], wk[:, n, :], xs[:, :], start=True, stop=True).then_inc(proj_ready, 1)
                    else:
                        t, half = (n - PAIRS) // 2, n % 2
                        pe.matmul(bank[:, :], xs[:, t * P:(t + 1) * P], wv[:, half * 512:(half + 1) * 512],
                                  start=True, stop=True).then_inc(proj_ready, 1)
                pe.wait_ge(q_saved, PAIRS + 4)
                pe.wait_ge(k_saved, PAIRS)

                def scores(h):
                    if h >= 3:
                        pe.wait_ge(exp_ready, 2 * (h - 2))
                    rows = slice(HD * (h % 2), HD * (h % 2) + HD)
                    out, qh, kh = ps[h % 3], q[rows, h // 2, :], k[rows, h // 2, :]
                    pe.matmul(out[:, 0:P], qh[:, 0:P], kh[:, 0:P], start=True, stop=False)
                    pe.matmul(out[:, 0:P], c.ident_bf[:, :], c.future[:, :], start=False, stop=True)
                    pe.matmul(out[:, P:3 * P], qh[:, P:], kh[:, :], start=True, stop=False, skip_group_check=True)
                    pe.matmul(out[:, 2 * P:3 * P], c.ident_bf[:, :], c.future[:, :], start=False, stop=True,
                              skip_group_check=True).then_inc(scores_ready, 1)

                def turn(h):
                    pe.wait_ge(prob_ready, 2 * h + 2)
                    if h >= 2:
                        pe.wait_ge(turned_saved, h - 1)
                    for j in range(3):
                        ins = pe.transpose(pt[h % 2][:, j * P:(j + 1) * P], prob[:, h % 3, j * P:(j + 1) * P], c.ident[:, :])
                    ins.then_inc(turn_ready, 1)

                def weigh(h):
                    n, rows = h // 2, slice(HD * (h % 2), HD * (h % 2) + HD)
                    pe.wait_ge(turned_saved, h + 1)
                    if h % 2 == 0 and n >= 2:
                        pe.wait_ge(z_saved, n - 1)
                    out, cols = pz[n % 2], slice(h * HD, (h + 1) * HD)
                    pe.matmul(out[rows, 0:SEQ], v[:, 0, cols], turned[:, h % 2, 0:SEQ], start=True, stop=False,
                              skip_group_check=True)
                    pe.matmul(out[rows, P:SEQ], v[:, 1, cols], turned[:, h % 2, SEQ:], start=False, stop=True,
                              skip_group_check=True).then_inc(z_ready, 1)

                for h in range(HEADS + 3):
                    if h < HEADS:
                        scores(h)
                    if 0 <= h - 2 < HEADS:
                        turn(h - 2)
                    if 0 <= h - 3 < HEADS:
                        weigh(h - 3)
                pe.wait_ge(z_saved, PAIRS)
                for t in range(2):
                    for n in range(PAIRS):
                        ins = pe.matmul(po[:, t, :], z[:, n, t * P:(t + 1) * P], wo[:, n, :],
                                        start=(n == 0), stop=(n == PAIRS - 1))
                ins.then_inc(out_ready, 1)

            @block.scalar
            def _(act):
                for n in range(PAIRS + 4):
                    act.wait_ge(proj_ready, n + 1)
                    bank = ps[n % 3]
                    if n < PAIRS:
                        act.activation(q[:, n, :], bank[:, 0:SEQ], ACT.Identity, bias=bq8[:, n:n + 1], scale=1 / 8)\
                           .then_inc(q_saved, 1)
                    else:
                        t, half = (n - PAIRS) // 2, n % 2
                        act.activation(v[:, t, half * 512:(half + 1) * 512], bank[:, :], ACT.Copy).then_inc(q_saved, 1)

                def exp(h):
                    act.wait_ge(max_ready, 2 * h + 2)
                    if h >= 3:
                        act.wait_ge(turn_ready, h - 2)
                    row = prob[:, h % 3, :]
                    act.activation(row[:, 0:P], ps[h % 3][:, 0:P], ACT.Exp, bias=neg_max[:, h, 0:1],
                                   accum_out=total[:, h, 0:1]).then_inc(exp_ready, 1)
                    act.activation(row[:, P:], ps[h % 3][:, P:3 * P], ACT.Exp, bias=neg_max[:, h, 1:2],
                                   accum_out=total[:, h, 1:2]).then_inc(exp_ready, 1)

                def save_z(n):
                    act.wait_ge(z_ready, 2 * n + 2)
                    act.activation(z[:, n, :], pz[n % 2][:, 0:SEQ], ACT.Identity, bias=bv[:, n:n + 1]).then_inc(z_saved, 1)

                for h in range(HEADS + 3):
                    if h < HEADS:
                        exp(h)
                    if h >= 4 and h % 2 == 0:
                        save_z(h // 2 - 2)

            @block.vector
            def _(dve):
                for n in range(PAIRS):
                    dve.wait_ge(q_saved, n + 1)
                    dve.tensor_scalar(k[:, n, :], ps[n % 3][:, SEQ:], bk[:, n:n + 1], None, ALU.add).then_inc(k_saved, 1)

                def row_max(h):
                    dve.wait_ge(scores_ready, h + 1)
                    dve.tensor_reduce(neg_max[:, h, 0:1], ps[h % 3][:, 0:P], AX.X, ALU.max, negate=True).then_inc(max_ready, 1)
                    dve.tensor_reduce(neg_max[:, h, 1:2], ps[h % 3][:, P:3 * P], AX.X, ALU.max, negate=True).then_inc(max_ready, 1)

                for h in range(HEADS + 3):
                    if h < HEADS:
                        row_max(h)
                    if 0 <= h - 1 < HEADS:
                        dve.wait_ge(exp_ready, 2 * h)
                        dve.reciprocal(total[:, h - 1, :], total[:, h - 1, :]).then_inc(recip_ready, 1)
                    if 0 <= h - 2 < HEADS:
                        dve.wait_ge(turn_ready, h - 1)
                        if h >= 4:
                            dve.wait_ge(z_ready, h - 3)
                        dve.tensor_copy(turned[:, h % 2, :], pt[h % 2][:, 0:3 * P]).then_inc(turned_saved, 1)
                dve.wait_ge(out_ready, 1)
                dve.tensor_tensor(st.s[:, bass.ds(i * 2, 2), :], po[:, :, :],
                                  bo[:, :].unsqueeze(1).to_broadcast([P, 2, D]), ALU.add)


def layer3_ffn(nc, c, st, a):
    E = 6
    with ExitStack() as ctx:
        mem = Memory(nc, ctx)
        w1 = mem.sb("l3f_w1", [P, E + 1, P])
        w3 = mem.sb("l3f_w3", [P, E + 1, P])
        w2 = mem.sb("l3f_w2", [P, E + 1, D])
        gw = mem.sb("l3f_gw", [P, E])
        gb = mem.sb("l3f_gb", [P, E])
        w_tok = mem.sb("l3f_w_tok", [P, BLK, E + 1])
        load(nc, [(w1[:, 0:E, :], a["L3_ffn_ew1"]), (w3[:, 0:E, :], a["L3_ffn_ew3"]), (w2[:, 0:E, :], a["L3_ffn_ew2"]),
                  (w1[:, E, :], a["L3_ffn_fc1"]), (w3[:, E, :], a["L3_ffn_fc2"]), (w2[:, E, :], a["L3_ffn_fc3"]),
                  (gw[:, :], a["L3_ffn_gate_w"]), (gb[:, :], a["L3_ffn_gate_b"])])
        top_two(nc, c, st, "l3r", st.xnt, gw, gb, E, w_tok, softmax=False)
        with phase(nc, ["shared_weight"]) as (block, _, (shared_weight,)):
            @block.gpsimd
            def _(pool):
                pool.memset(w_tok[:, :, E:E + 1], 1.0).then_inc(shared_weight, 1)
                pool.wait_ge(shared_weight, 1)
        experts(nc, c, st, "l3e", st.xnt, w_tok, E + 1, 1, ACT.Silu, w1, w2, w3=w3)


def gated_stack(nc, a, out):
    with ExitStack() as ctx:
        mem = Memory(nc, ctx)
        c, st = Constants(mem), State(mem)
        constants(nc, c)
        load(nc, [(st.x[:, :, :], a["x"])])
        layers = ((layer0_attention, layer0_ffn), (layer1_attention, layer1_ffn), (layer2_attention, layer2_ffn),
                  (layer3_attention, layer3_ffn))
        for n, (mixer, ffn) in enumerate(layers):
            layer_norm(nc, c, f"norm{n}", st.x, st.xn, st.xnt)
            mixer(nc, c, st, a)
            ffn(nc, c, st, a)
            combine(nc, st, n)
        with phase(nc, ["out_stored"]) as (block, _, (out_stored,)):
            @block.sync
            def _(sp):
                sp.dma_start(out.rearrange("s (t p) d -> p (s t) d", p=P), st.x[:, :, :]).then_inc(out_stored, 16)
                sp.wait_ge(out_stored, 16)



def heads_in(w):
    n, m, d = w.shape
    return w.transpose(1, 0, 2).reshape(m, n * d // 128, 128)
def rows(b, n=128):
    return np.broadcast_to(b, (n,) + b.shape)
def units_t(w):
    e, f, ch = w.shape
    return w.transpose(2, 0, 1).reshape(ch, e * f // 128, 128)
def units(w):
    e, ch, f = w.shape
    return w.transpose(1, 0, 2).reshape(ch, e * f // 128, 128)
def down(w):
    e, f, o = w.shape
    return w.reshape(e * f // 128, 128, o).transpose(1, 0, 2)
def layout(i):
    o = {}
    o["x"] = i["L0_attn_hidden_states"].reshape(32, 128, 128).transpose(1, 0, 2)
    for n in ("Q", "K"):
        o[f"L3_attn_W_{n}"] = heads_in(i[f"L3_attn_W_{n}"])
        o[f"L3_attn_b_{n}"] = i[f"L3_attn_b_{n}"].reshape(8, 128).T
    o["L3_attn_W_V"] = heads_in(i["L3_attn_W_V"]).reshape(128, 1024)
    o["L3_attn_b_V"] = i["L3_attn_b_V"].reshape(8, 128).T
    o["L3_attn_W_O"] = i["L3_attn_W_O"].reshape(8, 128, 128).transpose(1, 0, 2)
    o["L3_attn_b_O"] = rows(i["L3_attn_b_O"])
    o["L3_ffn_ew1"] = units_t(i["L3_ffn_ew1"])
    o["L3_ffn_ew3"] = units_t(i["L3_ffn_ew3"])
    o["L3_ffn_ew2"] = i["L3_ffn_ew2"].transpose(2, 0, 1)
    o["L3_ffn_fc1"] = i["L3_ffn_fc1"].T
    o["L3_ffn_fc2"] = i["L3_ffn_fc2"].T
    o["L3_ffn_fc3"] = i["L3_ffn_fc3"].T
    o["L3_ffn_gate_w"] = i["L3_ffn_gate_w"].T
    o["L3_ffn_gate_b"] = rows(i["L3_ffn_gate_b"])
    for n in ("Wq", "Wk", "Wv", "Wb", "Wmix", "Wo"):
        o[f"L0_attn_{n}"] = i[f"L0_attn_{n}"].T
    o["L0_attn_Wb_wide"] = np.repeat(i["L0_attn_Wb"].T, 32, axis=1)
    for n in ("q", "k", "v"):
        o[f"L0_attn_conv_{n}"] = i[f"L0_attn_conv_{n}"]
    o["L0_attn_norm_w"] = np.broadcast_to(i["L0_attn_norm_w"], (4, 32)).reshape(128, 1)
    for n in ("Wq", "Wk", "Wv"):
        o[f"L0_ffn_{n}"] = i[f"L0_ffn_{n}"].reshape(128, 16, 8)
    for n in ("bq", "bk", "bv"):
        o[f"L0_ffn_{n}"] = i[f"L0_ffn_{n}"].reshape(4, 4, 8).transpose(1, 2, 0)
    o["L0_ffn_Wo"] = i["L0_ffn_Wo"].reshape(4, 4, 8, 128).transpose(1, 2, 0, 3)
    for n in ("bo", "gb", "ln1_g", "ln1_b", "ln2_g", "ln2_b"):
        o[f"L0_ffn_{n}"] = rows(i[f"L0_ffn_{n}"])
    o["L0_ffn_W1"] = units(i["L0_ffn_W1"])
    o["L0_ffn_b1"] = i["L0_ffn_b1"].reshape(16, 128).T
    o["L0_ffn_W2"] = down(i["L0_ffn_W2"])
    o["L0_ffn_b2"], o["L0_ffn_gW"] = i["L0_ffn_b2"], i["L0_ffn_gW"]
    o["L1_attn_w_in"] = i["L1_attn_w_in"].reshape(128, 4, 128)
    o["L1_attn_conv_w"] = i["L1_attn_conv_w"].reshape(2, 128, 4).transpose(1, 0, 2)
    o["L1_attn_conv_b"] = i["L1_attn_conv_b"].reshape(2, 128).T
    o["L1_attn_w_B"] = i["L1_attn_w_B"].reshape(2, 128, 16).transpose(1, 0, 2)
    o["L1_attn_w_C"] = i["L1_attn_w_C"].reshape(16, 2, 128)
    o["L1_attn_w_out"] = i["L1_attn_w_out"].reshape(2, 128, 128).transpose(1, 0, 2)
    o["L1_ffn_W1"] = units_t(i["L1_ffn_W1"])
    o["L1_ffn_W3"] = units_t(i["L1_ffn_W3"])
    o["L1_ffn_W2"] = down(i["L1_ffn_W2"].transpose(0, 2, 1))
    o["L1_ffn_Wg"] = i["L1_ffn_Wg"].T
    o["L2_attn_w1"] = i["L2_attn_w1"]
    o["L2_attn_w2"] = i["L2_attn_w2"]
    o["L2_attn_v"] = i["L2_attn_v"]
    o["L2_ffn_centroids"] = i["L2_ffn_centroids"].T
    o["L2_ffn_ln_g"] = rows(i["L2_ffn_ln_g"])
    o["L2_ffn_ln_b"] = rows(i["L2_ffn_ln_b"])
    o["L2_ffn_w1"] = units(i["L2_ffn_w1"])
    o["L2_ffn_b1"] = i["L2_ffn_b1"].reshape(32, 128).T
    o["L2_ffn_w2"] = down(i["L2_ffn_w2"])
    o["L2_ffn_b2"] = i["L2_ffn_b2"]
    return o


def kernel(**inputs):
    import concourse.bacc as _bacc
    from concourse.bass_utils import run_bass_kernel_spmd as _run

    nc = _bacc.Bacc("TRN2", target_bir_lowering=False, num_devices=1)
    arrays, aps = {}, {}
    for name, array in layout({k: np.asarray(v) for k, v in inputs.items()}).items():
        array = np.ascontiguousarray(array)
        arrays[f"in_{name}_dram"] = array
        aps[name] = nc.dram_tensor(f"in_{name}_dram", array.shape, mybir.dt.from_np(array.dtype), kind="ExternalInput").ap()
    out = nc.dram_tensor("out_0_dram", (BATCH, SEQ, D), F32, kind="ExternalOutput").ap()
    gated_stack(nc, aps, out)
    r = _run(nc, [arrays], core_ids=[0])
    return r.results[0]["out_0_dram"]
```

```python
from contextlib import ExitStack, contextmanager

import concourse.bass as bass
import numpy as np
from concourse import mybir

F32 = mybir.dt.float32
BF16 = mybir.dt.bfloat16
I32 = mybir.dt.int32
ALU = mybir.AluOpType
ACT = mybir.ActivationFunctionType
AX = mybir.AxisListType

P = 128
D = 128
BATCH = 16
SEQ = 256
TOK = BATCH * SEQ
BLK = TOK // P
GB = 4
GT = GB * P
GRP = TOK // GT
LN_EPS = 1e-5


@contextmanager
def phase(nc, names, steps=1):
    with ExitStack() as ctx:
        sems = [ctx.enter_context(nc.semaphore(n)) for n in names]
        step = ctx.enter_context(nc.Fori(0, steps)) if steps > 1 else 0
        with nc.Block() as block:
            yield block, step, sems
        numbers = sorted(s.num for s in sems)
        while numbers:
            run = 1
            while run < len(numbers) and numbers[run] == numbers[0] + run:
                run += 1
            nc.sync.sem_clear(range(numbers[0], numbers[0] + run))
            numbers = numbers[run:]
        nc.all_engine_barrier()


class Chain:

    def __init__(self, engine, sem):
        self.engine, self.sem, self.count = engine, sem, 0

    def __call__(self, instruction):
        self.count += 1
        instruction.then_inc(self.sem, 1)
        self.engine.wait_ge(self.sem, self.count)


class Memory:

    def __init__(self, nc, ctx):
        self.nc, self.ctx = nc, ctx

    def sb(self, name, shape, dt=F32):
        return self.ctx.enter_context(self.nc.sbuf_tensor(name, shape, dt))

    def psum(self, name, shape, dt=F32):
        return self.ctx.enter_context(self.nc.psum_tensor(name, shape, dt))


def load(nc, pairs):
    with phase(nc, ["loaded_sp", "loaded_act"]) as (block, _, (loaded_sp, loaded_act)):
        @block.sync
        def _(sp):
            mine = pairs[0::2]
            for dst, src in mine:
                sp.dma_start(dst, src).then_inc(loaded_sp, 16)
            sp.wait_ge(loaded_sp, 16 * len(mine))

        @block.scalar
        def _(act):
            mine = pairs[1::2]
            for dst, src in mine:
                act.dma_start(dst, src).then_inc(loaded_act, 16)
            if mine:
                act.wait_ge(loaded_act, 16 * len(mine))


def constants(nc, c):
    with phase(nc, ["filled", "cut"]) as (block, _, (filled, cut)):
        @block.gpsimd
        def _(pool):
            pool.memset(c.ident[:, :], 0.0).then_inc(filled, 1)
            pool.memset(c.ones[:, :], 1.0).then_inc(filled, 1)
            pool.memset(c.minus_half[:, :], -0.5).then_inc(filled, 1)
            pool.memset(c.triu[:, :], 1.0).then_inc(filled, 1)
            pool.memset(c.ident_bf[:, :], 0.0).then_inc(filled, 1)
            pool.memset(c.future[:, :], 0.0).then_inc(filled, 1)
            pool.wait_ge(filled, 6)
            pool.affine_select(out=c.ident[:, :], in_=c.ident[:, :], compare_op=ALU.not_equal, fill=1.0,
                               base=0, pattern=[[-1, P]], channel_multiplier=1).then_inc(cut, 1)
            pool.affine_select(out=c.ident_bf[:, :], in_=c.ident_bf[:, :], compare_op=ALU.not_equal, fill=1.0,
                               base=0, pattern=[[-1, P]], channel_multiplier=1).then_inc(cut, 1)
            pool.affine_select(out=c.triu[:, :], in_=c.triu[:, :], compare_op=ALU.is_gt, fill=0.0,
                               base=0, pattern=[[1, P]], channel_multiplier=-1).then_inc(cut, 1)
            pool.affine_select(out=c.future[:, :], in_=c.future[:, :], compare_op=ALU.is_ge, fill=-1e5,
                               base=0, pattern=[[-1, P]], channel_multiplier=1).then_inc(cut, 1)
            pool.wait_ge(cut, 4)


class Constants:
    def __init__(self, mem):
        self.ident = mem.sb("ident", [P, P])
        self.ones = mem.sb("ones", [P, P])
        self.triu = mem.sb("triu", [P, P])
        self.minus_half = mem.sb("minus_half", [P, GB])
        self.ident_bf = mem.sb("ident_bf", [P, P], BF16)
        self.future = mem.sb("future", [P, P], BF16)


class State:

    def __init__(self, mem):
        self.x = mem.sb("x_tok", [P, BLK, D])
        self.xn = mem.sb("xn_tok", [P, BLK, D])
        self.xnt = mem.sb("xn_ch", [P, TOK])
        self.s = mem.sb("mixer_out", [P, BLK, D])
        self.g = mem.sb("ffn_out", [P, BLK, D])


GROUPS = 4


def combine_group(dve, st, gate, rows, last):
    last(dve.tensor_tensor(gate, gate, st.s[:, rows, :], ALU.mult))
    return dve.tensor_tensor(st.x[:, rows, :], st.x[:, rows, :], gate, ALU.add)


def finish(nc, st, out):
    out = out.rearrange("s (t p) d -> p (s t) d", p=P)
    with nc.sbuf_tensor("fin_gate", [P, 2, GB, D], F32) as gate, \
            phase(nc, ["fin_gate_ready", "fin_dve_step", "fin_combined", "fin_stored"], GRP // GROUPS) as (block, i, sems):
        gate_ready, dve_step, combined, stored = sems

        @block.scalar
        def _(act):
            for g in range(GROUPS):
                if g >= 2:
                    act.wait_ge(combined, g - 1)
                act.activation(gate[:, g % 2, :, :], st.g[:, bass.ds((i * GROUPS + g) * GB, GB), :], ACT.Silu)\
                   .then_inc(gate_ready, 1)

        @block.vector
        def _(dve):
            link = Chain(dve, dve_step)
            for g in range(GROUPS):
                dve.wait_ge(gate_ready, g + 1)
                combine_group(dve, st, gate[:, g % 2, :, :], bass.ds((i * GROUPS + g) * GB, GB), link).then_inc(combined, 1)

        @block.sync
        def _(sp):
            for g in range(GROUPS):
                rows = bass.ds((i * GROUPS + g) * GB, GB)
                sp.wait_ge(combined, g + 1)
                sp.dma_start(out[:, rows, :], st.x[:, rows, :]).then_inc(stored, 16)
            sp.wait_ge(stored, 16 * GROUPS)


def layer_norm(nc, c, name, src, dst, dst_ch=None, gain=None, shift=None, combined=None):
    with ExitStack() as ctx:
        mem = Memory(nc, ctx)
        gate = mem.sb(name + "_gate", [P, 2, GB, D]) if combined else None
        stats = mem.sb(name + "_stats", [P, 2, GB, 6])
        mv = mem.sb(name + "_mv", [P, 2, GB, 2])
        rstd = mem.sb(name + "_rstd", [P, 2, GB])
        norm = mem.sb(name + "_norm", [P, 2, GB, D])
        pt = [mem.psum(f"{name}_pt{n}", [P, GB, P]) for n in range(2)]
        names = ["gate_ready", "dve_step", "stats_ready", "pool_step", "rstd_ready", "norm_ready", "turned", "ch_saved",
                 "tok_saved"]
        with phase(nc, [name + "_" + n for n in names], GRP // GROUPS) as (block, i, sems):
            gate_ready, dve_step, stats_ready, pool_step, rstd_ready, norm_ready, turned, ch_saved, tok_saved = sems

            def rows(g):
                return bass.ds((i * GROUPS + g) * GB, GB)

            @block.vector
            def _(dve):
                link = Chain(dve, dve_step)

                def measure(g):
                    if combined:
                        dve.wait_ge(gate_ready, g + 1)
                        link(combine_group(dve, combined, gate[:, g % 2, :, :], rows(g), link))
                    for j in range(GB):
                        ins = dve.bn_stats(stats[:, g % 2, j, :], src[:, (i * GROUPS + g) * GB + j, :])
                    link(ins)
                    for j in range(GB):
                        ins = dve.bn_aggr(mv[:, g % 2, j, :], stats[:, g % 2, j, :])
                    ins.then_inc(stats_ready, 1)

                def normalize(g):
                    dve.wait_ge(rstd_ready, g + 1)
                    if g >= 2:
                        if dst is not None:
                            dve.wait_ge(tok_saved, g - 1)
                        if dst_ch is not None:
                            dve.wait_ge(turned, g - 1)
                    for j in range(GB):
                        ins = dve.tensor_scalar(norm[:, g % 2, j, :], src[:, (i * GROUPS + g) * GB + j, :],
                                                mv[:, g % 2, j, 0:1], rstd[:, g % 2, j:j + 1], ALU.subtract, ALU.mult)
                    if gain is not None:
                        link(ins)
                        y, spread = norm[:, g % 2, :, :], [P, GB, D]
                        link(dve.tensor_tensor(y, y, gain.unsqueeze(1).to_broadcast(spread), ALU.mult))
                        ins = dve.tensor_tensor(y, y, shift.unsqueeze(1).to_broadcast(spread), ALU.add)
                    ins.then_inc(norm_ready, 1)

                for g in range(GROUPS + 1):
                    if g < GROUPS:
                        measure(g)
                    if g >= 1:
                        normalize(g - 1)

            @block.gpsimd
            def _(pool):
                link = Chain(pool, pool_step)
                for g in range(GROUPS):
                    pool.wait_ge(stats_ready, g + 1)
                    if g >= 2:
                        pool.wait_ge(norm_ready, g - 1)
                    r = rstd[:, g % 2, :]
                    link(pool.tensor_scalar(r, mv[:, g % 2, :, 1], LN_EPS, None, ALU.add))
                    pool.tensor_tensor(r, r, c.minus_half[:, :], ALU.pow).then_inc(rstd_ready, 1)

            if dst_ch is not None:
                @block.tensor
                def _(pe):
                    for g in range(GROUPS):
                        pe.wait_ge(norm_ready, g + 1)
                        if g >= 2:
                            pe.wait_ge(ch_saved, g - 1)
                        for j in range(GB):
                            ins = pe.transpose(pt[g % 2][:, j, :], norm[:, g % 2, j, :], c.ident[:, :])
                        ins.then_inc(turned, 1)

            @block.scalar
            def _(act):
                for g in range(GROUPS + 1):
                    if combined and g < GROUPS:
                        if g >= 2:
                            act.wait_ge(stats_ready, g - 1)
                        act.activation(gate[:, g % 2, :, :], combined.g[:, rows(g), :], ACT.Silu).then_inc(gate_ready, 1)
                    if g >= 1:
                        if dst is not None:
                            act.wait_ge(norm_ready, g)
                            act.activation(dst[:, rows(g - 1), :], norm[:, (g - 1) % 2, :, :], ACT.Copy).then_inc(tok_saved, 1)
                        if dst_ch is not None:
                            act.wait_ge(turned, g)
                            act.activation(dst_ch[:, bass.ds((i * GROUPS + g - 1) * GT, GT)],
                                           pt[(g - 1) % 2][:, :, :].rearrange("p a b -> p (a b)"), ACT.Copy).then_inc(ch_saved, 1)


WAYS = 16
ROUNDS = 6
EXPONENT = 0x7F800000
GONE = 1e30


def token_scores(nc, name, src_ch, w, n_exp, score):
    with nc.psum_tensor(name + "_ps", [P, BLK, n_exp], F32) as ps, \
            phase(nc, [name + "_scores_ready"]) as (block, _, (scores_ready,)):
        @block.tensor
        def _(pe):
            for b in range(BLK):
                ins = pe.matmul(ps[:, b, :], src_ch[:, b * P:(b + 1) * P], w[:, :], start=True, stop=True)
            ins.then_inc(scores_ready, 1)

        @block.vector
        def _(dve):
            dve.wait_ge(scores_ready, 1)
            dve.tensor_copy(score[:, :, :], ps[:, :, :].rearrange("p b e -> p e b"))


def choose(nc, c, name, score, chosen, n_exp, count, in_turn=False):
    with ExitStack() as ctx:
        mem = Memory(nc, ctx)
        E = 1 if in_turn else n_exp
        T = WAYS - 1
        biggest = mem.sb(name + "_biggest", [P, 1])
        bound = mem.sb(name + "_bound", [P, 1])
        index = mem.sb(name + "_index", [P, T])
        width = mem.sb(name + "_width", [P, ROUNDS])
        offsets = mem.sb(name + "_offsets", [P, ROUNDS, T])
        low = mem.sb(name + "_low", [P, E])
        thr = mem.sb(name + "_thr", [P, E, T])
        reached = mem.sb(name + "_reached", [P, E, T, BLK])
        part = mem.sb(name + "_part", [P, E, T])
        over = mem.sb(name + "_over", [P, E, T])
        kept = mem.sb(name + "_kept", [P, E])
        tie = mem.sb(name + "_tie", [P, E, BLK])
        before = mem.sb(name + "_before", [P, E, BLK + 1])
        one = mem.sb(name + "_one", [P, BLK])
        need = mem.sb(name + "_need", [P, E])
        p_count = mem.psum(name + "_count", [P, E, T])
        p_before = mem.psum(name + "_p_before", [P, E, BLK])

        names = [name + "_" + n for n in ("dve_step", "set", "biggest_ready", "bound_ready")]
        with phase(nc, names) as (block, _, (dve_step, set_, biggest_ready, bound_ready)):
            @block.gpsimd
            def _(pool):
                pool.iota(index[:, :], pattern=[[1, T]], base=1, channel_multiplier=0, allow_small_or_imprecise_dtypes=True)\
                    .then_inc(set_, 1)
                pool.memset(one[:, :], 1.0).then_inc(set_, 1)
                pool.memset(before[:, :, :], 0.0).then_inc(set_, 1)
                pool.wait_ge(biggest_ready, 1)
                pool.partition_all_reduce(bound[:, :], biggest[:, :], P, bass.bass_isa.ReduceOp.max).then_inc(bound_ready, 1)

            @block.vector
            def _(dve):
                link = Chain(dve, dve_step)
                link(dve.tensor_reduce(biggest[:, :], score[:, :, :], AX.XY, ALU.max, apply_absolute_value=True))
                dve.tensor_scalar(biggest[:, :], biggest[:, :], 1e-30, None, ALU.max).then_inc(biggest_ready, 1)
                dve.wait_ge(bound_ready, 1)
                link(dve.tensor_scalar(bound[:, :].bitcast(I32), bound[:, :].bitcast(I32), EXPONENT, None, ALU.bitwise_and))
                link(dve.tensor_scalar(bound[:, :], bound[:, :], 2.0, None, ALU.mult))
                dve.wait_ge(set_, 3)
                for r in range(ROUNDS):
                    link(dve.tensor_scalar(width[:, r:r + 1], bound[:, :], 2.0 / WAYS ** (r + 1), None, ALU.mult))
                    link(dve.tensor_scalar(offsets[:, r, :], index[:, :], width[:, r:r + 1], None, ALU.mult))

        for turn in range(n_exp if in_turn else 1):
            s = score[:, turn:turn + 1, :] if in_turn else score[:, :, :]
            got = chosen[:, turn:turn + 1, :] if in_turn else chosen[:, :, :]
            wide = [P, E, T, BLK]
            names = [name + "_" + n for n in ("dve_step", "part_ready", "count_ready", "tie_ready", "before_ready")]
            with phase(nc, names) as (block, _, (dve_step, part_ready, count_ready, tie_ready, before_ready)):
                @block.tensor
                def _(pe):
                    for r in range(ROUNDS):
                        pe.wait_ge(part_ready, r + 1)
                        pe.matmul(p_count[:, :, :], c.ones[:, :], part[:, :, :], start=True, stop=True).then_inc(count_ready, 1)
                    pe.wait_ge(part_ready, ROUNDS + 1)
                    pe.matmul(p_count[:, :, 0], c.ones[:, :], part[:, :, 0], start=True, stop=True).then_inc(count_ready, 1)
                    pe.wait_ge(tie_ready, 1)
                    pe.matmul(p_before[:, :, :], c.ones[:, :], before[:, :, 0:BLK], start=True, stop=False)
                    pe.matmul(p_before[:, :, :], c.triu[:, :], tie[:, :, :], start=False, stop=True).then_inc(before_ready, 1)

                @block.vector
                def _(dve):
                    link = Chain(dve, dve_step)
                    link(dve.tensor_scalar(low[:, :], bound[:, 0:1].to_broadcast([P, E]), -1.0, None, ALU.mult))
                    for r in range(ROUNDS):
                        link(dve.tensor_tensor(thr[:, :, :], low[:, :].unsqueeze(2).to_broadcast([P, E, T]),
                                               offsets[:, r, :].unsqueeze(1).to_broadcast([P, E, T]), ALU.add))
                        link(dve.tensor_tensor(reached[:, :, :, :], s.unsqueeze(2).to_broadcast(wide),
                                               thr[:, :, :].unsqueeze(3).to_broadcast(wide), ALU.is_ge))
                        dve.tensor_reduce(part[:, :, :], reached[:, :, :, :], AX.X, ALU.add).then_inc(part_ready, 1)
                        dve.wait_ge(count_ready, r + 1)
                        link(dve.tensor_scalar(over[:, :, :], p_count[:, :, :], count - 0.5, None, ALU.is_ge))
                        link(dve.tensor_reduce(kept[:, :], over[:, :, :], AX.X, ALU.add))
                        link(dve.scalar_tensor_tensor(low[:, :], kept[:, :], width[:, r:r + 1], low[:, :], ALU.mult, ALU.add))
                    spread = [P, E, BLK]
                    link(dve.tensor_tensor(tie[:, :, :], s, low[:, :].unsqueeze(2).to_broadcast(spread), ALU.is_ge))
                    link(dve.tensor_scalar(low[:, :], low[:, :], width[:, ROUNDS - 1:ROUNDS], None, ALU.add))
                    link(dve.tensor_tensor(got, s, low[:, :].unsqueeze(2).to_broadcast(spread), ALU.is_ge))
                    dve.tensor_reduce(part[:, :, 0], got, AX.X, ALU.add).then_inc(part_ready, 1)
                    link(dve.tensor_tensor(tie[:, :, :], tie[:, :, :], got, ALU.subtract))
                    for e in range(E):
                        ins = dve.tensor_tensor_scan(before[:, e, 1:], one[:, :], tie[:, e, :], 0.0, ALU.mult, ALU.add)
                        if e < E - 1:
                            link(ins)
                    ins.then_inc(tie_ready, 1)
                    dve.wait_ge(count_ready, ROUNDS + 1)
                    link(dve.tensor_scalar(need[:, :], p_count[:, :, 0], -1.0, float(count), ALU.mult, ALU.add))
                    dve.wait_ge(before_ready, 1)
                    room = reached[:, :, 0, :]
                    link(dve.tensor_tensor(room, p_before[:, :, :], need[:, :].unsqueeze(2).to_broadcast(spread), ALU.is_lt))
                    link(dve.tensor_tensor(room, room, tie[:, :, :], ALU.mult))
                    link(dve.tensor_tensor(got, got, room, ALU.add))
                    if in_turn and turn < n_exp - 1:
                        later = [P, n_exp - turn - 1, BLK]
                        link(dve.tensor_scalar(room, got, -GONE, None, ALU.mult))
                        link(dve.tensor_tensor(score[:, turn + 1:, :], score[:, turn + 1:, :], room.to_broadcast(later), ALU.add))


def experts(nc, c, st, name, src_ch, w_tok, n_exp, chunks, func, w1, w2, b1=None, w3=None, b2=None, residual=None):
    units = n_exp * chunks
    gated = w3 is not None
    with ExitStack() as ctx:
        mem = Memory(nc, ctx)
        act_out = mem.sb(name + "_act", [P, 2, GT]) if gated else None
        hidden = mem.sb(name + "_hidden", [P, 2, chunks, GT])
        acc = mem.sb(name + "_acc", [P, GB, D])
        w_now = mem.sb(name + "_w", [P, GB, n_exp])
        wt = mem.sb(name + "_wt", [n_exp, GB, P]) if b2 is not None else None
        ph1 = [mem.psum(f"{name}_ph1{k}", [P, GT]) for k in range(2)]
        ph3 = [mem.psum(f"{name}_ph3{k}", [P, GT]) for k in range(2)] if gated else None
        py = [mem.psum(f"{name}_py{k}", [P, GB, D]) for k in range(2)]
        names = ["h1_ready", "h3_ready", "act_ready", "hidden_ready", "y_ready", "added", "w_ready", "wt_ready", "wt_saved"]
        with phase(nc, [name + "_" + n for n in names], GRP) as (block, i, sems):
            h1_ready, h3_ready, act_ready, hidden_ready, y_ready, added, w_ready, wt_ready, wt_saved = sems
            tokens = bass.ds(i * GT, GT)

            @block.tensor
            def _(pe):
                def up(u):
                    if u >= 2:
                        pe.wait_ge(hidden_ready, u - 1)
                    pe.matmul(ph1[u % 2][:, :], w1[:, u, :], src_ch[:, tokens], start=True, stop=True).then_inc(h1_ready, 1)
                    if gated:
                        pe.matmul(ph3[u % 2][:, :], w3[:, u, :], src_ch[:, tokens], start=True, stop=True).then_inc(h3_ready, 1)

                def down(e):
                    pe.wait_ge(hidden_ready, chunks * (e + 1))
                    if e >= 2:
                        pe.wait_ge(added, GB * (e - 1))
                    for j in range(GB):
                        for f in range(chunks):
                            ins = pe.matmul(py[e % 2][:, j, :], hidden[:, e % 2, f, j * P:(j + 1) * P],
                                            w2[:, e * chunks + f, :], start=(f == 0), stop=(f == chunks - 1))
                    ins.then_inc(y_ready, 1)

                for e in range(n_exp + 1):
                    if e < n_exp:
                        for f in range(chunks):
                            up(e * chunks + f)
                            if f == 0 and e >= 1:
                                down(e - 1)
                    else:
                        down(e - 1)
                if b2 is not None:
                    e = n_exp
                    pe.wait_ge(w_ready, 1)
                    pe.wait_ge(added, GB * (e - 1))
                    for j in range(GB):
                        pe.transpose(py[e % 2][0:n_exp, j, :], w_now[:, j, :], c.ident[:, :]).then_inc(wt_ready, 1)
                    pe.wait_ge(wt_saved, 1)
                    pe.wait_ge(added, GB * e)
                    for j in range(GB):
                        ins = pe.matmul(py[1 - e % 2][:, j, :], wt[:, j, :], b2[:, :], start=True, stop=True)
                    ins.then_inc(y_ready, 1)

            @block.scalar
            def _(act):
                for u in range(units):
                    act.wait_ge(h1_ready, u + 1)
                    e, f = u // chunks, u % chunks
                    if gated:
                        if u >= 2:
                            act.wait_ge(hidden_ready, u - 1)
                        act.activation(act_out[:, u % 2, :], ph1[u % 2][:, :], func).then_inc(act_ready, 1)
                    else:
                        if f == 0 and e >= 2:
                            act.wait_ge(y_ready, e - 1)
                        act.activation(hidden[:, e % 2, f, :], ph1[u % 2][:, :], func, bias=b1[:, u:u + 1])\
                           .then_inc(hidden_ready, 1)
                if b2 is not None:
                    act.wait_ge(wt_ready, GB)
                    act.activation(wt[:, :, :], py[n_exp % 2][0:n_exp, :, :], ACT.Copy).then_inc(wt_saved, 1)

            @block.vector
            def _(dve):
                def add(e):
                    dve.wait_ge(y_ready, e + 1)
                    for j in range(GB):
                        y = py[e % 2][:, j, :] if e < n_exp else py[1 - e % 2][:, j, :]
                        out = acc[:, j, :] if e < last else st.g[:, i * GB + j, :]
                        if e > 0:
                            dve.wait_ge(added, GB * (e - 1) + j + 1)
                        if e == n_exp:
                            ins = dve.tensor_tensor(out, y, acc[:, j, :], ALU.add)
                        elif e == 0 and residual is None:
                            ins = dve.tensor_scalar(out, y, w_now[:, j, e:e + 1], None, ALU.mult)
                        else:
                            more = acc[:, j, :] if e else residual[:, i * GB + j, :]
                            ins = dve.scalar_tensor_tensor(out, y, w_now[:, j, e:e + 1], more, ALU.mult, ALU.add)
                        ins.then_inc(added, 1)

                last = n_exp if b2 is not None else n_exp - 1
                dve.tensor_copy(w_now[:, :, :], w_tok[:, bass.ds(i * GB, GB), :]).then_inc(w_ready, 1)
                dve.wait_ge(w_ready, 1)
                for e in range(n_exp + 1):
                    if gated and e < n_exp:
                        for f in range(chunks):
                            u = e * chunks + f
                            dve.wait_ge(act_ready, u + 1)
                            dve.wait_ge(h3_ready, u + 1)
                            if f == 0 and e >= 2:
                                dve.wait_ge(y_ready, e - 1)
                            dve.tensor_tensor(hidden[:, e % 2, f, :], ph3[u % 2][:, :], act_out[:, u % 2, :], ALU.mult)\
                               .then_inc(hidden_ready, 1)
                    if e >= 1:
                        add(e - 1)
                if b2 is not None:
                    add(n_exp)


def top_two(nc, c, st, name, src_ch, gate_w, gate_b, n_exp, w_tok, softmax):
    with ExitStack() as ctx:
        mem = Memory(nc, ctx)
        prob = mem.sb(name + "_prob", [P, BLK, n_exp])
        rank = mem.sb(name + "_rank", [P, BLK, n_exp])
        beats = mem.sb(name + "_beats", [P, BLK, n_exp])
        small = mem.sb(name + "_small", [P, BLK])
        pl = mem.psum(name + "_pl", [P, BLK, n_exp])
        wide = [P, BLK, n_exp]
        with phase(nc, [name + "_" + n for n in ("logits_ready", "dve_step", "shifted", "prob_ready")]) as (block, _, sems):
            logits_ready, dve_step, shifted, prob_ready = sems

            @block.tensor
            def _(pe):
                for b in range(BLK):
                    pe.matmul(pl[:, b, :], src_ch[:, b * P:(b + 1) * P], gate_w[:, :], start=True, stop=True)\
                      .then_inc(logits_ready, 1)

            @block.scalar
            def _(act):
                act.wait_ge(shifted, 1)
                act.activation(prob[:, :, :], prob[:, :, :], ACT.Exp if softmax else ACT.Sigmoid).then_inc(prob_ready, 1)

            @block.vector
            def _(dve):
                link = Chain(dve, dve_step)
                spread = small[:, :].unsqueeze(2).to_broadcast(wide)
                dve.wait_ge(logits_ready, BLK)
                ins = dve.tensor_tensor(prob[:, :, :], pl[:, :, :], gate_b[:, :].unsqueeze(1).to_broadcast(wide), ALU.add)
                if softmax:
                    link(ins)
                    link(dve.tensor_reduce(small[:, :], prob[:, :, :], AX.X, ALU.max))
                    ins = dve.tensor_tensor(prob[:, :, :], prob[:, :, :], spread, ALU.subtract)
                ins.then_inc(shifted, 1)
                dve.wait_ge(prob_ready, 1)
                if softmax:
                    link(dve.tensor_reduce(small[:, :], prob[:, :, :], AX.X, ALU.add))
                    link(dve.reciprocal(small[:, :], small[:, :]))
                    link(dve.tensor_tensor(prob[:, :, :], prob[:, :, :], spread, ALU.mult))
                link(dve.memset(rank[:, :, :], 0.0))
                for e in range(n_exp):
                    one = prob[:, :, e:e + 1]
                    if e + 1 < n_exp:
                        rest = [P, BLK, n_exp - e - 1]
                        link(dve.tensor_tensor(beats[:, :, e + 1:], one.to_broadcast(rest), prob[:, :, e + 1:], ALU.is_ge))
                        link(dve.tensor_tensor(rank[:, :, e + 1:], rank[:, :, e + 1:], beats[:, :, e + 1:], ALU.add))
                    if e:
                        rest = [P, BLK, e]
                        link(dve.tensor_tensor(beats[:, :, :e], one.to_broadcast(rest), prob[:, :, :e], ALU.is_gt))
                        link(dve.tensor_tensor(rank[:, :, :e], rank[:, :, :e], beats[:, :, :e], ALU.add))
                link(dve.tensor_scalar(rank[:, :, :], rank[:, :, :], 1.5, None, ALU.is_lt))
                out = w_tok[:, :, 0:n_exp]
                link(dve.tensor_tensor(out, prob[:, :, :], rank[:, :, :], ALU.mult))
                if not softmax:
                    link(dve.tensor_reduce(small[:, :], out, AX.X, ALU.add))
                    link(dve.tensor_scalar(small[:, :], small[:, :], 1e-8, None, ALU.add))
                    link(dve.reciprocal(small[:, :], small[:, :]))
                    link(dve.tensor_tensor(out, out, spread, ALU.mult))


CHUNK = 32
HEADS = 4
HD = 32
CPB = P // CHUNK
MATS = BLK * HEADS * CPB
NSEQ = GT // SEQ


def delta_masks(nc, m):
    with phase(nc, ["gd_zero", "gd_same", "gd_cut"]) as (block, _, (zero, same, cut)):
        @block.gpsimd
        def _(pool):
            for t in (m.same, m.minus_same, m.minus_strict, m.causal):
                pool.memset(t[:, :], 0.0).then_inc(zero, 1)
            pool.wait_ge(zero, 4)
            for t, value in ((m.same, 1.0), (m.minus_same, -1.0), (m.minus_strict, -1.0), (m.causal, 1.0)):
                for n in range(CPB):
                    part = slice(n * CHUNK, (n + 1) * CHUNK)
                    pool.memset(t[part, part], value).then_inc(same, 1)
            pool.wait_ge(same, 4 * CPB)
            pool.affine_select(out=m.minus_strict[:, :], in_=m.minus_strict[:, :], compare_op=ALU.is_gt, fill=0.0,
                               base=0, pattern=[[1, P]], channel_multiplier=-1).then_inc(cut, 1)
            pool.affine_select(out=m.causal[:, :], in_=m.causal[:, :], compare_op=ALU.is_ge, fill=0.0,
                               base=0, pattern=[[1, P]], channel_multiplier=-1).then_inc(cut, 1)
            pool.wait_ge(cut, 2)


class DeltaState:
    def __init__(self, nc, mem):
        self.same = mem.sb("gd_m_same", [P, P])
        self.minus_same = mem.sb("gd_m_minus_same", [P, P])
        self.minus_strict = mem.sb("gd_m_strict", [P, P])
        self.causal = mem.sb("gd_m_causal", [P, P])
        self.beta = mem.sb("gd_beta", [P, BLK, 2 * HEADS])
        self.q_ch = mem.sb("gd_q_ch", [P, TOK])
        self.k_ch = mem.sb("gd_k_ch", [P, TOK])
        self.k_tok = mem.sb("gd_k_tok", [P, BLK, D])
        self.v_tok = mem.sb("gd_v_tok", [P, BLK, D])
        self.tri = nc.dram_tensor("gd_tri", (MATS * CHUNK * CHUNK,), F32, kind="Internal").ap()


def gates(nc, st, m, w_b, w_gates):
    beta_ch = st.g[:, :, :].rearrange("p b d -> p (b d)")
    with ExitStack() as ctx:
        mem = Memory(nc, ctx)
        p_tok = mem.psum("gd_p_tok", [P, BLK, 2 * HEADS])
        p_ch = [mem.psum(f"gd_p_ch{n}", [P, GT]) for n in range(2)]
        with phase(nc, ["gd_tok_ready", "gd_ch_ready", "gd_ch_saved"]) as (block, _, (tok_ready, ch_ready, ch_saved)):
            @block.tensor
            def _(pe):
                for b in range(BLK):
                    ins = pe.matmul(p_tok[:, b, :], st.xnt[:, b * P:(b + 1) * P], w_gates[:, :], start=True, stop=True)
                ins.then_inc(tok_ready, 1)
                for g in range(GRP):
                    if g >= 2:
                        pe.wait_ge(ch_saved, g - 1)
                    pe.matmul(p_ch[g % 2][:, :], w_b[:, :], st.xnt[:, g * GT:(g + 1) * GT], start=True, stop=True)\
                      .then_inc(ch_ready, 1)

            @block.scalar
            def _(act):
                act.wait_ge(tok_ready, 1)
                act.activation(m.beta[:, :, :], p_tok[:, :, :], ACT.Sigmoid)
                for g in range(GRP):
                    act.wait_ge(ch_ready, g + 1)
                    act.activation(beta_ch[:, g * GT:(g + 1) * GT], p_ch[g % 2][:, :], ACT.Sigmoid).then_inc(ch_saved, 1)


def project(nc, c, st, m, w3, taps):
    TAPS = 4
    PAD = TAPS - 1
    beta_ch = st.g[:, :, :].rearrange("p b d -> p (b d)")
    with ExitStack() as ctx:
        mem = Memory(nc, ctx)
        padded = mem.sb("gp_padded", [P, 3, NSEQ, PAD + SEQ])
        y = mem.sb("gp_y", [P, 3, NSEQ, SEQ])
        square = mem.sb("gp_square", [P, 2, GT])
        kb = mem.sb("gp_kb", [P, GT])
        tri = mem.sb("gp_tri", [P, HEADS, GB, P])
        eps = mem.sb("gp_eps", [P, 1])
        bank = [mem.psum(f"gp_bank{n}", [P, 512]) for n in range(8)]
        flat = y[:, :, :, :].rearrange("p a b c -> p a (b c)")
        with phase(nc, ["gp_set"]) as (block, _, (set_,)):
            @block.gpsimd
            def _(pool):
                pool.memset(padded[:, :, :, :], 0.0).then_inc(set_, 1)
                pool.memset(eps[:, :], 1e-6).then_inc(set_, 1)
                pool.wait_ge(set_, 2)
        names = ["gp_" + n for n in ("in_ready", "x_saved", "dve_step", "conv_ready", "silu_ready", "square_ready", "sum_ready",
                                     "root_ready", "unit_ready", "kb_ready", "turn_ready", "v_saved", "tri_ready", "tri_masked",
                                     "tri_stored", "k_saved")]
        with phase(nc, names, GRP) as (block, i, sems):
            (in_ready, x_saved, dve_step, conv_ready, silu_ready, square_ready, sum_ready, root_ready, unit_ready, kb_ready,
             turn_ready, v_saved, tri_ready, tri_masked, tri_stored, k_saved) = sems
            tokens = bass.ds(i * GT, GT)

            @block.tensor
            def _(pe):
                for n in range(3):
                    pe.matmul(bank[n][:, :], w3[:, n, :], st.xnt[:, tokens], start=True, stop=True).then_inc(in_ready, 1)
                for n in range(2):
                    pe.wait_ge(square_ready, n + 1)
                    pe.matmul(bank[3 + n][:, :], m.same[:, :], square[:, n, :], start=True, stop=True).then_inc(sum_ready, 1)
                pe.wait_ge(silu_ready, 3)
                for j in range(GB):
                    ins = pe.transpose(bank[5][:, j * P:(j + 1) * P], flat[:, 2, j * P:(j + 1) * P], c.ident[:, :])
                ins.then_inc(turn_ready, 1)
                pe.wait_ge(unit_ready, 2)
                for j in range(GB):
                    ins = pe.transpose(bank[6][:, j * P:(j + 1) * P], flat[:, 1, j * P:(j + 1) * P], c.ident[:, :])
                ins.then_inc(turn_ready, 1)
                pe.wait_ge(kb_ready, 1)
                for h in range(HEADS):
                    rows = slice(h * HD, (h + 1) * HD)
                    for j in range(GB):
                        cols = slice(j * P, (j + 1) * P)
                        ins = pe.matmul(bank[h][:, cols], flat[rows, 1, cols], kb[rows, cols], start=True, stop=True)
                    ins.then_inc(tri_ready, 1)

            @block.scalar
            def _(act):
                for n in range(3):
                    act.wait_ge(in_ready, n + 1)
                    act.activation(padded[:, n, :, PAD:], bank[n][:, :].rearrange("p (a b) -> p a b", a=NSEQ), ACT.Copy)\
                       .then_inc(x_saved, 1)
                for n in range(3):
                    act.wait_ge(conv_ready, n + 1)
                    act.activation(y[:, n, :, :], y[:, n, :, :], ACT.Silu).then_inc(silu_ready, 1)
                for n in range(2):
                    act.wait_ge(silu_ready, n + 1)
                    act.activation(square[:, n, :], flat[:, n, :], ACT.Square).then_inc(square_ready, 1)
                act.wait_ge(turn_ready, 1)
                act.activation(m.v_tok[:, bass.ds(i * GB, GB), :], bank[5][:, :].rearrange("p (a b) -> p a b", a=GB), ACT.Copy)\
                   .then_inc(v_saved, 1)
                for n in range(2):
                    act.wait_ge(sum_ready, n + 1)
                    act.activation(square[:, n, :], bank[3 + n][:, :], ACT.Sqrt, bias=eps[:, 0:1]).then_inc(root_ready, 1)
                act.wait_ge(turn_ready, 2)
                act.activation(m.k_tok[:, bass.ds(i * GB, GB), :], bank[6][:, :].rearrange("p (a b) -> p a b", a=GB), ACT.Copy)\
                   .then_inc(k_saved, 1)

            @block.vector
            def _(dve):
                link = Chain(dve, dve_step)
                for n in range(3):
                    dve.wait_ge(x_saved, n + 1)
                    out = y[:, n, :, :]
                    for k in range(TAPS):
                        x = padded[:, n, :, k:k + SEQ]
                        if k == 0:
                            link(dve.tensor_scalar(out, x, taps[:, n, k:k + 1], None, ALU.mult))
                        else:
                            ins = dve.scalar_tensor_tensor(out, x, taps[:, n, k:k + 1], out, ALU.mult, ALU.add)
                            if k < TAPS - 1:
                                link(ins)
                    ins.then_inc(conv_ready, 1)
                for n in range(2):
                    dve.wait_ge(root_ready, n + 1)
                    link(dve.reciprocal(square[:, n, :], square[:, n, :]))
                    dve.tensor_tensor(flat[:, n, :], flat[:, n, :], square[:, n, :], ALU.mult).then_inc(unit_ready, 1)
                dve.wait_ge(unit_ready, 2)
                dve.tensor_tensor(kb[:, :], flat[:, 1, :], beta_ch[:, tokens], ALU.mult).then_inc(kb_ready, 1)
                for h in range(HEADS):
                    dve.wait_ge(tri_ready, h + 1)
                    dve.tensor_tensor(tri[:, h, :, :], bank[h][:, :].rearrange("p (a b) -> p a b", a=GB),
                                      m.minus_strict[:, :].unsqueeze(1).to_broadcast([P, GB, P]), ALU.mult).then_inc(tri_masked, 1)

            @block.gpsimd
            def _(pool):
                pool.wait_ge(unit_ready, 2)
                pool.tensor_copy(m.q_ch[:, tokens], flat[:, 0, :])
                pool.tensor_copy(m.k_ch[:, tokens], flat[:, 1, :])

            @block.sync
            def _(sp):
                sp.wait_ge(tri_masked, HEADS)
                size = GB * HEADS * CPB * CHUNK * CHUNK
                mats = m.tri[bass.ds(i * size, size)].rearrange("(b h n j i) -> n j h b i", h=HEADS, n=CPB, j=CHUNK, i=CHUNK)
                for n in range(CPB):
                    part = slice(n * CHUNK, (n + 1) * CHUNK)
                    for h in range(HEADS):
                        sp.dma_start(mats[n, :, h, :, :], tri[part, h, :, part]).then_inc(tri_stored, 16)
                sp.wait_ge(tri_stored, 16 * CPB * HEADS)


def invert(nc, m):
    LM = MATS // P
    with ExitStack() as ctx:
        mem = Memory(nc, ctx)
        at = mem.sb("gi_at", [P, LM, CHUNK, CHUNK])
        prod = mem.sb("gi_prod", [P, LM, CHUNK * CHUNK])
        upd = mem.sb("gi_upd", [P, LM, CHUNK])
        lanes = m.tri.rearrange("(p n) -> p n", p=P)
        flat = at[:, :, :, :].rearrange("p a b c -> p (a b c)")
        with phase(nc, ["gi_loaded", "gi_dve_step", "gi_inverted", "gi_stored"]) as (block, _, sems):
            loaded, dve_step, inverted, stored = sems

            @block.sync
            def _(sp):
                sp.dma_start(flat, lanes).then_inc(loaded, 16)
                sp.wait_ge(inverted, 1)
                sp.dma_start(lanes, flat).then_inc(stored, 16)
                sp.wait_ge(stored, 16)

            @block.vector
            def _(dve):
                link = Chain(dve, dve_step)
                dve.wait_ge(loaded, 16)
                for i in range(2, CHUNK):
                    full = [P, LM, i, i]
                    terms = prod[:, :, 0:i * i].rearrange("p a (k j) -> p a k j", k=i)
                    link(dve.tensor_tensor(terms, at[:, :, 0:i, 0:i], at[:, :, 0:i, i].unsqueeze(2).to_broadcast(full), ALU.mult))
                    link(dve.tensor_reduce(upd[:, :, 0:i], terms, AX.X, ALU.add))
                    link(dve.tensor_tensor(at[:, :, 0:i, i], at[:, :, 0:i, i], upd[:, :, 0:i], ALU.add))
                diag = at[:, :, :, :].rearrange("p a b c -> p a (b c)")[:, :, 0:CHUNK * CHUNK:CHUNK + 1]
                dve.tensor_scalar(diag, diag, 1.0, None, ALU.add).then_inc(inverted, 1)


def recur(nc, c, st, m, w_o, norm_w):
    with ExitStack() as ctx:
        mem = Memory(nc, ctx)
        inv = mem.sb("gr_inv", [P, GB, HEADS, P])
        q = mem.sb("gr_q", [P, GT])
        k = mem.sb("gr_k", [P, GT])
        k_tok = mem.sb("gr_k_tok", [P, GB, D])
        v_tok = mem.sb("gr_v_tok", [P, GB, D])
        beta = mem.sb("gr_beta", [P, GB, 2 * HEADS])
        vk = mem.sb("gr_vk", [P, GB, HEADS, 2 * HD])
        u = mem.sb("gr_u", [P, GB, D])
        w = mem.sb("gr_w", [P, GB, D])
        attn = mem.sb("gr_attn", [P, HEADS, GB, P])
        kv = mem.sb("gr_kv", [P, CPB, GB, P])
        trans = mem.sb("gr_trans", [P, CPB, GB, P])
        q_eff = mem.sb("gr_q_eff", [P, GB, P])
        state = mem.sb("gr_state", [P, 2, NSEQ, P])
        o_ch = mem.sb("gr_o_ch", [P, GB, P])
        o = u
        square = vk[:, 0:2, :, :].rearrange("p b h x -> p (b h x)").rearrange("p (a x) -> p a x", x=HD)
        power = mem.sb("gr_power", [P, GB * HEADS])
        half = mem.sb("gr_half", [P, GB * HEADS])
        bank = [mem.psum(f"gr_bank{n}", [P, 4, P]) for n in range(8)]
        with phase(nc, ["gr_set"]) as (block, _, (set_,)):
            @block.gpsimd
            def _(pool):
                pool.memset(inv[:, :, :, :], 0.0).then_inc(set_, 1)
                pool.memset(half[:, :], -0.5).then_inc(set_, 1)
                pool.wait_ge(set_, 2)
        names = ["gr_" + n for n in ("inv_loaded", "qk_loaded", "tok_loaded", "vk_ready", "uw_ready", "u_saved", "w_saved",
                                     "attn_ready", "attn_masked", "kv_ready", "kv_masked", "wk_ready", "wk_masked", "trans_ready",
                                     "qw_ready", "intra_ready", "q_eff_ready", "s_ready", "s_saved", "o_ready", "o_saved",
                                     "o_turned", "dve_step", "mixed", "squared", "power_sum", "pool_step", "power_ready",
                                     "normed", "n_turned", "n_saved", "out_ready")]
        with phase(nc, names, GRP) as (block, i, sems):
            (inv_loaded, qk_loaded, tok_loaded, vk_ready, uw_ready, u_saved, w_saved, attn_ready, attn_masked, kv_ready,
             kv_masked, wk_ready, wk_masked, trans_ready, qw_ready, intra_ready, q_eff_ready, s_ready, s_saved, o_ready,
             o_saved, o_turned, dve_step, mixed, squared, power_sum, pool_step, power_ready, normed, n_turned, n_saved,
             out_ready) = sems
            tokens, rows = bass.ds(i * GT, GT), bass.ds(i * GB, GB)
            CH = SEQ // CHUNK

            @block.sync
            def _(sp):
                sp.dma_start(k_tok[:, :, :], m.k_tok[:, rows, :]).then_inc(tok_loaded, 16)
                sp.dma_start(v_tok[:, :, :], m.v_tok[:, rows, :]).then_inc(tok_loaded, 16)
                sp.dma_start(beta[:, :, :], m.beta[:, rows, :]).then_inc(tok_loaded, 16)
                sp.dma_start(q[:, :], m.q_ch[:, tokens]).then_inc(qk_loaded, 16)
                sp.dma_start(k[:, :], m.k_ch[:, tokens]).then_inc(qk_loaded, 16)

            @block.scalar
            def _(act):
                size = GB * HEADS * CPB * CHUNK * CHUNK
                mats = m.tri[bass.ds(i * size, size)].rearrange("(b h n j i) -> n j b h i", h=HEADS, n=CPB, j=CHUNK, i=CHUNK)
                for n in range(CPB):
                    part = slice(n * CHUNK, (n + 1) * CHUNK)
                    for b in range(GB):
                        act.dma_start(inv[part, b, :, part], mats[n, :, b, :, :]).then_inc(inv_loaded, 16)
                for t in range(2):
                    act.wait_ge(uw_ready, t + 1)
                    src = bank[4 + t][:, :, :].rearrange("p a b -> p (a b)").rearrange("p (b h x) -> p b h x", b=2, h=HEADS)
                    for dst, part, sem in ((u, slice(0, HD), u_saved), (w, slice(HD, 2 * HD), w_saved)):
                        act.activation(dst[:, 2 * t:2 * t + 2, :].rearrange("p b (h x) -> p b h x", h=HEADS),
                                       src[:, :, :, part], ACT.Copy).then_inc(sem, 1)
                act.wait_ge(o_ready, 1)
                act.activation(o_ch[:, :, :], bank[1][:, :, :], ACT.Copy).then_inc(o_saved, 1)
                act.wait_ge(mixed, 1)
                act.activation(square, o[:, :, :].rearrange("p b (h x) -> p (b h) x", h=HEADS), ACT.Square)\
                   .then_inc(squared, 1)
                act.wait_ge(n_turned, 1)
                act.activation(o_ch[:, :, :], bank[5][:, :, :], ACT.Copy, scale=norm_w[:, 0:1]).then_inc(n_saved, 1)
                act.wait_ge(out_ready, 1)
                act.activation(st.s[:, rows, :], bank[6][:, :, :], ACT.Copy)

            @block.tensor
            def _(pe):
                pe.wait_ge(qk_loaded, 32)
                for h in range(HEADS):
                    part = slice(h * HD, (h + 1) * HD)
                    for b in range(GB):
                        cols = slice(b * P, (b + 1) * P)
                        ins = pe.matmul(bank[h][:, b, :], k[part, cols], q[part, cols], start=True, stop=True)
                    ins.then_inc(attn_ready, 1)
                pe.wait_ge(vk_ready, 2)
                pe.wait_ge(inv_loaded, 16 * CPB * GB)
                for b in range(GB):
                    out = bank[4 + b // 2][:, :, :].rearrange("p a b -> p (a b)").rearrange("p (b h x) -> p b h x", b=2, h=HEADS)
                    for h in range(HEADS):
                        ins = pe.matmul(out[:, b % 2, h, :], inv[:, b, h, :], vk[:, b, h, :], start=True, stop=True)
                    if b % 2:
                        ins.then_inc(uw_ready, 1)
                pe.wait_ge(tok_loaded, 48)
                pe.wait_ge(u_saved, 2)
                for n in range(CPB):
                    part = slice(n * CHUNK, (n + 1) * CHUNK)
                    pe.wait_ge(attn_masked, n + 1)
                    for b in range(GB):
                        ins = pe.matmul(bank[n][:, b, :], k_tok[part, b, :], u[part, b, :], start=True, stop=True)
                    ins.then_inc(kv_ready, 1)
                pe.wait_ge(w_saved, 2)
                for n in range(CPB):
                    part = slice(n * CHUNK, (n + 1) * CHUNK)
                    for b in range(GB):
                        ins = pe.matmul(bank[4 + n][:, b, :], w[part, b, :], k_tok[part, b, :], start=True, stop=True)
                    ins.then_inc(wk_ready, 1)
                for src, n, sem in ((w, 0, qw_ready), (u, 1, intra_ready)):
                    pe.wait_ge(kv_masked, n + 1)
                    for b in range(GB):
                        for h in range(HEADS):
                            part = slice(h * HD, (h + 1) * HD)
                            ins = pe.matmul(bank[n][part, b, :], src[:, b, part], attn[:, h, b, :], start=(b == 0),
                                            stop=(n == 0), skip_group_check=True)
                    ins.then_inc(sem, 1)
                pe.wait_ge(q_eff_ready, 1)
                pe.wait_ge(trans_ready, CPB)
                pe.wait_ge(kv_masked, CPB)
                for t in range(1, CH):
                    for s in range(NSEQ):
                        if t > 1:
                            pe.wait_ge(s_saved, NSEQ * (t - 2) + s + 1)
                        b, n = 2 * s + t // CPB, t % CPB
                        now = kv[:, 0, 2 * s, :] if t == 1 else state[:, t % 2, s, :]
                        if t < CH - 1:
                            pe.matmul(bank[2 + s][:, 0, :], trans[:, n, b, :], now, start=True, stop=True).then_inc(s_ready, 1)
                        cols = slice(n * CHUNK, (n + 1) * CHUNK)
                        ins = pe.matmul(bank[1][:, b, cols], now, q_eff[:, b, cols], start=False, stop=True,
                                        skip_group_check=True)
                ins.then_inc(o_ready, 1)
                pe.wait_ge(o_saved, 1)
                pe.wait_ge(wk_masked, CPB)
                for b in range(GB):
                    ins = pe.transpose(bank[4][:, b, :], o_ch[:, b, :], c.ident[:, :])
                ins.then_inc(o_turned, 1)
                pe.wait_ge(normed, 1)
                for b in range(GB):
                    ins = pe.transpose(bank[5][:, b, :], o[:, b, :], c.ident[:, :])
                ins.then_inc(n_turned, 1)
                pe.wait_ge(n_saved, 1)
                for b in range(GB):
                    ins = pe.matmul(bank[6][:, b, :], o_ch[:, b, :], w_o[:, :], start=True, stop=True)
                ins.then_inc(out_ready, 1)

            @block.vector
            def _(dve):
                link = Chain(dve, dve_step)
                wide = [P, GB, HEADS, HD]
                dve.wait_ge(tok_loaded, 48)
                by_head = lambda t: t[:, :, :].rearrange("p b (h x) -> p b h x", h=HEADS)
                for n, src in enumerate((v_tok, k_tok)):
                    dve.tensor_tensor(vk[:, :, :, n * HD:(n + 1) * HD], by_head(src),
                                      beta[:, :, 0:HEADS].unsqueeze(3).to_broadcast(wide), ALU.mult).then_inc(vk_ready, 1)
                spread = [P, GB, P]
                for h in range(HEADS):
                    dve.wait_ge(attn_ready, h + 1)
                    dve.tensor_tensor(attn[:, h, :, :], bank[h][:, :, :], m.causal[:, :].unsqueeze(1).to_broadcast(spread), ALU.mult)\
                       .then_inc(attn_masked, 1)
                for n in range(CPB):
                    dve.wait_ge(kv_ready, n + 1)
                    dve.tensor_tensor(kv[:, n, :, :], bank[n][:, :, :], m.same[:, :].unsqueeze(1).to_broadcast(spread), ALU.mult)\
                       .then_inc(kv_masked, 1)
                for n in range(CPB):
                    dve.wait_ge(wk_ready, n + 1)
                    dve.tensor_tensor(trans[:, n, :, :], bank[4 + n][:, :, :], m.minus_same[:, :].unsqueeze(1).to_broadcast(spread),
                                      ALU.mult).then_inc(wk_masked, 1)
                dve.wait_ge(qw_ready, 1)
                dve.tensor_tensor(q_eff[:, :, :], q[:, :].rearrange("p (a b) -> p a b", a=GB), bank[0][:, :, :], ALU.subtract)\
                   .then_inc(q_eff_ready, 1)
                for t in range(1, CH - 1):
                    for s in range(NSEQ):
                        b, n = 2 * s + t // CPB, t % CPB
                        dve.wait_ge(s_ready, NSEQ * (t - 1) + s + 1)
                        dve.tensor_tensor(state[:, (t + 1) % 2, s, :], bank[2 + s][:, 0, :], kv[:, n, b, :], ALU.add)\
                           .then_inc(s_saved, 1)
                dve.wait_ge(o_turned, 1)
                link(dve.tensor_tensor(o[:, :, :], bank[4][:, :, :], v_tok[:, :, :], ALU.subtract))
                link(dve.tensor_tensor(by_head(o), by_head(o), beta[:, :, HEADS:].unsqueeze(3).to_broadcast(wide), ALU.mult))
                dve.tensor_tensor(o[:, :, :], o[:, :, :], v_tok[:, :, :], ALU.add).then_inc(mixed, 1)
                dve.wait_ge(squared, 1)
                dve.tensor_reduce(power[:, :], square, AX.X, ALU.add).then_inc(power_sum, 1)
                dve.wait_ge(power_ready, 1)
                heads = o[:, :, :].rearrange("p b (h x) -> p (b h) x", h=HEADS)
                dve.tensor_tensor(heads, heads, power[:, :].unsqueeze(2).to_broadcast([P, GB * HEADS, HD]), ALU.mult)\
                   .then_inc(normed, 1)

            @block.gpsimd
            def _(pool):
                link = Chain(pool, pool_step)
                for n in range(CPB):
                    pool.wait_ge(wk_masked, n + 1)
                    pool.tensor_tensor(trans[:, n, :, :], trans[:, n, :, :], c.ident[:, :].unsqueeze(1).to_broadcast([P, GB, P]),
                                       ALU.add).then_inc(trans_ready, 1)
                pool.wait_ge(power_sum, 1)
                link(pool.tensor_scalar(power[:, :], power[:, :], 1.0 / HD, LN_EPS, ALU.mult, ALU.add))
                pool.tensor_tensor(power[:, :], power[:, :], half[:, :], ALU.pow).then_inc(power_ready, 1)


def layer0_attention(nc, c, st, a):
    with ExitStack() as ctx:
        mem = Memory(nc, ctx)
        w3 = mem.sb("l0_w_qkv", [P, 3, P])
        taps = mem.sb("l0_taps", [P, 3, 4])
        w_b = mem.sb("l0_w_beta", [P, P])
        w_gates = mem.sb("l0_w_gates", [P, 2 * HEADS])
        w_o = mem.sb("l0_w_o", [P, D])
        norm_w = mem.sb("l0_norm_w", [P, 1])
        m = DeltaState(nc, mem)
        load(nc, [(w3[:, 0, :], a["L0_attn_Wq"]), (w3[:, 1, :], a["L0_attn_Wk"]), (w3[:, 2, :], a["L0_attn_Wv"]),
                  (taps[:, 0, :], a["L0_attn_conv_q"]), (taps[:, 1, :], a["L0_attn_conv_k"]), (taps[:, 2, :], a["L0_attn_conv_v"]),
                  (w_b[:, :], a["L0_attn_Wb_wide"]), (w_gates[:, 0:HEADS], a["L0_attn_Wb"]), (w_gates[:, HEADS:], a["L0_attn_Wmix"]),
                  (w_o[:, :], a["L0_attn_Wo"]), (norm_w[:, :], a["L0_attn_norm_w"])])
        delta_masks(nc, m)
        gates(nc, st, m, w_b, w_gates)
        project(nc, c, st, m, w3, taps)
        invert(nc, m)
        recur(nc, c, st, m, w_o, norm_w)


def attention16(nc, c, st, a):
    HEADS, HD, QUAD = 16, 8, 32
    Q = HEADS // 4
    SCALE = HD ** -0.5
    NB = 4
    ALL = NB * HEADS
    PLAN = [("qk", n, 4 * n - 4) for n in range(Q)] + [("v", 0, -3), ("v", 1, -1), ("out", 0, HEADS + 5)]
    jobs = {}
    for b in range(NB):
        for what, n, at in PLAN:
            jobs.setdefault(max(b * HEADS + at, 0), []).append((what, b, n))
    last = max(jobs) + 1
    order = [job for t in sorted(jobs) for job in jobs[t]]
    turn_of = {job: n for n, job in enumerate(order)}
    by_act = [sum(j[0] != "out" for j in order[:n]) for n in range(len(order) + 1)]
    by_dve = [n - m for n, m in enumerate(by_act)]
    with ExitStack() as ctx:
        mem = Memory(nc, ctx)
        wq = mem.sb("l0a_wq", [P, HEADS, QUAD])
        wk = mem.sb("l0a_wk", [P, HEADS, QUAD])
        wv = mem.sb("l0a_wv", [P, HEADS, QUAD])
        wo = mem.sb("l0a_wo", [P, Q, D])
        bq = mem.sb("l0a_bq", [P, Q])
        bk = mem.sb("l0a_bk", [P, Q])
        bv = mem.sb("l0a_bv", [P, Q])
        bo = mem.sb("l0a_bo", [P, D])
        with phase(nc, ["l0a_clear"]) as (block, _, (clear,)):
            @block.gpsimd
            def _(pool):
                for t in (wq, wk, wv, wo):
                    pool.memset(t[:, :, :], 0.0).then_inc(clear, 1)
                for t in (bq, bk, bv):
                    pool.memset(t[:, :], 0.0).then_inc(clear, 1)
                pool.wait_ge(clear, 7)
        pairs = [(wq[:, :, 0:HD], a["L0_ffn_Wq"]), (wk[:, :, 0:HD], a["L0_ffn_Wk"]), (wv[:, :, 0:HD], a["L0_ffn_Wv"]),
                 (bo[:, :], a["L0_ffn_bo"])]
        for s in range(4):
            rows = slice(QUAD * s, QUAD * s + HD)
            pairs += [(bq[rows, :], a["L0_ffn_bq"][s]), (bk[rows, :], a["L0_ffn_bk"][s]), (bv[rows, :], a["L0_ffn_bv"][s]),
                      (wo[rows, :, :], a["L0_ffn_Wo"][s])]
        load(nc, pairs)
        with phase(nc, ["l0a_scaled"]) as (block, _, (scaled,)):
            @block.vector
            def _(dve):
                dve.tensor_scalar(bq[:, :], bq[:, :], SCALE, None, ALU.mult).then_inc(scaled, 1)
        xs = mem.sb("l0a_x", [P, 2, SEQ])
        q = mem.sb("l0a_q", [P, 2, Q, SEQ])
        k = mem.sb("l0a_k", [P, 2, Q, SEQ])
        v = mem.sb("l0a_v", [P, 2, 2, HEADS * QUAD])
        prob = mem.sb("l0a_prob", [P, 3, 2, SEQ])
        turned = mem.sb("l0a_prob_t", [P, 2, 2, SEQ])
        neg_max = mem.sb("l0a_neg_max", [P, 4, 2])
        total = mem.sb("l0a_total", [P, 4, 2])
        z = mem.sb("l0a_z", [P, 2, Q, SEQ])
        ps = [mem.psum(f"l0a_ps{n}", [P, 2, SEQ]) for n in range(3)]
        pt = [mem.psum(f"l0a_pt{n}", [P, 2, SEQ]) for n in range(2)]
        pz = [mem.psum(f"l0a_pz{n}", [P, SEQ]) for n in range(2)]
        px = mem.psum("l0a_px", [P, 512])
        names = ["l0a_" + n for n in ("x_ready", "job_ready", "job_saved", "out_saved", "scores_ready", "max_ready", "exp_ready",
                                      "dve_step", "prob_ready", "turn_ready", "turned_saved", "z_ready", "z_saved")]
        with phase(nc, names, BATCH // NB) as (block, i, sems):
            (x_ready, job_ready, job_saved, out_saved, scores_ready, max_ready, exp_ready, dve_step, prob_ready, turn_ready,
             turned_saved, z_ready, z_saved) = sems

            @block.gpsimd
            def _(pool):
                for b in range(NB):
                    if b >= 2:
                        pool.wait_ge(job_ready, turn_of["qk", b - 2, Q - 1] + 1)
                    pool.tensor_copy(xs[:, b % 2, :], st.xnt[:, bass.ds(i * (NB * SEQ) + b * SEQ, SEQ)]).then_inc(x_ready, 1)

            @block.tensor
            def _(pe):
                def job(what, b, n):
                    m = turn_of[what, b, n]
                    if by_act[m]:
                        pe.wait_ge(job_saved, by_act[m])
                    if by_dve[m]:
                        pe.wait_ge(out_saved, by_dve[m])
                    if what == "out":
                        pe.wait_ge(z_saved, Q * (b + 1))
                        for t in range(2):
                            for g in range(Q):
                                ins = pe.matmul(px[:, t * P:(t + 1) * P], z[:, b % 2, g, t * P:(t + 1) * P], wo[:, g, :],
                                                start=(g == 0), stop=(g == Q - 1))
                    else:
                        pe.wait_ge(x_ready, b + 1)
                        x = xs[:, b % 2, :]
                    if what == "qk":
                        pe.matmul(px[:, 0:SEQ], wq[:, 4 * n:4 * n + 4, :], x, start=True, stop=True)
                        ins = pe.matmul(px[:, SEQ:], wk[:, 4 * n:4 * n + 4, :], x, start=True, stop=True)
                    if what == "v":
                        ins = pe.matmul(px[:, :], x[:, n * P:(n + 1) * P], wv[:, :, :], start=True, stop=True)
                    ins.then_inc(job_ready, 1)

                def scores(m):
                    b, h = m // HEADS, m % HEADS
                    if h % 4 == 0:
                        pe.wait_ge(job_saved, by_act[turn_of["qk", b, h // 4] + 1])
                    if m >= 3:
                        pe.wait_ge(exp_ready, 2 * (m - 2))
                    rows = slice(QUAD * (h % 4), QUAD * (h % 4) + QUAD)
                    for t in range(2):
                        ins = pe.matmul(ps[m % 3][:, t, :], q[rows, b % 2, h // 4, t * P:(t + 1) * P], k[rows, b % 2, h // 4, :],
                                        start=True, stop=True)
                    ins.then_inc(scores_ready, 1)

                def turn(m):
                    pe.wait_ge(prob_ready, 2 * m + 2)
                    if m >= 2:
                        pe.wait_ge(turned_saved, m - 1)
                    for t in range(2):
                        for s in range(2):
                            ins = pe.transpose(pt[m % 2][:, s, t * P:(t + 1) * P], prob[:, m % 3, t, s * P:(s + 1) * P],
                                               c.ident[:, :])
                    ins.then_inc(turn_ready, 1)

                def weigh(m):
                    b, h = m // HEADS, m % HEADS
                    g = m // 4
                    if h == 0:
                        pe.wait_ge(job_saved, by_act[turn_of["v", b, 1] + 1])
                    if h % 4 == 0 and g >= 2:
                        pe.wait_ge(z_saved, g - 1)
                    pe.wait_ge(turned_saved, m + 1)
                    rows = slice(QUAD * (h % 4), QUAD * (h % 4) + QUAD)
                    for s in range(2):
                        ins = pe.matmul(pz[g % 2][rows, :], v[:, b % 2, s, h * QUAD:(h + 1) * QUAD], turned[:, m % 2, s, :],
                                        start=(s == 0), stop=(s == 1))
                    ins.then_inc(z_ready, 1)

                for m in range(max(ALL + 3, last)):
                    for j in jobs.get(m, []):
                        job(*j)
                    if m < ALL:
                        scores(m)
                    if 0 <= m - 2 < ALL:
                        turn(m - 2)
                    if 0 <= m - 3 < ALL:
                        weigh(m - 3)

            @block.scalar
            def _(act):
                def save(what, b, n):
                    act.wait_ge(job_ready, turn_of[what, b, n] + 1)
                    if what == "qk":
                        if b >= 2:
                            act.wait_ge(scores_ready, HEADS * (b - 2) + 4 * n + 4)
                        act.activation(q[:, b % 2, n, :], px[:, 0:SEQ], ACT.Identity, bias=bq[:, n:n + 1], scale=SCALE)
                        act.activation(k[:, b % 2, n, :], px[:, SEQ:], ACT.Identity, bias=bk[:, n:n + 1]).then_inc(job_saved, 1)
                    else:
                        if b >= 2:
                            act.wait_ge(z_ready, HEADS * (b - 1))
                        act.activation(v[:, b % 2, n, :], px[:, :], ACT.Copy).then_inc(job_saved, 1)

                def exp(m):
                    act.wait_ge(max_ready, m + 1)
                    if m >= 3:
                        act.wait_ge(turn_ready, m - 2)
                    for t in range(2):
                        act.activation(prob[:, m % 3, t, :], ps[m % 3][:, t, :], ACT.Exp, bias=neg_max[:, m % 4, t:t + 1],
                                       accum_out=total[:, m % 4, t:t + 1]).then_inc(exp_ready, 1)

                def save_z(g):
                    b = g // Q
                    act.wait_ge(z_ready, 4 * g + 4)
                    if b >= 2 and g % Q == 0:
                        act.wait_ge(job_ready, turn_of["out", b - 2, 0] + 1)
                    act.activation(z[:, b % 2, g % Q, :], pz[g % 2][:, :], ACT.Identity, bias=bv[:, g % Q:g % Q + 1])\
                       .then_inc(z_saved, 1)

                for m in range(max(ALL + 4, last)):
                    for j in jobs.get(m, []):
                        if j[0] != "out":
                            save(*j)
                    if m < ALL:
                        exp(m)
                    if m >= 7 and m % 4 == 3 and m // 4 - 1 < ALL // 4:
                        save_z(m // 4 - 1)

            @block.vector
            def _(dve):
                link = Chain(dve, dve_step)
                for m in range(max(ALL + 2, last)):
                    if m < ALL:
                        dve.wait_ge(scores_ready, m + 1)
                        dve.tensor_reduce(neg_max[:, m % 4, :], ps[m % 3][:, :, :], AX.X, ALU.max, negate=True).then_inc(max_ready, 1)
                    if 1 <= m <= ALL:
                        n = m - 1
                        dve.wait_ge(exp_ready, 2 * n + 2)
                        link(dve.reciprocal(total[:, n % 4, :], total[:, n % 4, :]))
                        for t in range(2):
                            dve.tensor_scalar(prob[:, n % 3, t, :], prob[:, n % 3, t, :], total[:, n % 4, t:t + 1], None, ALU.mult)\
                               .then_inc(prob_ready, 1)
                    if 2 <= m < ALL + 2:
                        n = m - 2
                        dve.wait_ge(turn_ready, n + 1)
                        if n >= 2:
                            dve.wait_ge(z_ready, n - 1)
                        dve.tensor_copy(turned[:, n % 2, :, :], pt[n % 2][:, :, :]).then_inc(turned_saved, 1)
                    for what, b, n in jobs.get(m, []):
                        if what == "out":
                            rows = st.g[:, bass.ds(i * (2 * NB) + 2 * b, 2), :]
                            dve.wait_ge(job_ready, turn_of[what, b, n] + 1)
                            ins = dve.tensor_tensor(rows, px[:, 0:2 * P].rearrange("p (a b) -> p a b", a=2),
                                                    bo[:, :].unsqueeze(1).to_broadcast([P, 2, D]), ALU.add)
                            ins.then_inc(out_saved, 1)
                            dve.wait_ge(out_saved, b + 1)
                            dve.tensor_tensor(rows, rows, st.xn[:, bass.ds(i * (2 * NB) + 2 * b, 2), :], ALU.add)


def layer0_ffn(nc, c, st, a):
    E, F = 8, 256
    U = E * F // P
    attention16(nc, c, st, a)
    with ExitStack() as ctx:
        mem = Memory(nc, ctx)
        w1 = mem.sb("l0f_w1", [P, U, P])
        w2 = mem.sb("l0f_w2", [P, U, D])
        b1 = mem.sb("l0f_b1", [P, U])
        b2 = mem.sb("l0f_b2", [E, D])
        gw = mem.sb("l0f_gw", [P, E])
        gb = mem.sb("l0f_gb", [P, E])
        norms = mem.sb("l0f_norms", [P, 4, D])
        w_tok = mem.sb("l0f_w_tok", [P, BLK, E])
        h_tok = mem.sb("l0f_h_tok", [P, BLK, D])
        h_ch = mem.sb("l0f_h_ch", [P, TOK])
        load(nc, [(w1[:, :, :], a["L0_ffn_W1"]), (w2[:, :, :], a["L0_ffn_W2"]), (b1[:, :], a["L0_ffn_b1"]),
                  (b2[:, :], a["L0_ffn_b2"]), (gw[:, :], a["L0_ffn_gW"]), (gb[:, :], a["L0_ffn_gb"]),
                  (norms[:, 0, :], a["L0_ffn_ln1_g"]), (norms[:, 1, :], a["L0_ffn_ln1_b"]),
                  (norms[:, 2, :], a["L0_ffn_ln2_g"]), (norms[:, 3, :], a["L0_ffn_ln2_b"])])
        layer_norm(nc, c, "l0n1", st.g, h_tok, h_ch, norms[:, 0, :], norms[:, 1, :])
        top_two(nc, c, st, "l0r", h_ch, gw, gb, E, w_tok, softmax=True)
        experts(nc, c, st, "l0e", h_ch, w_tok, E, F // P, ACT.Relu, w1, w2, b1=b1, b2=b2, residual=h_tok)
        layer_norm(nc, c, "l0n2", st.g, st.g, None, norms[:, 2, :], norms[:, 3, :])


def layer1_attention(nc, c, st, a):
    INNER, STATES, TAPS = 256, 16, 4
    CH = INNER // P
    PAD = TAPS - 1
    NSEQ = GT // SEQ
    with ExitStack() as ctx:
        mem = Memory(nc, ctx)
        w_in = mem.sb("l1_w_in", [P, 2 * CH, P])
        conv_w = mem.sb("l1_conv_w", [P, CH, TAPS])
        conv_b = mem.sb("l1_conv_b", [P, CH])
        w_b = mem.sb("l1_w_b", [P, CH, STATES])
        w_c = mem.sb("l1_w_c", [STATES, CH, P])
        w_out = mem.sb("l1_w_out", [P, CH, D])
        load(nc, [(w_in[:, :, :], a["L1_attn_w_in"]), (conv_w[:, :, :], a["L1_attn_conv_w"]), (conv_b[:, :], a["L1_attn_conv_b"]),
                  (w_b[:, :, :], a["L1_attn_w_B"]), (w_c[:, :, :], a["L1_attn_w_C"]), (w_out[:, :, :], a["L1_attn_w_out"])])
        padded = mem.sb("l1_padded", [P, CH, NSEQ, PAD + SEQ])
        conv = mem.sb("l1_conv", [P, CH, NSEQ, SEQ])
        zs = mem.sb("l1_zs", [P, CH, GT])
        decay = mem.sb("l1_decay", [STATES, SEQ])
        drive = mem.sb("l1_drive", [STATES, NSEQ, SEQ])
        state = mem.sb("l1_state", [STATES, NSEQ, SEQ])
        yz = mem.sb("l1_yz", [P, CH, GT])
        p_in = [mem.psum(f"l1_p_in{n}", [P, NSEQ, SEQ]) for n in range(2 * CH)]
        p_b = mem.psum("l1_p_b", [STATES, NSEQ, SEQ])
        p_y = [mem.psum(f"l1_p_y{n}", [P, GT]) for n in range(CH)]
        p_o = mem.psum("l1_p_o", [P, GB, D])
        with phase(nc, ["l1_set"]) as (block, _, (l1_set,)):
            @block.gpsimd
            def _(pool):
                pool.memset(padded[:, :, :, :], 0.0).then_inc(l1_set, 1)
                pool.memset(decay[:, :], 0.9).then_inc(l1_set, 1)
                pool.wait_ge(l1_set, 2)
        names = ["l1_" + n for n in ("in_ready", "x_saved", "z_saved", "dve_step", "conv_ready", "xc_ready", "b_ready",
                                     "drive_ready", "state_ready", "y_ready", "yz_ready", "o_ready")]
        with phase(nc, names, GRP) as (block, i, sems):
            (in_ready, x_saved, z_saved, dve_step, conv_ready, xc_ready, b_ready, drive_ready, state_ready, y_ready,
             yz_ready, o_ready) = sems

            @block.tensor
            def _(pe):
                for n in range(2 * CH):
                    pe.matmul(p_in[n][:, :, :], w_in[:, n, :], st.xnt[:, bass.ds(i * GT, GT)], start=True, stop=True)\
                      .then_inc(in_ready, 1)
                for n in range(CH):
                    pe.wait_ge(xc_ready, n + 1)
                    ins = pe.matmul(p_b[:, :, :], w_b[:, n, :], conv[:, n, :, :], start=(n == 0), stop=(n == CH - 1))
                ins.then_inc(b_ready, 1)
                pe.wait_ge(state_ready, NSEQ)
                for n in range(CH):
                    pe.matmul(p_y[n][:, :], w_c[:, n, :], state[:, :, :], start=True, stop=True).then_inc(y_ready, 1)
                pe.wait_ge(yz_ready, CH)
                for j in range(GB):
                    for n in range(CH):
                        ins = pe.matmul(p_o[:, j, :], yz[:, n, j * P:(j + 1) * P], w_out[:, n, :],
                                        start=(n == 0), stop=(n == CH - 1))
                ins.then_inc(o_ready, 1)

            @block.scalar
            def _(act):
                for n in range(CH):
                    act.wait_ge(in_ready, n + 1)
                    act.activation(padded[:, n, :, PAD:], p_in[n][:, :, :], ACT.Copy).then_inc(x_saved, 1)
                for n in range(CH):
                    act.wait_ge(in_ready, CH + n + 1)
                    act.activation(zs[:, n, :].rearrange("p (a b) -> p a b", a=NSEQ), p_in[CH + n][:, :, :], ACT.Silu)\
                       .then_inc(z_saved, 1)
                for n in range(CH):
                    act.wait_ge(conv_ready, n + 1)
                    act.activation(conv[:, n, :, :], conv[:, n, :, :], ACT.Silu, bias=conv_b[:, n:n + 1]).then_inc(xc_ready, 1)
                act.wait_ge(b_ready, 1)
                act.activation(drive[:, :, :], p_b[:, :, :], ACT.Copy, scale=0.1).then_inc(drive_ready, 1)
                act.wait_ge(o_ready, 1)
                act.activation(st.s[:, bass.ds(i * GB, GB), :], p_o[:, :, :], ACT.Copy)

            @block.vector
            def _(dve):
                link = Chain(dve, dve_step)
                for n in range(CH):
                    dve.wait_ge(x_saved, n + 1)
                    out = conv[:, n, :, :]
                    for k in range(TAPS):
                        x = padded[:, n, :, k:k + SEQ]
                        if k == 0:
                            link(dve.tensor_scalar(out, x, conv_w[:, n, k:k + 1], None, ALU.mult))
                        else:
                            ins = dve.scalar_tensor_tensor(out, x, conv_w[:, n, k:k + 1], out, ALU.mult, ALU.add)
                            if k < TAPS - 1:
                                link(ins)
                    ins.then_inc(conv_ready, 1)
                dve.wait_ge(drive_ready, 1)
                for s in range(NSEQ):
                    dve.tensor_tensor_scan(state[:, s, :], decay[:, :], drive[:, s, :], 0.0, ALU.mult, ALU.add)\
                       .then_inc(state_ready, 1)
                for n in range(CH):
                    dve.wait_ge(y_ready, n + 1)
                    dve.wait_ge(z_saved, n + 1)
                    dve.tensor_tensor(yz[:, n, :], p_y[n][:, :], zs[:, n, :], ALU.mult).then_inc(yz_ready, 1)


def layer1_ffn(nc, c, st, a):
    E, H = 8, 256
    with ExitStack() as ctx:
        mem = Memory(nc, ctx)
        w1 = mem.sb("l1f_w1", [P, E * H // P, P])
        w3 = mem.sb("l1f_w3", [P, E * H // P, P])
        w2 = mem.sb("l1f_w2", [P, E * H // P, D])
        gw = mem.sb("l1f_gw", [P, E])
        w_tok = mem.sb("l1f_w_tok", [P, BLK, E])
        load(nc, [(w1[:, :, :], a["L1_ffn_W1"]), (w3[:, :, :], a["L1_ffn_W3"]), (w2[:, :, :], a["L1_ffn_W2"]),
                  (gw[:, :], a["L1_ffn_Wg"])])
        with ExitStack() as inner:
            mem = Memory(nc, inner)
            score = mem.sb("l1f_score", [P, E, BLK])
            chosen = mem.sb("l1f_chosen", [P, E, BLK])
            token_scores(nc, "l1f", st.xnt, gw, E, score)
            choose(nc, c, "l1c", score, chosen, E, TOK // E)
            softmax_of_chosen(nc, c, score, chosen, w_tok, E)
        experts(nc, c, st, "l1e", st.xnt, w_tok, E, H // P, ACT.Silu, w1, w2, w3=w3)


def softmax_of_chosen(nc, c, score, chosen, w_tok, n_exp):
    with ExitStack() as ctx:
        mem = Memory(nc, ctx)
        best = mem.sb("l1s_best", [P, n_exp])
        top = mem.sb("l1s_top", [P, n_exp])
        part = mem.sb("l1s_part", [P, n_exp])
        recip = mem.sb("l1s_recip", [P, n_exp])
        p_sum = mem.psum("l1s_sum", [P, n_exp])
        wide = [P, n_exp, BLK]
        with phase(nc, ["l1s_dve_step", "l1s_best_ready", "l1s_top_ready", "l1s_shifted", "l1s_exp_ready", "l1s_part_ready",
                        "l1s_sum_ready"]) as (block, _, sems):
            dve_step, best_ready, top_ready, shifted, exp_ready, part_ready, sum_ready = sems

            @block.vector
            def _(dve):
                link = Chain(dve, dve_step)
                dve.tensor_reduce(best[:, :], score[:, :, :], AX.X, ALU.max).then_inc(best_ready, 1)
                dve.wait_ge(top_ready, 1)
                dve.tensor_tensor(score[:, :, :], score[:, :, :], top[:, :].unsqueeze(2).to_broadcast(wide), ALU.subtract)\
                   .then_inc(shifted, 1)
                dve.wait_ge(exp_ready, 1)
                link(dve.tensor_tensor(score[:, :, :], score[:, :, :], chosen[:, :, :], ALU.mult))
                dve.tensor_reduce(part[:, :], score[:, :, :], AX.X, ALU.add).then_inc(part_ready, 1)
                dve.wait_ge(sum_ready, 1)
                link(dve.reciprocal(recip[:, :], p_sum[:, :]))
                link(dve.tensor_tensor(w_tok[:, :, :].rearrange("p b e -> p e b"), score[:, :, :],
                                       recip[:, :].unsqueeze(2).to_broadcast(wide), ALU.mult))

            @block.gpsimd
            def _(pool):
                pool.wait_ge(best_ready, 1)
                pool.partition_all_reduce(top[:, :], best[:, :], P, bass.bass_isa.ReduceOp.max).then_inc(top_ready, 1)

            @block.scalar
            def _(act):
                act.wait_ge(shifted, 1)
                act.activation(score[:, :, :], score[:, :, :], ACT.Exp).then_inc(exp_ready, 1)

            @block.tensor
            def _(pe):
                pe.wait_ge(part_ready, 1)
                pe.matmul(p_sum[:, :], c.ones[:, :], part[:, :], start=True, stop=True).then_inc(sum_ready, 1)


WINDOW = 16
BEFORE = (WINDOW - 1) // 2
PITCH = SEQ + WINDOW


def layer2_attention(nc, c, st, a):
    KG = 4
    with ExitStack() as ctx:
        mem = Memory(nc, ctx)
        band = nc.dram_tensor("l2_band", (BATCH * SEQ * PITCH,), F32, kind="Internal").ap()
        w1 = mem.sb("l2_w1", [P, D])
        w2 = mem.sb("l2_w2", [P, D])
        v = mem.sb("l2_v", [P, 1])
        zero = mem.sb("l2_zero", [P, 2, PITCH])
        padded = mem.sb("l2_padded", [P, WINDOW - 1 + SEQ])
        load(nc, [(w1[:, :], a["L2_attn_w1"]), (w2[:, :], a["L2_attn_w2"]), (v[:, :], a["L2_attn_v"])])
        with phase(nc, ["l2_zero_set", "l2_band_cleared"]) as (block, _, (zero_set, band_cleared)):
            @block.gpsimd
            def _(pool):
                pool.memset(zero[:, :, :], 0.0).then_inc(zero_set, 1)
                pool.memset(padded[:, :], 0.0).then_inc(zero_set, 1)

            @block.sync
            def _(sp):
                sp.wait_ge(zero_set, 2)
                for b in range(BATCH):
                    rows = band[b * SEQ * PITCH:(b + 1) * SEQ * PITCH].rearrange("(t p n) -> p t n", t=2, p=P)
                    sp.dma_start(rows, zero[:, :, :]).then_inc(band_cleared, 16)
                sp.wait_ge(band_cleared, 16 * BATCH)

        with ExitStack() as inner:
            mem = Memory(nc, inner)
            q = mem.sb("l2_q", [P, SEQ])
            th = mem.sb("l2_tanh", [P, WINDOW, SEQ])
            prob = mem.sb("l2_prob", [P, 2, WINDOW])
            small = mem.sb("l2_small", [P, 2])
            pp = mem.psum("l2_pp", [P, SEQ])
            pq = mem.psum("l2_pq", [P, SEQ])
            ps = mem.psum("l2_ps", [P, 2, WINDOW])
            names = ["l2_" + n for n in ("proj_ready", "p_saved", "q_saved", "sum_ready", "tanh_ready", "score_ready", "dve_step",
                                         "shifted", "exp_ready", "weight_ready", "stored")]
            with phase(nc, names, BATCH) as (block, i, sems):
                (proj_ready, p_saved, q_saved, sum_ready, tanh_ready, score_ready, dve_step, shifted, exp_ready, weight_ready,
                 stored) = sems

                @block.tensor
                def _(pe):
                    x = st.xnt[:, bass.ds(i * SEQ, SEQ)]
                    pe.matmul(pp[:, :], w2[:, :], x, start=True, stop=True).then_inc(proj_ready, 1)
                    pe.matmul(pq[:, :], w1[:, :], x, start=True, stop=True).then_inc(proj_ready, 1)
                    for k in range(WINDOW):
                        pe.wait_ge(tanh_ready, k // KG + 1)
                        for t in range(2):
                            ins = pe.matmul(ps[:, t, k:k + 1], th[:, k, t * P:(t + 1) * P], v[:, :], start=True, stop=True)
                    ins.then_inc(score_ready, 1)

                @block.scalar
                def _(act):
                    act.wait_ge(proj_ready, 1)
                    act.activation(padded[:, BEFORE:BEFORE + SEQ], pp[:, :], ACT.Copy).then_inc(p_saved, 1)
                    for n in range(WINDOW // KG):
                        act.wait_ge(sum_ready, KG * (n + 1))
                        part = th[:, n * KG:(n + 1) * KG, :]
                        act.activation(part, part, ACT.Tanh).then_inc(tanh_ready, 1)
                    act.wait_ge(shifted, 1)
                    act.activation(prob[:, :, :], prob[:, :, :], ACT.Exp).then_inc(exp_ready, 1)

                @block.vector
                def _(dve):
                    link = Chain(dve, dve_step)
                    spread = small[:, :].unsqueeze(2).to_broadcast([P, 2, WINDOW])
                    dve.wait_ge(proj_ready, 2)
                    dve.tensor_copy(q[:, :], pq[:, :]).then_inc(q_saved, 1)
                    dve.wait_ge(q_saved, 1)
                    dve.wait_ge(p_saved, 1)
                    for k in range(WINDOW):
                        dve.tensor_tensor(th[:, k, :], padded[:, k:k + SEQ], q[:, :], ALU.add).then_inc(sum_ready, 1)
                    dve.wait_ge(score_ready, 1)
                    link(dve.tensor_reduce(small[:, :], ps[:, :, :], AX.X, ALU.max))
                    dve.tensor_tensor(prob[:, :, :], ps[:, :, :], spread, ALU.subtract).then_inc(shifted, 1)
                    dve.wait_ge(exp_ready, 1)
                    link(dve.tensor_reduce(small[:, :], prob[:, :, :], AX.X, ALU.add))
                    link(dve.reciprocal(small[:, :], small[:, :]))
                    dve.tensor_tensor(prob[:, :, :], prob[:, :, :], spread, ALU.mult).then_inc(weight_ready, 1)

                @block.sync
                def _(sp):
                    sp.wait_ge(weight_ready, 1)
                    rows = band[bass.ds(i * (SEQ * PITCH), SEQ * PITCH)]
                    for t in range(2):
                        dst = bass.AP(rows.tensor, rows.offset + t * P * (PITCH + 1), [[PITCH + 1, P], [1, WINDOW]])
                        sp.dma_start(dst, prob[:, t, :]).then_inc(stored, 16)
                    sp.wait_ge(stored, 32)

        with ExitStack() as inner:
            mem = Memory(nc, inner)
            NB = 2
            rows_sb = mem.sb("l2_rows", [P, 2 * NB, SEQ])
            turned = mem.sb("l2_turned", [P, 4 * NB, P])
            pt = [mem.psum(f"l2_pt{n}", [P, 4, P]) for n in range(NB)]
            po = mem.psum("l2_po", [P, 2 * NB, D])
            with phase(nc, ["l2_loaded", "l2_turn_ready", "l2_turn_saved", "l2_out_ready"], BATCH // NB) as (block, i, sems):
                loaded, turn_ready, turn_saved, out_ready = sems

                @block.sync
                def _(sp):
                    src = band[bass.ds(i * (NB * SEQ * PITCH), NB * SEQ * PITCH)].rearrange("(n p w) -> p n w", p=P, w=PITCH)
                    sp.dma_start(rows_sb[:, :, :], src[:, :, BEFORE:BEFORE + SEQ]).then_inc(loaded, 16)

                @block.tensor
                def _(pe):
                    pe.wait_ge(loaded, 16)
                    for n in range(NB):
                        for t in range(2):
                            for s in range(2):
                                ins = pe.transpose(pt[n][:, 2 * t + s, :], rows_sb[:, 2 * n + t, s * P:(s + 1) * P], c.ident[:, :])
                        ins.then_inc(turn_ready, 1)
                    for n in range(NB):
                        pe.wait_ge(turn_saved, n + 1)
                        for t in range(2):
                            for s in range(2):
                                ins = pe.matmul(po[:, 2 * n + t, :], turned[:, 4 * n + 2 * t + s, :],
                                                st.xn[:, i * (2 * NB) + 2 * n + s, :], start=(s == 0), stop=(s == 1))
                    ins.then_inc(out_ready, 1)

                @block.vector
                def _(dve):
                    for n in range(NB):
                        dve.wait_ge(turn_ready, n + 1)
                        dve.tensor_copy(turned[:, 4 * n:4 * n + 4, :], pt[n][:, :, :]).then_inc(turn_saved, 1)

                @block.scalar
                def _(act):
                    act.wait_ge(out_ready, 1)
                    act.activation(st.s[:, bass.ds(i * (2 * NB), 2 * NB), :], po[:, :, :], ACT.Copy)


def layer2_ffn(nc, c, st, a):
    E, F = 8, 512
    U = E * F // P
    with ExitStack() as ctx:
        mem = Memory(nc, ctx)
        w1 = mem.sb("l2f_w1", [P, U, P])
        w2 = mem.sb("l2f_w2", [P, U, D])
        b1 = mem.sb("l2f_b1", [P, U])
        b2 = mem.sb("l2f_b2", [E, D])
        cent = mem.sb("l2f_cent", [P, E])
        gain = mem.sb("l2f_gain", [P, D])
        shift = mem.sb("l2f_shift", [P, D])
        w_tok = mem.sb("l2f_w_tok", [P, BLK, E])
        norm_ch = mem.sb("l2f_norm_ch", [P, TOK])
        load(nc, [(w1[:, :, :], a["L2_ffn_w1"]), (w2[:, :, :], a["L2_ffn_w2"]), (b1[:, :], a["L2_ffn_b1"]),
                  (b2[:, :], a["L2_ffn_b2"]), (cent[:, :], a["L2_ffn_centroids"]), (gain[:, :], a["L2_ffn_ln_g"]),
                  (shift[:, :], a["L2_ffn_ln_b"])])
        layer_norm(nc, c, "l2n", st.xn, None, norm_ch, gain[:, :], shift[:, :])
        with ExitStack() as inner:
            mem = Memory(nc, inner)
            score = mem.sb("l2f_score", [P, E, BLK])
            chosen = mem.sb("l2f_chosen", [P, E, BLK])
            token_scores(nc, "l2f", norm_ch, cent, E, score)
            choose(nc, c, "l2c", score, chosen, E, TOK // E, in_turn=True)
            with phase(nc, ["l2f_w_ready"]) as (block, _, (w_ready,)):
                @block.vector
                def _(dve):
                    dve.tensor_copy(w_tok[:, :, :], chosen[:, :, :].rearrange("p e b -> p b e")).then_inc(w_ready, 1)
        experts(nc, c, st, "l2e", norm_ch, w_tok, E, F // P, ACT.Gelu_apprx_tanh, w1, w2, b1=b1, b2=b2, residual=st.xn)


def layer3_attention(nc, c, st, a):
    HEADS, HD = 16, 64
    PAIRS = HEADS // 2
    HALF = HEADS * HD // 2
    NB = 4
    ALL = NB * HEADS
    PLAN = [("qk", n, 2 * n - 4) for n in range(PAIRS)] + [("v", n, 2 * n - 3) for n in range(4)] + [("out", 0, HEADS + 5)]
    jobs = {}
    for b in range(NB):
        for what, n, at in PLAN:
            jobs.setdefault(max(b * HEADS + at, 0), []).append((what, b, n))
    last = max(jobs) + 1
    order = [job for t in sorted(jobs) for job in jobs[t]]
    turn_of = {job: n for n, job in enumerate(order)}
    by_act = [sum(j[0] != "out" for j in order[:n]) for n in range(len(order) + 1)]
    by_dve = [sum(j[0] != "v" for j in order[:n]) for n in range(len(order) + 1)]
    with ExitStack() as ctx:
        mem = Memory(nc, ctx)
        wq = mem.sb("l3_wq", [P, PAIRS, P])
        wk = mem.sb("l3_wk", [P, PAIRS, P])
        wv = mem.sb("l3_wv", [P, HEADS * HD])
        wo = mem.sb("l3_wo", [P, PAIRS, D])
        bq = mem.sb("l3_bq", [P, PAIRS])
        bk = mem.sb("l3_bk", [P, PAIRS])
        bv = mem.sb("l3_bv", [P, PAIRS])
        bo = mem.sb("l3_bo", [P, D])
        load(nc, [(wq[:, :, :], a["L3_attn_W_Q"]), (wk[:, :, :], a["L3_attn_W_K"]), (wv[:, :], a["L3_attn_W_V"]),
                  (wo[:, :, :], a["L3_attn_W_O"]), (bq[:, :], a["L3_attn_b_Q"]), (bk[:, :], a["L3_attn_b_K"]),
                  (bv[:, :], a["L3_attn_b_V"]), (bo[:, :], a["L3_attn_b_O"])])
        bq8 = mem.sb("l3_bq8", [P, PAIRS])
        with phase(nc, ["l3_bias_ready"]) as (block, _, (bias_ready,)):
            @block.vector
            def _(dve):
                dve.tensor_scalar(bq8[:, :], bq[:, :], 1 / 8, None, ALU.mult).then_inc(bias_ready, 1)
        xs = mem.sb("l3_x", [P, 2, SEQ])
        q = mem.sb("l3_q", [P, 2, PAIRS, SEQ])
        k = mem.sb("l3_k", [P, 2, PAIRS, SEQ])
        v = mem.sb("l3_v", [P, 2, 2, HEADS * HD])
        prob = mem.sb("l3_prob", [P, 3, 3 * P])
        turned = mem.sb("l3_prob_t", [P, 2, 3 * P])
        neg_max = mem.sb("l3_neg_max", [P, 4, 2])
        total = mem.sb("l3_total", [P, 4, 2])
        z = mem.sb("l3_z", [P, 2, PAIRS, SEQ])
        ps = [mem.psum(f"l3_ps{n}", [P, 512]) for n in range(3)]
        pt = [mem.psum(f"l3_pt{n}", [P, 512]) for n in range(2)]
        pz = [mem.psum(f"l3_pz{n}", [P, 512]) for n in range(2)]
        px = mem.psum("l3_px", [P, 512])
        names = ["l3_" + n for n in ("x_ready", "job_ready", "job_saved", "k_saved", "scores_ready", "max_ready", "exp_ready",
                                     "dve_step", "prob_ready", "turn_ready", "turned_saved", "z_ready", "z_saved")]
        with phase(nc, names, BATCH // NB) as (block, i, sems):
            (x_ready, job_ready, job_saved, k_saved, scores_ready, max_ready, exp_ready, dve_step, prob_ready, turn_ready,
             turned_saved, z_ready, z_saved) = sems

            @block.gpsimd
            def _(pool):
                for b in range(NB):
                    if b >= 2:
                        pool.wait_ge(job_ready, turn_of["qk", b - 2, PAIRS - 1] + 1)
                    pool.tensor_copy(xs[:, b % 2, :], st.xnt[:, bass.ds(i * (NB * SEQ) + b * SEQ, SEQ)]).then_inc(x_ready, 1)

            @block.tensor
            def _(pe):
                def job(what, b, n):
                    m = turn_of[what, b, n]
                    if by_act[m]:
                        pe.wait_ge(job_saved, by_act[m])
                    if by_dve[m]:
                        pe.wait_ge(k_saved, by_dve[m])
                    if what == "out":
                        pe.wait_ge(z_saved, PAIRS * (b + 1))
                        for t in range(2):
                            for g in range(PAIRS):
                                ins = pe.matmul(px[:, t * P:(t + 1) * P], z[:, b % 2, g, t * P:(t + 1) * P], wo[:, g, :],
                                                start=(g == 0), stop=(g == PAIRS - 1))
                    else:
                        pe.wait_ge(x_ready, b + 1)
                        x = xs[:, b % 2, :]
                    if what == "qk":
                        pe.matmul(px[:, 0:SEQ], wq[:, n, :], x, start=True, stop=True)
                        ins = pe.matmul(px[:, SEQ:], wk[:, n, :], x, start=True, stop=True)
                    if what == "v":
                        t, half = n % 2, n // 2
                        ins = pe.matmul(px[:, :], x[:, t * P:(t + 1) * P], wv[:, half * HALF:(half + 1) * HALF],
                                        start=True, stop=True)
                    ins.then_inc(job_ready, 1)

                def scores(m):
                    b, h = m // HEADS, m % HEADS
                    if h % 2 == 0:
                        done = turn_of["qk", b, h // 2] + 1
                        pe.wait_ge(job_saved, by_act[done])
                        pe.wait_ge(k_saved, by_dve[done])
                    if m >= 3:
                        pe.wait_ge(exp_ready, 2 * (m - 2))
                    rows = slice(HD * (h % 2), HD * (h % 2) + HD)
                    out, qh, kh = ps[m % 3], q[rows, b % 2, h // 2, :], k[rows, b % 2, h // 2, :]
                    pe.matmul(out[:, 0:P], qh[:, 0:P], kh[:, 0:P], start=True, stop=False)
                    pe.matmul(out[:, 0:P], c.ident_bf[:, :], c.future[:, :], start=False, stop=True)
                    pe.matmul(out[:, P:3 * P], qh[:, P:], kh[:, :], start=True, stop=False, skip_group_check=True)
                    pe.matmul(out[:, 2 * P:3 * P], c.ident_bf[:, :], c.future[:, :], start=False, stop=True,
                              skip_group_check=True).then_inc(scores_ready, 1)

                def turn(m):
                    pe.wait_ge(prob_ready, 2 * m + 2)
                    if m >= 2:
                        pe.wait_ge(turned_saved, m - 1)
                    for j in range(3):
                        ins = pe.transpose(pt[m % 2][:, j * P:(j + 1) * P], prob[:, m % 3, j * P:(j + 1) * P], c.ident[:, :])
                    ins.then_inc(turn_ready, 1)

                def weigh(m):
                    b, h = m // HEADS, m % HEADS
                    n, rows = m // 2, slice(HD * (h % 2), HD * (h % 2) + HD)
                    if h % 8 == 0:
                        pe.wait_ge(job_saved, by_act[turn_of["v", b, 2 * (h // 8) + 1] + 1])
                    if h % 2 == 0 and n >= 2:
                        pe.wait_ge(z_saved, n - 1)
                    pe.wait_ge(turned_saved, m + 1)
                    out, cols = pz[n % 2], slice(h * HD, (h + 1) * HD)
                    pe.matmul(out[rows, 0:SEQ], v[:, b % 2, 0, cols], turned[:, m % 2, 0:SEQ], start=True, stop=False,
                              skip_group_check=True)
                    pe.matmul(out[rows, P:SEQ], v[:, b % 2, 1, cols], turned[:, m % 2, SEQ:], start=False, stop=True,
                              skip_group_check=True).then_inc(z_ready, 1)

                for m in range(max(ALL + 3, last)):
                    for j in jobs.get(m, []):
                        job(*j)
                    if m < ALL:
                        scores(m)
                    if 0 <= m - 2 < ALL:
                        turn(m - 2)
                    if 0 <= m - 3 < ALL:
                        weigh(m - 3)

            @block.scalar
            def _(act):
                def save(what, b, n):
                    act.wait_ge(job_ready, turn_of[what, b, n] + 1)
                    if what == "qk":
                        if b >= 2:
                            act.wait_ge(scores_ready, HEADS * (b - 2) + 2 * n + 2)
                        act.activation(q[:, b % 2, n, :], px[:, 0:SEQ], ACT.Identity, bias=bq8[:, n:n + 1], scale=1 / 8)\
                           .then_inc(job_saved, 1)
                    else:
                        t, half = n % 2, n // 2
                        if b >= 2:
                            act.wait_ge(z_ready, HEADS * (b - 1))
                        act.activation(v[:, b % 2, t, half * HALF:(half + 1) * HALF], px[:, :], ACT.Copy).then_inc(job_saved, 1)

                def exp(m):
                    act.wait_ge(max_ready, 2 * m + 2)
                    if m >= 3:
                        act.wait_ge(turn_ready, m - 2)
                    row = prob[:, m % 3, :]
                    act.activation(row[:, 0:P], ps[m % 3][:, 0:P], ACT.Exp, bias=neg_max[:, m % 4, 0:1],
                                   accum_out=total[:, m % 4, 0:1]).then_inc(exp_ready, 1)
                    act.activation(row[:, P:], ps[m % 3][:, P:3 * P], ACT.Exp, bias=neg_max[:, m % 4, 1:2],
                                   accum_out=total[:, m % 4, 1:2]).then_inc(exp_ready, 1)

                def save_z(g):
                    b, n = g // PAIRS, g % PAIRS
                    act.wait_ge(z_ready, 2 * g + 2)
                    if b >= 2 and n == 0:
                        act.wait_ge(job_ready, turn_of["out", b - 2, 0] + 1)
                    act.activation(z[:, b % 2, n, :], pz[g % 2][:, 0:SEQ], ACT.Identity, bias=bv[:, n:n + 1]).then_inc(z_saved, 1)

                for m in range(max(ALL + 4, last)):
                    for j in jobs.get(m, []):
                        if j[0] != "out":
                            save(*j)
                    if m < ALL:
                        exp(m)
                    if m >= 5 and m % 2 == 1 and (m - 5) // 2 < ALL // 2:
                        save_z((m - 5) // 2)

            @block.vector
            def _(dve):
                link = Chain(dve, dve_step)
                for m in range(max(ALL + 2, last)):
                    for what, b, n in jobs.get(m, []):
                        if what == "qk":
                            dve.wait_ge(job_ready, turn_of[what, b, n] + 1)
                            if b >= 2:
                                dve.wait_ge(scores_ready, HEADS * (b - 2) + 2 * n + 2)
                            dve.wait_ge(job_saved, by_act[turn_of[what, b, n] + 1])
                            dve.tensor_scalar(k[:, b % 2, n, :], px[:, SEQ:], bk[:, n:n + 1], None, ALU.add).then_inc(k_saved, 1)
                    if m < ALL:
                        dve.wait_ge(scores_ready, m + 1)
                        dve.tensor_reduce(neg_max[:, m % 4, 0:1], ps[m % 3][:, 0:P], AX.X, ALU.max, negate=True).then_inc(max_ready, 1)
                        dve.tensor_reduce(neg_max[:, m % 4, 1:2], ps[m % 3][:, P:3 * P], AX.X, ALU.max, negate=True)\
                           .then_inc(max_ready, 1)
                    if 1 <= m <= ALL:
                        n = m - 1
                        dve.wait_ge(exp_ready, 2 * n + 2)
                        link(dve.reciprocal(total[:, n % 4, :], total[:, n % 4, :]))
                        row = prob[:, n % 3, :]
                        dve.tensor_scalar(row[:, 0:P], row[:, 0:P], total[:, n % 4, 0:1], None, ALU.mult).then_inc(prob_ready, 1)
                        dve.tensor_scalar(row[:, P:], row[:, P:], total[:, n % 4, 1:2], None, ALU.mult).then_inc(prob_ready, 1)
                    if 2 <= m < ALL + 2:
                        n = m - 2
                        dve.wait_ge(turn_ready, n + 1)
                        if n >= 2:
                            dve.wait_ge(z_ready, n - 1)
                        dve.tensor_copy(turned[:, n % 2, :], pt[n % 2][:, 0:3 * P]).then_inc(turned_saved, 1)
                    for what, b, n in jobs.get(m, []):
                        if what == "out":
                            dve.wait_ge(job_ready, turn_of[what, b, n] + 1)
                            dve.tensor_tensor(st.s[:, bass.ds(i * (2 * NB) + 2 * b, 2), :],
                                              px[:, 0:2 * P].rearrange("p (a b) -> p a b", a=2),
                                              bo[:, :].unsqueeze(1).to_broadcast([P, 2, D]), ALU.add).then_inc(k_saved, 1)


def layer3_ffn(nc, c, st, a):
    E = 6
    with ExitStack() as ctx:
        mem = Memory(nc, ctx)
        w1 = mem.sb("l3f_w1", [P, E + 1, P])
        w3 = mem.sb("l3f_w3", [P, E + 1, P])
        w2 = mem.sb("l3f_w2", [P, E + 1, D])
        gw = mem.sb("l3f_gw", [P, E])
        gb = mem.sb("l3f_gb", [P, E])
        w_tok = mem.sb("l3f_w_tok", [P, BLK, E + 1])
        load(nc, [(w1[:, 0:E, :], a["L3_ffn_ew1"]), (w3[:, 0:E, :], a["L3_ffn_ew3"]), (w2[:, 0:E, :], a["L3_ffn_ew2"]),
                  (w1[:, E, :], a["L3_ffn_fc1"]), (w3[:, E, :], a["L3_ffn_fc2"]), (w2[:, E, :], a["L3_ffn_fc3"]),
                  (gw[:, :], a["L3_ffn_gate_w"]), (gb[:, :], a["L3_ffn_gate_b"])])
        top_two(nc, c, st, "l3r", st.xnt, gw, gb, E, w_tok, softmax=False)
        with phase(nc, ["shared_weight"]) as (block, _, (shared_weight,)):
            @block.gpsimd
            def _(pool):
                pool.memset(w_tok[:, :, E:E + 1], 1.0).then_inc(shared_weight, 1)
                pool.wait_ge(shared_weight, 1)
        experts(nc, c, st, "l3e", st.xnt, w_tok, E + 1, 1, ACT.Silu, w1, w2, w3=w3)


def gated_stack(nc, a, out):
    with ExitStack() as ctx:
        mem = Memory(nc, ctx)
        c, st = Constants(mem), State(mem)
        constants(nc, c)
        load(nc, [(st.x[:, :, :], a["x"])])
        layers = ((layer0_attention, layer0_ffn), (layer1_attention, layer1_ffn), (layer2_attention, layer2_ffn),
                  (layer3_attention, layer3_ffn))
        for n, (mixer, ffn) in enumerate(layers):
            layer_norm(nc, c, f"norm{n}", st.x, st.xn, st.xnt, combined=st if n else None)
            mixer(nc, c, st, a)
            ffn(nc, c, st, a)
        finish(nc, st, out)



def heads_in(w):
    n, m, d = w.shape
    return w.transpose(1, 0, 2).reshape(m, n * d // 128, 128)
def rows(b, n=128):
    return np.broadcast_to(b, (n,) + b.shape)
def units_t(w):
    e, f, ch = w.shape
    return w.transpose(2, 0, 1).reshape(ch, e * f // 128, 128)
def units(w):
    e, ch, f = w.shape
    return w.transpose(1, 0, 2).reshape(ch, e * f // 128, 128)
def down(w):
    e, f, o = w.shape
    return w.reshape(e * f // 128, 128, o).transpose(1, 0, 2)
def layout(i):
    o = {}
    o["x"] = i["L0_attn_hidden_states"].reshape(32, 128, 128).transpose(1, 0, 2)
    for n in ("Q", "K"):
        o[f"L3_attn_W_{n}"] = heads_in(i[f"L3_attn_W_{n}"])
        o[f"L3_attn_b_{n}"] = i[f"L3_attn_b_{n}"].reshape(8, 128).T
    o["L3_attn_W_V"] = heads_in(i["L3_attn_W_V"]).reshape(128, 1024)
    o["L3_attn_b_V"] = i["L3_attn_b_V"].reshape(8, 128).T
    o["L3_attn_W_O"] = i["L3_attn_W_O"].reshape(8, 128, 128).transpose(1, 0, 2)
    o["L3_attn_b_O"] = rows(i["L3_attn_b_O"])
    o["L3_ffn_ew1"] = units_t(i["L3_ffn_ew1"])
    o["L3_ffn_ew3"] = units_t(i["L3_ffn_ew3"])
    o["L3_ffn_ew2"] = i["L3_ffn_ew2"].transpose(2, 0, 1)
    o["L3_ffn_fc1"] = i["L3_ffn_fc1"].T
    o["L3_ffn_fc2"] = i["L3_ffn_fc2"].T
    o["L3_ffn_fc3"] = i["L3_ffn_fc3"].T
    o["L3_ffn_gate_w"] = i["L3_ffn_gate_w"].T
    o["L3_ffn_gate_b"] = rows(i["L3_ffn_gate_b"])
    for n in ("Wq", "Wk", "Wv", "Wb", "Wmix", "Wo"):
        o[f"L0_attn_{n}"] = i[f"L0_attn_{n}"].T
    o["L0_attn_Wb_wide"] = np.repeat(i["L0_attn_Wb"].T, 32, axis=1)
    for n in ("q", "k", "v"):
        o[f"L0_attn_conv_{n}"] = i[f"L0_attn_conv_{n}"]
    o["L0_attn_norm_w"] = np.broadcast_to(i["L0_attn_norm_w"], (4, 32)).reshape(128, 1)
    for n in ("Wq", "Wk", "Wv"):
        o[f"L0_ffn_{n}"] = i[f"L0_ffn_{n}"].reshape(128, 16, 8)
    for n in ("bq", "bk", "bv"):
        o[f"L0_ffn_{n}"] = i[f"L0_ffn_{n}"].reshape(4, 4, 8).transpose(1, 2, 0)
    o["L0_ffn_Wo"] = i["L0_ffn_Wo"].reshape(4, 4, 8, 128).transpose(1, 2, 0, 3)
    for n in ("bo", "gb", "ln1_g", "ln1_b", "ln2_g", "ln2_b"):
        o[f"L0_ffn_{n}"] = rows(i[f"L0_ffn_{n}"])
    o["L0_ffn_W1"] = units(i["L0_ffn_W1"])
    o["L0_ffn_b1"] = i["L0_ffn_b1"].reshape(16, 128).T
    o["L0_ffn_W2"] = down(i["L0_ffn_W2"])
    o["L0_ffn_b2"], o["L0_ffn_gW"] = i["L0_ffn_b2"], i["L0_ffn_gW"]
    o["L1_attn_w_in"] = i["L1_attn_w_in"].reshape(128, 4, 128)
    o["L1_attn_conv_w"] = i["L1_attn_conv_w"].reshape(2, 128, 4).transpose(1, 0, 2)
    o["L1_attn_conv_b"] = i["L1_attn_conv_b"].reshape(2, 128).T
    o["L1_attn_w_B"] = i["L1_attn_w_B"].reshape(2, 128, 16).transpose(1, 0, 2)
    o["L1_attn_w_C"] = i["L1_attn_w_C"].reshape(16, 2, 128)
    o["L1_attn_w_out"] = i["L1_attn_w_out"].reshape(2, 128, 128).transpose(1, 0, 2)
    o["L1_ffn_W1"] = units_t(i["L1_ffn_W1"])
    o["L1_ffn_W3"] = units_t(i["L1_ffn_W3"])
    o["L1_ffn_W2"] = down(i["L1_ffn_W2"].transpose(0, 2, 1))
    o["L1_ffn_Wg"] = i["L1_ffn_Wg"].T
    o["L2_attn_w1"] = i["L2_attn_w1"]
    o["L2_attn_w2"] = i["L2_attn_w2"]
    o["L2_attn_v"] = i["L2_attn_v"]
    o["L2_ffn_centroids"] = i["L2_ffn_centroids"].T
    o["L2_ffn_ln_g"] = rows(i["L2_ffn_ln_g"])
    o["L2_ffn_ln_b"] = rows(i["L2_ffn_ln_b"])
    o["L2_ffn_w1"] = units(i["L2_ffn_w1"])
    o["L2_ffn_b1"] = i["L2_ffn_b1"].reshape(32, 128).T
    o["L2_ffn_w2"] = down(i["L2_ffn_w2"])
    o["L2_ffn_b2"] = i["L2_ffn_b2"]
    return o


def kernel(**inputs):
    import concourse.bacc as _bacc
    from concourse.bass_utils import run_bass_kernel_spmd as _run

    nc = _bacc.Bacc("TRN2", target_bir_lowering=False, num_devices=1)
    arrays, aps = {}, {}
    for name, array in layout({k: np.asarray(v) for k, v in inputs.items()}).items():
        array = np.ascontiguousarray(array)
        arrays[f"in_{name}_dram"] = array
        aps[name] = nc.dram_tensor(f"in_{name}_dram", array.shape, mybir.dt.from_np(array.dtype), kind="ExternalInput").ap()
    out = nc.dram_tensor("out_0_dram", (BATCH, SEQ, D), F32, kind="ExternalOutput").ap()
    gated_stack(nc, aps, out)
    r = _run(nc, [arrays], core_ids=[0])
    return r.results[0]["out_0_dram"]
```

```python
from contextlib import ExitStack, contextmanager

import concourse.bass as bass
import numpy as np
from concourse import mybir

F32 = mybir.dt.float32
BF16 = mybir.dt.bfloat16
I32 = mybir.dt.int32
ALU = mybir.AluOpType
ACT = mybir.ActivationFunctionType
AX = mybir.AxisListType

P = 128
D = 128
BATCH = 16
SEQ = 256
TOK = BATCH * SEQ
BLK = TOK // P
GB = 4
GT = GB * P
GRP = TOK // GT
LN_EPS = 1e-5


@contextmanager
def phase(nc, names, steps=1):
    with ExitStack() as ctx:
        sems = [ctx.enter_context(nc.semaphore(n)) for n in names]
        step = ctx.enter_context(nc.Fori(0, steps)) if steps > 1 else 0
        with nc.Block() as block:
            yield block, step, sems
        numbers = sorted(s.num for s in sems)
        while numbers:
            run = 1
            while run < len(numbers) and numbers[run] == numbers[0] + run:
                run += 1
            nc.sync.sem_clear(range(numbers[0], numbers[0] + run))
            numbers = numbers[run:]
        nc.all_engine_barrier()


class Chain:

    def __init__(self, engine, sem):
        self.engine, self.sem, self.count = engine, sem, 0

    def __call__(self, instruction):
        self.count += 1
        instruction.then_inc(self.sem, 1)
        self.engine.wait_ge(self.sem, self.count)


class Memory:

    def __init__(self, nc, ctx):
        self.nc, self.ctx = nc, ctx

    def sb(self, name, shape, dt=F32):
        return self.ctx.enter_context(self.nc.sbuf_tensor(name, shape, dt))

    def psum(self, name, shape, dt=F32):
        return self.ctx.enter_context(self.nc.psum_tensor(name, shape, dt))


def load(nc, pairs):
    with phase(nc, ["loaded_sp", "loaded_act"]) as (block, _, (loaded_sp, loaded_act)):
        @block.sync
        def _(sp):
            mine = pairs[0::2]
            for dst, src in mine:
                sp.dma_start(dst, src).then_inc(loaded_sp, 16)
            sp.wait_ge(loaded_sp, 16 * len(mine))

        @block.scalar
        def _(act):
            mine = pairs[1::2]
            for dst, src in mine:
                act.dma_start(dst, src).then_inc(loaded_act, 16)
            if mine:
                act.wait_ge(loaded_act, 16 * len(mine))


def constants(nc, c):
    with phase(nc, ["filled", "cut"]) as (block, _, (filled, cut)):
        @block.gpsimd
        def _(pool):
            pool.memset(c.ident[:, :], 0.0).then_inc(filled, 1)
            pool.memset(c.ones[:, :], 1.0).then_inc(filled, 1)
            pool.memset(c.minus_half[:, :], -0.5).then_inc(filled, 1)
            pool.memset(c.triu[:, :], 1.0).then_inc(filled, 1)
            pool.memset(c.ident_bf[:, :], 0.0).then_inc(filled, 1)
            pool.memset(c.future[:, :], 0.0).then_inc(filled, 1)
            pool.wait_ge(filled, 6)
            pool.affine_select(out=c.ident[:, :], in_=c.ident[:, :], compare_op=ALU.not_equal, fill=1.0,
                               base=0, pattern=[[-1, P]], channel_multiplier=1).then_inc(cut, 1)
            pool.affine_select(out=c.ident_bf[:, :], in_=c.ident_bf[:, :], compare_op=ALU.not_equal, fill=1.0,
                               base=0, pattern=[[-1, P]], channel_multiplier=1).then_inc(cut, 1)
            pool.affine_select(out=c.triu[:, :], in_=c.triu[:, :], compare_op=ALU.is_gt, fill=0.0,
                               base=0, pattern=[[1, P]], channel_multiplier=-1).then_inc(cut, 1)
            pool.affine_select(out=c.future[:, :], in_=c.future[:, :], compare_op=ALU.is_ge, fill=-1e5,
                               base=0, pattern=[[-1, P]], channel_multiplier=1).then_inc(cut, 1)
            pool.wait_ge(cut, 4)


class Constants:
    def __init__(self, mem):
        self.ident = mem.sb("ident", [P, P])
        self.ones = mem.sb("ones", [P, P])
        self.triu = mem.sb("triu", [P, P])
        self.minus_half = mem.sb("minus_half", [P, GB])
        self.ident_bf = mem.sb("ident_bf", [P, P], BF16)
        self.future = mem.sb("future", [P, P], BF16)


class State:

    def __init__(self, mem):
        self.x = mem.sb("x_tok", [P, BLK, D])
        self.xn = mem.sb("xn_tok", [P, BLK, D])
        self.xnt = mem.sb("xn_ch", [P, TOK])
        self.s = mem.sb("mixer_out", [P, BLK, D])
        self.g = mem.sb("ffn_out", [P, BLK, D])


GROUPS = 4


def combine_group(dve, st, gate, rows, last):
    last(dve.tensor_tensor(gate, gate, st.s[:, rows, :], ALU.mult))
    return dve.tensor_tensor(st.x[:, rows, :], st.x[:, rows, :], gate, ALU.add)


def finish(nc, st, out):
    out = out.rearrange("s (t p) d -> p (s t) d", p=P)
    with nc.sbuf_tensor("fin_gate", [P, 2, GB, D], F32) as gate, \
            phase(nc, ["fin_gate_ready", "fin_dve_step", "fin_combined", "fin_stored"], GRP // GROUPS) as (block, i, sems):
        gate_ready, dve_step, combined, stored = sems

        @block.scalar
        def _(act):
            for g in range(GROUPS):
                if g >= 2:
                    act.wait_ge(combined, g - 1)
                act.activation(gate[:, g % 2, :, :], st.g[:, bass.ds((i * GROUPS + g) * GB, GB), :], ACT.Silu)\
                   .then_inc(gate_ready, 1)

        @block.vector
        def _(dve):
            link = Chain(dve, dve_step)
            for g in range(GROUPS):
                dve.wait_ge(gate_ready, g + 1)
                combine_group(dve, st, gate[:, g % 2, :, :], bass.ds((i * GROUPS + g) * GB, GB), link).then_inc(combined, 1)

        @block.sync
        def _(sp):
            for g in range(GROUPS):
                rows = bass.ds((i * GROUPS + g) * GB, GB)
                sp.wait_ge(combined, g + 1)
                sp.dma_start(out[:, rows, :], st.x[:, rows, :]).then_inc(stored, 16)
            sp.wait_ge(stored, 16 * GROUPS)


def layer_norm(nc, c, name, src, dst, dst_ch=None, gain=None, shift=None, combined=None):
    with ExitStack() as ctx:
        mem = Memory(nc, ctx)
        gate = mem.sb(name + "_gate", [P, 2, GB, D]) if combined else None
        stats = mem.sb(name + "_stats", [P, 2, GB, 6])
        mv = mem.sb(name + "_mv", [P, 2, GB, 2])
        rstd = mem.sb(name + "_rstd", [P, 2, GB])
        norm = mem.sb(name + "_norm", [P, 2, GB, D])
        pt = [mem.psum(f"{name}_pt{n}", [P, GB, P]) for n in range(2)]
        names = ["gate_ready", "dve_step", "stats_ready", "pool_step", "rstd_ready", "norm_ready", "turned", "ch_saved",
                 "tok_saved"]
        with phase(nc, [name + "_" + n for n in names], GRP // GROUPS) as (block, i, sems):
            gate_ready, dve_step, stats_ready, pool_step, rstd_ready, norm_ready, turned, ch_saved, tok_saved = sems

            def rows(g):
                return bass.ds((i * GROUPS + g) * GB, GB)

            @block.vector
            def _(dve):
                link = Chain(dve, dve_step)

                def measure(g):
                    if combined:
                        dve.wait_ge(gate_ready, g + 1)
                        link(combine_group(dve, combined, gate[:, g % 2, :, :], rows(g), link))
                    for j in range(GB):
                        ins = dve.bn_stats(stats[:, g % 2, j, :], src[:, (i * GROUPS + g) * GB + j, :])
                    link(ins)
                    for j in range(GB):
                        ins = dve.bn_aggr(mv[:, g % 2, j, :], stats[:, g % 2, j, :])
                    ins.then_inc(stats_ready, 1)

                def normalize(g):
                    dve.wait_ge(rstd_ready, g + 1)
                    if g >= 2:
                        if dst is not None:
                            dve.wait_ge(tok_saved, g - 1)
                        if dst_ch is not None:
                            dve.wait_ge(turned, g - 1)
                    for j in range(GB):
                        ins = dve.tensor_scalar(norm[:, g % 2, j, :], src[:, (i * GROUPS + g) * GB + j, :],
                                                mv[:, g % 2, j, 0:1], rstd[:, g % 2, j:j + 1], ALU.subtract, ALU.mult)
                    if gain is not None:
                        link(ins)
                        y, spread = norm[:, g % 2, :, :], [P, GB, D]
                        link(dve.tensor_tensor(y, y, gain.unsqueeze(1).to_broadcast(spread), ALU.mult))
                        ins = dve.tensor_tensor(y, y, shift.unsqueeze(1).to_broadcast(spread), ALU.add)
                    ins.then_inc(norm_ready, 1)

                for g in range(GROUPS + 1):
                    if g < GROUPS:
                        measure(g)
                    if g >= 1:
                        normalize(g - 1)

            @block.gpsimd
            def _(pool):
                link = Chain(pool, pool_step)
                for g in range(GROUPS):
                    pool.wait_ge(stats_ready, g + 1)
                    if g >= 2:
                        pool.wait_ge(norm_ready, g - 1)
                    r = rstd[:, g % 2, :]
                    link(pool.tensor_scalar(r, mv[:, g % 2, :, 1], LN_EPS, None, ALU.add))
                    pool.tensor_tensor(r, r, c.minus_half[:, :], ALU.pow).then_inc(rstd_ready, 1)

            if dst_ch is not None:
                @block.tensor
                def _(pe):
                    for g in range(GROUPS):
                        pe.wait_ge(norm_ready, g + 1)
                        if g >= 2:
                            pe.wait_ge(ch_saved, g - 1)
                        for j in range(GB):
                            ins = pe.transpose(pt[g % 2][:, j, :], norm[:, g % 2, j, :], c.ident[:, :])
                        ins.then_inc(turned, 1)

            @block.scalar
            def _(act):
                for g in range(GROUPS + 1):
                    if combined and g < GROUPS:
                        if g >= 2:
                            act.wait_ge(stats_ready, g - 1)
                        act.activation(gate[:, g % 2, :, :], combined.g[:, rows(g), :], ACT.Silu).then_inc(gate_ready, 1)
                    if g >= 1:
                        if dst is not None:
                            act.wait_ge(norm_ready, g)
                            act.activation(dst[:, rows(g - 1), :], norm[:, (g - 1) % 2, :, :], ACT.Copy).then_inc(tok_saved, 1)
                        if dst_ch is not None:
                            act.wait_ge(turned, g)
                            act.activation(dst_ch[:, bass.ds((i * GROUPS + g - 1) * GT, GT)],
                                           pt[(g - 1) % 2][:, :, :].rearrange("p a b -> p (a b)"), ACT.Copy).then_inc(ch_saved, 1)


WAYS = 16
ROUNDS = 6
EXPONENT = 0x7F800000
GONE = 1e30


def token_scores(nc, name, src_ch, w, n_exp, score):
    with nc.psum_tensor(name + "_ps", [P, BLK, n_exp], F32) as ps, \
            phase(nc, [name + "_scores_ready"]) as (block, _, (scores_ready,)):
        @block.tensor
        def _(pe):
            for b in range(BLK):
                ins = pe.matmul(ps[:, b, :], src_ch[:, b * P:(b + 1) * P], w[:, :], start=True, stop=True)
            ins.then_inc(scores_ready, 1)

        @block.vector
        def _(dve):
            dve.wait_ge(scores_ready, 1)
            dve.tensor_copy(score[:, :, :], ps[:, :, :].rearrange("p b e -> p e b"))


def choose(nc, c, name, score, chosen, n_exp, count, in_turn=False):
    with ExitStack() as ctx:
        mem = Memory(nc, ctx)
        E = 1 if in_turn else n_exp
        T = WAYS - 1
        biggest = mem.sb(name + "_biggest", [P, 1])
        bound = mem.sb(name + "_bound", [P, 1])
        index = mem.sb(name + "_index", [P, T])
        width = mem.sb(name + "_width", [P, ROUNDS])
        offsets = mem.sb(name + "_offsets", [P, ROUNDS, T])
        low = mem.sb(name + "_low", [P, E])
        thr = mem.sb(name + "_thr", [P, E, T])
        reached = mem.sb(name + "_reached", [P, E, T, BLK])
        part = mem.sb(name + "_part", [P, E, T])
        over = mem.sb(name + "_over", [P, E, T])
        kept = mem.sb(name + "_kept", [P, E])
        tie = mem.sb(name + "_tie", [P, E, BLK])
        before = mem.sb(name + "_before", [P, E, BLK + 1])
        one = mem.sb(name + "_one", [P, BLK])
        need = mem.sb(name + "_need", [P, E])
        p_count = mem.psum(name + "_count", [P, E, T])
        p_before = mem.psum(name + "_p_before", [P, E, BLK])

        names = [name + "_" + n for n in ("dve_step", "set", "biggest_ready", "bound_ready")]
        with phase(nc, names) as (block, _, (dve_step, set_, biggest_ready, bound_ready)):
            @block.gpsimd
            def _(pool):
                pool.iota(index[:, :], pattern=[[1, T]], base=1, channel_multiplier=0, allow_small_or_imprecise_dtypes=True)\
                    .then_inc(set_, 1)
                pool.memset(one[:, :], 1.0).then_inc(set_, 1)
                pool.memset(before[:, :, :], 0.0).then_inc(set_, 1)
                pool.wait_ge(biggest_ready, 1)
                pool.partition_all_reduce(bound[:, :], biggest[:, :], P, bass.bass_isa.ReduceOp.max).then_inc(bound_ready, 1)

            @block.vector
            def _(dve):
                link = Chain(dve, dve_step)
                link(dve.tensor_reduce(biggest[:, :], score[:, :, :], AX.XY, ALU.max, apply_absolute_value=True))
                dve.tensor_scalar(biggest[:, :], biggest[:, :], 1e-30, None, ALU.max).then_inc(biggest_ready, 1)
                dve.wait_ge(bound_ready, 1)
                link(dve.tensor_scalar(bound[:, :].bitcast(I32), bound[:, :].bitcast(I32), EXPONENT, None, ALU.bitwise_and))
                link(dve.tensor_scalar(bound[:, :], bound[:, :], 2.0, None, ALU.mult))
                dve.wait_ge(set_, 3)
                for r in range(ROUNDS):
                    link(dve.tensor_scalar(width[:, r:r + 1], bound[:, :], 2.0 / WAYS ** (r + 1), None, ALU.mult))
                    link(dve.tensor_scalar(offsets[:, r, :], index[:, :], width[:, r:r + 1], None, ALU.mult))

        for turn in range(n_exp if in_turn else 1):
            s = score[:, turn:turn + 1, :] if in_turn else score[:, :, :]
            got = chosen[:, turn:turn + 1, :] if in_turn else chosen[:, :, :]
            wide = [P, E, T, BLK]
            names = [name + "_" + n for n in ("dve_step", "part_ready", "count_ready", "tie_ready", "before_ready")]
            with phase(nc, names) as (block, _, (dve_step, part_ready, count_ready, tie_ready, before_ready)):
                @block.tensor
                def _(pe):
                    for r in range(ROUNDS):
                        pe.wait_ge(part_ready, r + 1)
                        pe.matmul(p_count[:, :, :], c.ones[:, :], part[:, :, :], start=True, stop=True).then_inc(count_ready, 1)
                    pe.wait_ge(part_ready, ROUNDS + 1)
                    pe.matmul(p_count[:, :, 0], c.ones[:, :], part[:, :, 0], start=True, stop=True).then_inc(count_ready, 1)
                    pe.wait_ge(tie_ready, 1)
                    pe.matmul(p_before[:, :, :], c.ones[:, :], before[:, :, 0:BLK], start=True, stop=False)
                    pe.matmul(p_before[:, :, :], c.triu[:, :], tie[:, :, :], start=False, stop=True).then_inc(before_ready, 1)

                @block.vector
                def _(dve):
                    link = Chain(dve, dve_step)
                    link(dve.tensor_scalar(low[:, :], bound[:, 0:1].to_broadcast([P, E]), -1.0, None, ALU.mult))
                    for r in range(ROUNDS):
                        link(dve.tensor_tensor(thr[:, :, :], low[:, :].unsqueeze(2).to_broadcast([P, E, T]),
                                               offsets[:, r, :].unsqueeze(1).to_broadcast([P, E, T]), ALU.add))
                        link(dve.tensor_tensor(reached[:, :, :, :], s.unsqueeze(2).to_broadcast(wide),
                                               thr[:, :, :].unsqueeze(3).to_broadcast(wide), ALU.is_ge))
                        dve.tensor_reduce(part[:, :, :], reached[:, :, :, :], AX.X, ALU.add).then_inc(part_ready, 1)
                        dve.wait_ge(count_ready, r + 1)
                        link(dve.tensor_scalar(over[:, :, :], p_count[:, :, :], count - 0.5, None, ALU.is_ge))
                        link(dve.tensor_reduce(kept[:, :], over[:, :, :], AX.X, ALU.add))
                        link(dve.scalar_tensor_tensor(low[:, :], kept[:, :], width[:, r:r + 1], low[:, :], ALU.mult, ALU.add))
                    spread = [P, E, BLK]
                    link(dve.tensor_tensor(tie[:, :, :], s, low[:, :].unsqueeze(2).to_broadcast(spread), ALU.is_ge))
                    link(dve.tensor_scalar(low[:, :], low[:, :], width[:, ROUNDS - 1:ROUNDS], None, ALU.add))
                    link(dve.tensor_tensor(got, s, low[:, :].unsqueeze(2).to_broadcast(spread), ALU.is_ge))
                    dve.tensor_reduce(part[:, :, 0], got, AX.X, ALU.add).then_inc(part_ready, 1)
                    link(dve.tensor_tensor(tie[:, :, :], tie[:, :, :], got, ALU.subtract))
                    for e in range(E):
                        ins = dve.tensor_tensor_scan(before[:, e, 1:], one[:, :], tie[:, e, :], 0.0, ALU.mult, ALU.add)
                        if e < E - 1:
                            link(ins)
                    ins.then_inc(tie_ready, 1)
                    dve.wait_ge(count_ready, ROUNDS + 1)
                    link(dve.tensor_scalar(need[:, :], p_count[:, :, 0], -1.0, float(count), ALU.mult, ALU.add))
                    dve.wait_ge(before_ready, 1)
                    room = reached[:, :, 0, :]
                    link(dve.tensor_tensor(room, p_before[:, :, :], need[:, :].unsqueeze(2).to_broadcast(spread), ALU.is_lt))
                    link(dve.tensor_tensor(room, room, tie[:, :, :], ALU.mult))
                    link(dve.tensor_tensor(got, got, room, ALU.add))
                    if in_turn and turn < n_exp - 1:
                        later = [P, n_exp - turn - 1, BLK]
                        link(dve.tensor_scalar(room, got, -GONE, None, ALU.mult))
                        link(dve.tensor_tensor(score[:, turn + 1:, :], score[:, turn + 1:, :], room.to_broadcast(later), ALU.add))


def experts(nc, c, st, name, src_ch, w_tok, n_exp, chunks, func, w1, w2, b1=None, w3=None, b2=None, residual=None):
    gated = w3 is not None
    biased = b2 is not None
    G = 2
    NX = G * n_exp
    with ExitStack() as ctx:
        mem = Memory(nc, ctx)
        act_out = mem.sb(name + "_act", [P, 2, GT]) if gated else None
        hidden = mem.sb(name + "_hidden", [P, 2, chunks, GT])
        acc = mem.sb(name + "_acc", [P, G, GB, D])
        w_now = mem.sb(name + "_w", [P, G, GB, n_exp])
        ph1 = [mem.psum(f"{name}_ph1{k}", [P, GT]) for k in range(2)]
        ph3 = [mem.psum(f"{name}_ph3{k}", [P, GT]) for k in range(2)] if gated else None
        py = [mem.psum(f"{name}_py{k}", [P, GB, D]) for k in range(2)]
        if biased:
            wt = mem.sb(name + "_wt", [n_exp, G, GB, P])
            p_wt = mem.psum(name + "_p_wt", [n_exp, GB, P])
            p_bias = mem.psum(name + "_p_bias", [P, GB, D])
        names = ["h1_ready", "h3_ready", "act_ready", "hidden_ready", "y_ready", "added", "w_ready", "wt_ready", "wt_saved",
                 "bias_ready", "bias_added"]
        with phase(nc, [name + "_" + n for n in names], GRP // G) as (block, i, sems):
            (h1_ready, h3_ready, act_ready, hidden_ready, y_ready, added, w_ready, wt_ready, wt_saved, bias_ready,
             bias_added) = sems

            @block.tensor
            def _(pe):
                def up(u):
                    unit, g = u % (n_exp * chunks), u // (n_exp * chunks)
                    x = src_ch[:, bass.ds(i * (G * GT) + g * GT, GT)]
                    if u >= 2:
                        pe.wait_ge(hidden_ready, u - 1)
                    pe.matmul(ph1[u % 2][:, :], w1[:, unit, :], x, start=True, stop=True).then_inc(h1_ready, 1)
                    if gated:
                        pe.matmul(ph3[u % 2][:, :], w3[:, unit, :], x, start=True, stop=True).then_inc(h3_ready, 1)

                def down(x):
                    pe.wait_ge(hidden_ready, chunks * (x + 1))
                    if x >= 2:
                        pe.wait_ge(added, GB * (x - 1))
                    for j in range(GB):
                        for f in range(chunks):
                            ins = pe.matmul(py[x % 2][:, j, :], hidden[:, x % 2, f, j * P:(j + 1) * P],
                                            w2[:, (x % n_exp) * chunks + f, :], start=(f == 0), stop=(f == chunks - 1))
                    ins.then_inc(y_ready, 1)

                def turn_weights(g):
                    pe.wait_ge(w_ready, 1)
                    if g >= 1:
                        pe.wait_ge(wt_saved, g)
                    for j in range(GB):
                        ins = pe.transpose(p_wt[:, j, :], w_now[:, g, j, :], c.ident[:, :])
                    ins.then_inc(wt_ready, 1)

                def bias(g):
                    pe.wait_ge(wt_saved, g + 1)
                    if g >= 1:
                        pe.wait_ge(bias_added, g)
                    for j in range(GB):
                        ins = pe.matmul(p_bias[:, j, :], wt[:, g, j, :], b2[:, :], start=True, stop=True)
                    ins.then_inc(bias_ready, 1)

                for x in range(NX + 1):
                    if x < NX:
                        for f in range(chunks):
                            up(x * chunks + f)
                            if f == 0:
                                if biased and x % n_exp == 0:
                                    turn_weights(x // n_exp)
                                if biased and x % n_exp == 1:
                                    bias(x // n_exp)
                                if x >= 1:
                                    down(x - 1)
                    else:
                        down(x - 1)

            @block.scalar
            def _(act):
                for u in range(NX * chunks):
                    act.wait_ge(h1_ready, u + 1)
                    x, f = u // chunks, u % chunks
                    if gated:
                        if u >= 2:
                            act.wait_ge(hidden_ready, u - 1)
                        act.activation(act_out[:, u % 2, :], ph1[u % 2][:, :], func).then_inc(act_ready, 1)
                    else:
                        if f == 0 and x >= 2:
                            act.wait_ge(y_ready, x - 1)
                        unit = u % (n_exp * chunks)
                        act.activation(hidden[:, x % 2, f, :], ph1[u % 2][:, :], func, bias=b1[:, unit:unit + 1])\
                           .then_inc(hidden_ready, 1)
                    if biased and unit == 0:
                        g = x // n_exp
                        act.wait_ge(wt_ready, g + 1)
                        act.activation(wt[:, g, :, :], p_wt[:, :, :], ACT.Copy).then_inc(wt_saved, 1)

            @block.vector
            def _(dve):
                def add(x):
                    g, e = x // n_exp, x % n_exp
                    if biased and e == 0:
                        dve.wait_ge(bias_ready, g + 1)
                        dve.tensor_tensor(acc[:, g, :, :], p_bias[:, :, :], residual[:, bass.ds((i * G + g) * GB, GB), :], ALU.add)\
                           .then_inc(bias_added, 1)
                        dve.wait_ge(bias_added, g + 1)
                    dve.wait_ge(y_ready, x + 1)
                    for j in range(GB):
                        y, now = py[x % 2][:, j, :], acc[:, g, j, :]
                        out = now if e < n_exp - 1 else st.g[:, (i * G + g) * GB + j, :]
                        if e > 0:
                            dve.wait_ge(added, GB * (x - 1) + j + 1)
                        if e == 0 and not biased:
                            ins = dve.tensor_scalar(out, y, w_now[:, g, j, e:e + 1], None, ALU.mult)
                        else:
                            ins = dve.scalar_tensor_tensor(out, y, w_now[:, g, j, e:e + 1], now, ALU.mult, ALU.add)
                        ins.then_inc(added, 1)

                dve.tensor_copy(w_now[:, :, :, :].rearrange("p g b e -> p (g b) e"), w_tok[:, bass.ds(i * (G * GB), G * GB), :])\
                   .then_inc(w_ready, 1)
                dve.wait_ge(w_ready, 1)
                for x in range(NX + 1):
                    if gated and x < NX:
                        for f in range(chunks):
                            u = x * chunks + f
                            dve.wait_ge(act_ready, u + 1)
                            dve.wait_ge(h3_ready, u + 1)
                            if f == 0 and x >= 2:
                                dve.wait_ge(y_ready, x - 1)
                            dve.tensor_tensor(hidden[:, x % 2, f, :], ph3[u % 2][:, :], act_out[:, u % 2, :], ALU.mult)\
                               .then_inc(hidden_ready, 1)
                    if x >= 1:
                        add(x - 1)


def top_two(nc, c, st, name, src_ch, gate_w, gate_b, n_exp, w_tok, softmax):
    with ExitStack() as ctx:
        mem = Memory(nc, ctx)
        prob = mem.sb(name + "_prob", [P, BLK, n_exp])
        rank = mem.sb(name + "_rank", [P, BLK, n_exp])
        beats = mem.sb(name + "_beats", [P, BLK, n_exp])
        small = mem.sb(name + "_small", [P, BLK])
        pl = mem.psum(name + "_pl", [P, BLK, n_exp])
        wide = [P, BLK, n_exp]
        with phase(nc, [name + "_" + n for n in ("logits_ready", "dve_step", "shifted", "prob_ready")]) as (block, _, sems):
            logits_ready, dve_step, shifted, prob_ready = sems

            @block.tensor
            def _(pe):
                for b in range(BLK):
                    pe.matmul(pl[:, b, :], src_ch[:, b * P:(b + 1) * P], gate_w[:, :], start=True, stop=True)\
                      .then_inc(logits_ready, 1)

            @block.scalar
            def _(act):
                act.wait_ge(shifted, 1)
                act.activation(prob[:, :, :], prob[:, :, :], ACT.Exp if softmax else ACT.Sigmoid).then_inc(prob_ready, 1)

            @block.vector
            def _(dve):
                link = Chain(dve, dve_step)
                spread = small[:, :].unsqueeze(2).to_broadcast(wide)
                dve.wait_ge(logits_ready, BLK)
                ins = dve.tensor_tensor(prob[:, :, :], pl[:, :, :], gate_b[:, :].unsqueeze(1).to_broadcast(wide), ALU.add)
                if softmax:
                    link(ins)
                    link(dve.tensor_reduce(small[:, :], prob[:, :, :], AX.X, ALU.max))
                    ins = dve.tensor_tensor(prob[:, :, :], prob[:, :, :], spread, ALU.subtract)
                ins.then_inc(shifted, 1)
                dve.wait_ge(prob_ready, 1)
                if softmax:
                    link(dve.tensor_reduce(small[:, :], prob[:, :, :], AX.X, ALU.add))
                    link(dve.reciprocal(small[:, :], small[:, :]))
                    link(dve.tensor_tensor(prob[:, :, :], prob[:, :, :], spread, ALU.mult))
                link(dve.memset(rank[:, :, :], 0.0))
                for e in range(n_exp):
                    one = prob[:, :, e:e + 1]
                    if e + 1 < n_exp:
                        rest = [P, BLK, n_exp - e - 1]
                        link(dve.tensor_tensor(beats[:, :, e + 1:], one.to_broadcast(rest), prob[:, :, e + 1:], ALU.is_ge))
                        link(dve.tensor_tensor(rank[:, :, e + 1:], rank[:, :, e + 1:], beats[:, :, e + 1:], ALU.add))
                    if e:
                        rest = [P, BLK, e]
                        link(dve.tensor_tensor(beats[:, :, :e], one.to_broadcast(rest), prob[:, :, :e], ALU.is_gt))
                        link(dve.tensor_tensor(rank[:, :, :e], rank[:, :, :e], beats[:, :, :e], ALU.add))
                link(dve.tensor_scalar(rank[:, :, :], rank[:, :, :], 1.5, None, ALU.is_lt))
                out = w_tok[:, :, 0:n_exp]
                link(dve.tensor_tensor(out, prob[:, :, :], rank[:, :, :], ALU.mult))
                if not softmax:
                    link(dve.tensor_reduce(small[:, :], out, AX.X, ALU.add))
                    link(dve.tensor_scalar(small[:, :], small[:, :], 1e-8, None, ALU.add))
                    link(dve.reciprocal(small[:, :], small[:, :]))
                    link(dve.tensor_tensor(out, out, spread, ALU.mult))


CHUNK = 32
HEADS = 4
HD = 32
CPB = P // CHUNK
MATS = BLK * HEADS * CPB
NSEQ = GT // SEQ


def delta_masks(nc, m):
    with phase(nc, ["gd_zero", "gd_same", "gd_cut"]) as (block, _, (zero, same, cut)):
        @block.gpsimd
        def _(pool):
            for t in (m.same, m.minus_same, m.minus_strict, m.causal):
                pool.memset(t[:, :], 0.0).then_inc(zero, 1)
            pool.wait_ge(zero, 4)
            for t, value in ((m.same, 1.0), (m.minus_same, -1.0), (m.minus_strict, -1.0), (m.causal, 1.0)):
                for n in range(CPB):
                    part = slice(n * CHUNK, (n + 1) * CHUNK)
                    pool.memset(t[part, part], value).then_inc(same, 1)
            pool.wait_ge(same, 4 * CPB)
            pool.affine_select(out=m.minus_strict[:, :], in_=m.minus_strict[:, :], compare_op=ALU.is_gt, fill=0.0,
                               base=0, pattern=[[1, P]], channel_multiplier=-1).then_inc(cut, 1)
            pool.affine_select(out=m.causal[:, :], in_=m.causal[:, :], compare_op=ALU.is_ge, fill=0.0,
                               base=0, pattern=[[1, P]], channel_multiplier=-1).then_inc(cut, 1)
            pool.wait_ge(cut, 2)


class DeltaState:
    def __init__(self, nc, mem):
        self.same = mem.sb("gd_m_same", [P, P])
        self.minus_same = mem.sb("gd_m_minus_same", [P, P])
        self.minus_strict = mem.sb("gd_m_strict", [P, P])
        self.causal = mem.sb("gd_m_causal", [P, P])
        self.beta = mem.sb("gd_beta", [P, BLK, 2 * HEADS])
        self.q_ch = mem.sb("gd_q_ch", [P, TOK])
        self.k_ch = mem.sb("gd_k_ch", [P, TOK])
        self.k_tok = mem.sb("gd_k_tok", [P, BLK, D])
        self.v_tok = mem.sb("gd_v_tok", [P, BLK, D])
        self.tri = nc.dram_tensor("gd_tri", (MATS * CHUNK * CHUNK,), F32, kind="Internal").ap()


def gates(nc, st, m, w_b, w_gates):
    beta_ch = st.g[:, :, :].rearrange("p b d -> p (b d)")
    with ExitStack() as ctx:
        mem = Memory(nc, ctx)
        p_tok = mem.psum("gd_p_tok", [P, BLK, 2 * HEADS])
        p_ch = [mem.psum(f"gd_p_ch{n}", [P, GT]) for n in range(2)]
        with phase(nc, ["gd_tok_ready", "gd_ch_ready", "gd_ch_saved"]) as (block, _, (tok_ready, ch_ready, ch_saved)):
            @block.tensor
            def _(pe):
                for b in range(BLK):
                    ins = pe.matmul(p_tok[:, b, :], st.xnt[:, b * P:(b + 1) * P], w_gates[:, :], start=True, stop=True)
                ins.then_inc(tok_ready, 1)
                for g in range(GRP):
                    if g >= 2:
                        pe.wait_ge(ch_saved, g - 1)
                    pe.matmul(p_ch[g % 2][:, :], w_b[:, :], st.xnt[:, g * GT:(g + 1) * GT], start=True, stop=True)\
                      .then_inc(ch_ready, 1)

            @block.scalar
            def _(act):
                act.wait_ge(tok_ready, 1)
                act.activation(m.beta[:, :, :], p_tok[:, :, :], ACT.Sigmoid)
                for g in range(GRP):
                    act.wait_ge(ch_ready, g + 1)
                    act.activation(beta_ch[:, g * GT:(g + 1) * GT], p_ch[g % 2][:, :], ACT.Sigmoid).then_inc(ch_saved, 1)


def project(nc, c, st, m, w3, taps):
    TAPS = 4
    PAD = TAPS - 1
    beta_ch = st.g[:, :, :].rearrange("p b d -> p (b d)")
    with ExitStack() as ctx:
        mem = Memory(nc, ctx)
        padded = mem.sb("gp_padded", [P, 3, NSEQ, PAD + SEQ])
        y = mem.sb("gp_y", [P, 3, NSEQ, SEQ])
        square = mem.sb("gp_square", [P, 2, GT])
        kb = mem.sb("gp_kb", [P, GT])
        tri = mem.sb("gp_tri", [P, HEADS, GB, P])
        eps = mem.sb("gp_eps", [P, 1])
        bank = [mem.psum(f"gp_bank{n}", [P, 512]) for n in range(8)]
        flat = y[:, :, :, :].rearrange("p a b c -> p a (b c)")
        with phase(nc, ["gp_set"]) as (block, _, (set_,)):
            @block.gpsimd
            def _(pool):
                pool.memset(padded[:, :, :, :], 0.0).then_inc(set_, 1)
                pool.memset(eps[:, :], 1e-6).then_inc(set_, 1)
                pool.wait_ge(set_, 2)
        names = ["gp_" + n for n in ("in_ready", "x_saved", "dve_step", "conv_ready", "silu_ready", "square_ready", "sum_ready",
                                     "root_ready", "unit_ready", "kb_ready", "turn_ready", "v_saved", "tri_ready", "tri_masked",
                                     "tri_stored", "k_saved")]
        with phase(nc, names, GRP) as (block, i, sems):
            (in_ready, x_saved, dve_step, conv_ready, silu_ready, square_ready, sum_ready, root_ready, unit_ready, kb_ready,
             turn_ready, v_saved, tri_ready, tri_masked, tri_stored, k_saved) = sems
            tokens = bass.ds(i * GT, GT)

            @block.tensor
            def _(pe):
                for n in range(3):
                    pe.matmul(bank[n][:, :], w3[:, n, :], st.xnt[:, tokens], start=True, stop=True).then_inc(in_ready, 1)
                for n in range(2):
                    pe.wait_ge(square_ready, n + 1)
                    pe.matmul(bank[3 + n][:, :], m.same[:, :], square[:, n, :], start=True, stop=True).then_inc(sum_ready, 1)
                pe.wait_ge(silu_ready, 3)
                for j in range(GB):
                    ins = pe.transpose(bank[5][:, j * P:(j + 1) * P], flat[:, 2, j * P:(j + 1) * P], c.ident[:, :])
                ins.then_inc(turn_ready, 1)
                pe.wait_ge(unit_ready, 2)
                for j in range(GB):
                    ins = pe.transpose(bank[6][:, j * P:(j + 1) * P], flat[:, 1, j * P:(j + 1) * P], c.ident[:, :])
                ins.then_inc(turn_ready, 1)
                pe.wait_ge(kb_ready, 1)
                for h in range(HEADS):
                    rows = slice(h * HD, (h + 1) * HD)
                    for j in range(GB):
                        cols = slice(j * P, (j + 1) * P)
                        ins = pe.matmul(bank[h][:, cols], flat[rows, 1, cols], kb[rows, cols], start=True, stop=True)
                    ins.then_inc(tri_ready, 1)

            @block.scalar
            def _(act):
                for n in range(3):
                    act.wait_ge(in_ready, n + 1)
                    act.activation(padded[:, n, :, PAD:], bank[n][:, :].rearrange("p (a b) -> p a b", a=NSEQ), ACT.Copy)\
                       .then_inc(x_saved, 1)
                for n in range(3):
                    act.wait_ge(conv_ready, n + 1)
                    act.activation(y[:, n, :, :], y[:, n, :, :], ACT.Silu).then_inc(silu_ready, 1)
                for n in range(2):
                    act.wait_ge(silu_ready, n + 1)
                    act.activation(square[:, n, :], flat[:, n, :], ACT.Square).then_inc(square_ready, 1)
                act.wait_ge(turn_ready, 1)
                act.activation(m.v_tok[:, bass.ds(i * GB, GB), :], bank[5][:, :].rearrange("p (a b) -> p a b", a=GB), ACT.Copy)\
                   .then_inc(v_saved, 1)
                for n in range(2):
                    act.wait_ge(sum_ready, n + 1)
                    act.activation(square[:, n, :], bank[3 + n][:, :], ACT.Sqrt, bias=eps[:, 0:1]).then_inc(root_ready, 1)
                act.wait_ge(turn_ready, 2)
                act.activation(m.k_tok[:, bass.ds(i * GB, GB), :], bank[6][:, :].rearrange("p (a b) -> p a b", a=GB), ACT.Copy)\
                   .then_inc(k_saved, 1)

            @block.vector
            def _(dve):
                link = Chain(dve, dve_step)
                for n in range(3):
                    dve.wait_ge(x_saved, n + 1)
                    out = y[:, n, :, :]
                    for k in range(TAPS):
                        x = padded[:, n, :, k:k + SEQ]
                        if k == 0:
                            link(dve.tensor_scalar(out, x, taps[:, n, k:k + 1], None, ALU.mult))
                        else:
                            ins = dve.scalar_tensor_tensor(out, x, taps[:, n, k:k + 1], out, ALU.mult, ALU.add)
                            if k < TAPS - 1:
                                link(ins)
                    ins.then_inc(conv_ready, 1)
                for n in range(2):
                    dve.wait_ge(root_ready, n + 1)
                    link(dve.reciprocal(square[:, n, :], square[:, n, :]))
                    dve.tensor_tensor(flat[:, n, :], flat[:, n, :], square[:, n, :], ALU.mult).then_inc(unit_ready, 1)
                dve.wait_ge(unit_ready, 2)
                dve.tensor_tensor(kb[:, :], flat[:, 1, :], beta_ch[:, tokens], ALU.mult).then_inc(kb_ready, 1)
                for h in range(HEADS):
                    dve.wait_ge(tri_ready, h + 1)
                    dve.tensor_tensor(tri[:, h, :, :], bank[h][:, :].rearrange("p (a b) -> p a b", a=GB),
                                      m.minus_strict[:, :].unsqueeze(1).to_broadcast([P, GB, P]), ALU.mult).then_inc(tri_masked, 1)

            @block.gpsimd
            def _(pool):
                pool.wait_ge(unit_ready, 2)
                pool.tensor_copy(m.q_ch[:, tokens], flat[:, 0, :])
                pool.tensor_copy(m.k_ch[:, tokens], flat[:, 1, :])

            @block.sync
            def _(sp):
                sp.wait_ge(tri_masked, HEADS)
                size = GB * HEADS * CPB * CHUNK * CHUNK
                mats = m.tri[bass.ds(i * size, size)].rearrange("(m n j i) -> n j m i", n=CPB, j=CHUNK, i=CHUNK)
                for n in range(CPB):
                    part = slice(n * CHUNK, (n + 1) * CHUNK)
                    sp.dma_start(mats[n, :, :, :], tri[part, :, :, part].rearrange("p h b i -> p (h b) i")).then_inc(tri_stored, 16)
                sp.wait_ge(tri_stored, 16 * CPB)


def invert(nc, m):
    LM = MATS // P
    with ExitStack() as ctx:
        mem = Memory(nc, ctx)
        at = mem.sb("gi_at", [P, LM, CHUNK, CHUNK])
        prod = mem.sb("gi_prod", [P, LM, CHUNK * CHUNK])
        upd = mem.sb("gi_upd", [P, LM, CHUNK])
        lanes = m.tri.rearrange("(p n) -> p n", p=P)
        flat = at[:, :, :, :].rearrange("p a b c -> p (a b c)")
        with phase(nc, ["gi_loaded", "gi_dve_step", "gi_inverted", "gi_stored"]) as (block, _, sems):
            loaded, dve_step, inverted, stored = sems

            @block.sync
            def _(sp):
                sp.dma_start(flat, lanes).then_inc(loaded, 16)
                sp.wait_ge(inverted, 1)
                sp.dma_start(lanes, flat).then_inc(stored, 16)
                sp.wait_ge(stored, 16)

            @block.vector
            def _(dve):
                link = Chain(dve, dve_step)
                dve.wait_ge(loaded, 16)
                for i in range(2, CHUNK):
                    full = [P, LM, i, i]
                    terms = prod[:, :, 0:i * i].rearrange("p a (k j) -> p a k j", k=i)
                    link(dve.tensor_tensor(terms, at[:, :, 0:i, 0:i], at[:, :, 0:i, i].unsqueeze(2).to_broadcast(full), ALU.mult))
                    link(dve.tensor_reduce(upd[:, :, 0:i], terms, AX.X, ALU.add))
                    link(dve.tensor_tensor(at[:, :, 0:i, i], at[:, :, 0:i, i], upd[:, :, 0:i], ALU.add))
                diag = at[:, :, :, :].rearrange("p a b c -> p a (b c)")[:, :, 0:CHUNK * CHUNK:CHUNK + 1]
                dve.tensor_scalar(diag, diag, 1.0, None, ALU.add).then_inc(inverted, 1)


def recur(nc, c, st, m, w_o, norm_w):
    with ExitStack() as ctx:
        mem = Memory(nc, ctx)
        inv = mem.sb("gr_inv", [P, HEADS, GB, P])
        q = mem.sb("gr_q", [P, GT])
        k = mem.sb("gr_k", [P, GT])
        k_tok = mem.sb("gr_k_tok", [P, GB, D])
        vk = mem.sb("gr_vk", [P, GB, HEADS, 2 * HD])
        u = mem.sb("gr_u", [P, GB, D])
        w = mem.sb("gr_w", [P, GB, D])
        attn = mem.sb("gr_attn", [P, HEADS, GB, P])
        kv = mem.sb("gr_kv", [P, CPB, GB, P])
        trans = mem.sb("gr_trans", [P, CPB, GB, P])
        q_eff = mem.sb("gr_q_eff", [P, GB, P])
        state = mem.sb("gr_state", [P, 2, NSEQ, P])
        o_ch = mem.sb("gr_o_ch", [P, GB, P])
        o = u
        square = vk[:, 0:2, :, :].rearrange("p b h x -> p (b h x)").rearrange("p (a x) -> p a x", x=HD)
        power = mem.sb("gr_power", [P, GB * HEADS])
        half = mem.sb("gr_half", [P, GB * HEADS])
        bank = [mem.psum(f"gr_bank{n}", [P, 4, P]) for n in range(8)]
        with phase(nc, ["gr_set"]) as (block, _, (set_,)):
            @block.gpsimd
            def _(pool):
                pool.memset(inv[:, :, :, :], 0.0).then_inc(set_, 1)
                pool.memset(half[:, :], -0.5).then_inc(set_, 1)
                pool.wait_ge(set_, 2)
        names = ["gr_" + n for n in ("inv_loaded", "qk_loaded", "toqk_loaded", "vk_ready", "uw_ready", "u_saved", "w_saved",
                                     "attn_ready", "attn_masked", "kv_ready", "kv_masked", "wk_ready", "wk_masked", "trans_ready",
                                     "qw_ready", "intra_ready", "q_eff_ready", "s_ready", "s_saved", "o_ready", "o_saved",
                                     "o_turned", "dve_step", "mixed", "squared", "power_sum", "pool_step", "power_ready",
                                     "normed", "n_turned", "n_saved", "out_ready")]
        with phase(nc, names, GRP) as (block, i, sems):
            (inv_loaded, qk_loaded, toqk_loaded, vk_ready, uw_ready, u_saved, w_saved, attn_ready, attn_masked, kv_ready,
             kv_masked, wk_ready, wk_masked, trans_ready, qw_ready, intra_ready, q_eff_ready, s_ready, s_saved, o_ready,
             o_saved, o_turned, dve_step, mixed, squared, power_sum, pool_step, power_ready, normed, n_turned, n_saved,
             out_ready) = sems
            tokens, rows = bass.ds(i * GT, GT), bass.ds(i * GB, GB)
            CH = SEQ // CHUNK

            @block.sync
            def _(sp):
                sp.dma_start(q[:, :], m.q_ch[:, tokens]).then_inc(qk_loaded, 16)
                sp.dma_start(k[:, :], m.k_ch[:, tokens]).then_inc(qk_loaded, 16)
                size = GB * HEADS * CPB * CHUNK * CHUNK
                mats = m.tri[bass.ds(i * size, size)].rearrange("(m n j i) -> n j m i", n=CPB, j=CHUNK, i=CHUNK)
                for n in range(CPB):
                    part = slice(n * CHUNK, (n + 1) * CHUNK)
                    sp.dma_start(inv[part, :, :, part].rearrange("p h b i -> p (h b) i"), mats[n, :, :, :]).then_inc(inv_loaded, 16)
                sp.dma_start(k_tok[:, :, :], m.k_tok[:, rows, :]).then_inc(toqk_loaded, 16)

            @block.scalar
            def _(act):
                for t in range(2):
                    act.wait_ge(uw_ready, t + 1)
                    src = bank[4 + t][:, :, :].rearrange("p a b -> p (a b)").rearrange("p (b h x) -> p b h x", b=2, h=HEADS)
                    for dst, part, sem in ((u, slice(0, HD), u_saved), (w, slice(HD, 2 * HD), w_saved)):
                        act.activation(dst[:, 2 * t:2 * t + 2, :].rearrange("p b (h x) -> p b h x", h=HEADS),
                                       src[:, :, :, part], ACT.Copy).then_inc(sem, 1)
                act.wait_ge(o_ready, 1)
                act.activation(o_ch[:, :, :], bank[1][:, :, :], ACT.Copy).then_inc(o_saved, 1)
                act.wait_ge(mixed, 1)
                act.activation(square, o[:, :, :].rearrange("p b (h x) -> p (b h) x", h=HEADS), ACT.Square)\
                   .then_inc(squared, 1)
                act.wait_ge(n_turned, 1)
                act.activation(o_ch[:, :, :], bank[5][:, :, :], ACT.Copy, scale=norm_w[:, 0:1]).then_inc(n_saved, 1)
                act.wait_ge(out_ready, 1)
                act.activation(st.s[:, rows, :], bank[6][:, :, :], ACT.Copy)

            @block.tensor
            def _(pe):
                pe.wait_ge(qk_loaded, 32)
                for h in range(HEADS):
                    part = slice(h * HD, (h + 1) * HD)
                    for b in range(GB):
                        cols = slice(b * P, (b + 1) * P)
                        ins = pe.matmul(bank[h][:, b, :], k[part, cols], q[part, cols], start=True, stop=True)
                    ins.then_inc(attn_ready, 1)
                pe.wait_ge(vk_ready, 2)
                pe.wait_ge(inv_loaded, 16 * CPB)
                for b in range(GB):
                    out = bank[4 + b // 2][:, :, :].rearrange("p a b -> p (a b)").rearrange("p (b h x) -> p b h x", b=2, h=HEADS)
                    for h in range(HEADS):
                        ins = pe.matmul(out[:, b % 2, h, :], inv[:, h, b, :], vk[:, b, h, :], start=True, stop=True)
                    if b % 2:
                        ins.then_inc(uw_ready, 1)
                pe.wait_ge(toqk_loaded, 16)
                pe.wait_ge(u_saved, 2)
                for n in range(CPB):
                    part = slice(n * CHUNK, (n + 1) * CHUNK)
                    pe.wait_ge(attn_masked, n + 1)
                    for b in range(GB):
                        ins = pe.matmul(bank[n][:, b, :], k_tok[part, b, :], u[part, b, :], start=True, stop=True)
                    ins.then_inc(kv_ready, 1)
                pe.wait_ge(w_saved, 2)
                for n in range(CPB):
                    part = slice(n * CHUNK, (n + 1) * CHUNK)
                    for b in range(GB):
                        ins = pe.matmul(bank[4 + n][:, b, :], w[part, b, :], k_tok[part, b, :], start=True, stop=True)
                    ins.then_inc(wk_ready, 1)
                for src, n, sem in ((w, 0, qw_ready), (u, 1, intra_ready)):
                    pe.wait_ge(kv_masked, n + 1)
                    for b in range(GB):
                        for h in range(HEADS):
                            part = slice(h * HD, (h + 1) * HD)
                            ins = pe.matmul(bank[n][part, b, :], src[:, b, part], attn[:, h, b, :], start=(b == 0),
                                            stop=(n == 0), skip_group_check=True)
                    ins.then_inc(sem, 1)
                pe.wait_ge(q_eff_ready, 1)
                pe.wait_ge(trans_ready, CPB)
                pe.wait_ge(kv_masked, CPB)
                for t in range(1, CH):
                    for s in range(NSEQ):
                        if t > 1:
                            pe.wait_ge(s_saved, NSEQ * (t - 2) + s + 1)
                        b, n = 2 * s + t // CPB, t % CPB
                        now = kv[:, 0, 2 * s, :] if t == 1 else state[:, t % 2, s, :]
                        if t < CH - 1:
                            pe.matmul(bank[2 + s][:, 0, :], trans[:, n, b, :], now, start=True, stop=True).then_inc(s_ready, 1)
                        cols = slice(n * CHUNK, (n + 1) * CHUNK)
                        ins = pe.matmul(bank[1][:, b, cols], now, q_eff[:, b, cols], start=False, stop=True,
                                        skip_group_check=True)
                ins.then_inc(o_ready, 1)
                pe.wait_ge(o_saved, 1)
                pe.wait_ge(wk_masked, CPB)
                for b in range(GB):
                    ins = pe.transpose(bank[4][:, b, :], o_ch[:, b, :], c.ident[:, :])
                ins.then_inc(o_turned, 1)
                pe.wait_ge(normed, 1)
                for b in range(GB):
                    ins = pe.transpose(bank[5][:, b, :], o[:, b, :], c.ident[:, :])
                ins.then_inc(n_turned, 1)
                pe.wait_ge(n_saved, 1)
                for b in range(GB):
                    ins = pe.matmul(bank[6][:, b, :], o_ch[:, b, :], w_o[:, :], start=True, stop=True)
                ins.then_inc(out_ready, 1)

            @block.vector
            def _(dve):
                link = Chain(dve, dve_step)
                wide = [P, GB, HEADS, HD]
                by_head = lambda t: t.rearrange("p b (h x) -> p b h x", h=HEADS)
                beta, v_tok = m.beta[:, rows, :], m.v_tok[:, rows, :]
                for n, src in enumerate((v_tok, m.k_tok[:, rows, :])):
                    dve.tensor_tensor(vk[:, :, :, n * HD:(n + 1) * HD], by_head(src),
                                      beta[:, :, 0:HEADS].unsqueeze(3).to_broadcast(wide), ALU.mult).then_inc(vk_ready, 1)
                spread = [P, GB, P]
                for h in range(HEADS):
                    dve.wait_ge(attn_ready, h + 1)
                    dve.tensor_tensor(attn[:, h, :, :], bank[h][:, :, :], m.causal[:, :].unsqueeze(1).to_broadcast(spread), ALU.mult)\
                       .then_inc(attn_masked, 1)
                for n in range(CPB):
                    dve.wait_ge(kv_ready, n + 1)
                    dve.tensor_tensor(kv[:, n, :, :], bank[n][:, :, :], m.same[:, :].unsqueeze(1).to_broadcast(spread), ALU.mult)\
                       .then_inc(kv_masked, 1)
                for n in range(CPB):
                    dve.wait_ge(wk_ready, n + 1)
                    dve.tensor_tensor(trans[:, n, :, :], bank[4 + n][:, :, :], m.minus_same[:, :].unsqueeze(1).to_broadcast(spread),
                                      ALU.mult).then_inc(wk_masked, 1)
                dve.wait_ge(qw_ready, 1)
                dve.tensor_tensor(q_eff[:, :, :], m.q_ch[:, tokens].rearrange("p (a b) -> p a b", a=GB), bank[0][:, :, :], ALU.subtract)\
                   .then_inc(q_eff_ready, 1)
                for t in range(1, CH - 1):
                    for s in range(NSEQ):
                        b, n = 2 * s + t // CPB, t % CPB
                        dve.wait_ge(s_ready, NSEQ * (t - 1) + s + 1)
                        dve.tensor_tensor(state[:, (t + 1) % 2, s, :], bank[2 + s][:, 0, :], kv[:, n, b, :], ALU.add)\
                           .then_inc(s_saved, 1)
                dve.wait_ge(o_turned, 1)
                link(dve.tensor_tensor(o[:, :, :], bank[4][:, :, :], v_tok, ALU.subtract))
                link(dve.tensor_tensor(by_head(o[:, :, :]), by_head(o[:, :, :]), beta[:, :, HEADS:].unsqueeze(3).to_broadcast(wide), ALU.mult))
                dve.tensor_tensor(o[:, :, :], o[:, :, :], v_tok, ALU.add).then_inc(mixed, 1)
                dve.wait_ge(squared, 1)
                dve.tensor_reduce(power[:, :], square, AX.X, ALU.add).then_inc(power_sum, 1)
                dve.wait_ge(power_ready, 1)
                heads = o[:, :, :].rearrange("p b (h x) -> p (b h) x", h=HEADS)
                dve.tensor_tensor(heads, heads, power[:, :].unsqueeze(2).to_broadcast([P, GB * HEADS, HD]), ALU.mult)\
                   .then_inc(normed, 1)

            @block.gpsimd
            def _(pool):
                link = Chain(pool, pool_step)
                for n in range(CPB):
                    pool.wait_ge(wk_masked, n + 1)
                    pool.tensor_tensor(trans[:, n, :, :], trans[:, n, :, :], c.ident[:, :].unsqueeze(1).to_broadcast([P, GB, P]),
                                       ALU.add).then_inc(trans_ready, 1)
                pool.wait_ge(power_sum, 1)
                link(pool.tensor_scalar(power[:, :], power[:, :], 1.0 / HD, LN_EPS, ALU.mult, ALU.add))
                pool.tensor_tensor(power[:, :], power[:, :], half[:, :], ALU.pow).then_inc(power_ready, 1)


def layer0_attention(nc, c, st, a):
    with ExitStack() as ctx:
        mem = Memory(nc, ctx)
        w3 = mem.sb("l0_w_qkv", [P, 3, P])
        taps = mem.sb("l0_taps", [P, 3, 4])
        w_b = mem.sb("l0_w_beta", [P, P])
        w_gates = mem.sb("l0_w_gates", [P, 2 * HEADS])
        w_o = mem.sb("l0_w_o", [P, D])
        norm_w = mem.sb("l0_norm_w", [P, 1])
        m = DeltaState(nc, mem)
        load(nc, [(w3[:, 0, :], a["L0_attn_Wq"]), (w3[:, 1, :], a["L0_attn_Wk"]), (w3[:, 2, :], a["L0_attn_Wv"]),
                  (taps[:, 0, :], a["L0_attn_conv_q"]), (taps[:, 1, :], a["L0_attn_conv_k"]), (taps[:, 2, :], a["L0_attn_conv_v"]),
                  (w_b[:, :], a["L0_attn_Wb_wide"]), (w_gates[:, 0:HEADS], a["L0_attn_Wb"]), (w_gates[:, HEADS:], a["L0_attn_Wmix"]),
                  (w_o[:, :], a["L0_attn_Wo"]), (norm_w[:, :], a["L0_attn_norm_w"])])
        delta_masks(nc, m)
        gates(nc, st, m, w_b, w_gates)
        project(nc, c, st, m, w3, taps)
        invert(nc, m)
        recur(nc, c, st, m, w_o, norm_w)


def attention16(nc, c, st, a):
    HEADS, HD, QUAD = 16, 8, 32
    Q = HEADS // 4
    SCALE = HD ** -0.5
    NB = 4
    ALL = NB * HEADS
    PLAN = [("qk", n, 4 * n - 4) for n in range(Q)] + [("v", 0, -3), ("v", 1, -1), ("out", 0, HEADS + 5)]
    jobs = {}
    for b in range(NB):
        for what, n, at in PLAN:
            jobs.setdefault(max(b * HEADS + at, 0), []).append((what, b, n))
    last = max(jobs) + 1
    order = [job for t in sorted(jobs) for job in jobs[t]]
    turn_of = {job: n for n, job in enumerate(order)}
    by_act = [sum(j[0] != "out" for j in order[:n]) for n in range(len(order) + 1)]
    by_dve = [n - m for n, m in enumerate(by_act)]
    with ExitStack() as ctx:
        mem = Memory(nc, ctx)
        wq = mem.sb("l0a_wq", [P, HEADS, QUAD])
        wk = mem.sb("l0a_wk", [P, HEADS, QUAD])
        wv = mem.sb("l0a_wv", [P, HEADS, QUAD])
        wo = mem.sb("l0a_wo", [P, Q, D])
        bq = mem.sb("l0a_bq", [P, Q])
        bk = mem.sb("l0a_bk", [P, Q])
        bv = mem.sb("l0a_bv", [P, Q])
        bo = mem.sb("l0a_bo", [P, D])
        with phase(nc, ["l0a_clear"]) as (block, _, (clear,)):
            @block.gpsimd
            def _(pool):
                for t in (wq, wk, wv, wo):
                    pool.memset(t[:, :, :], 0.0).then_inc(clear, 1)
                for t in (bq, bk, bv):
                    pool.memset(t[:, :], 0.0).then_inc(clear, 1)
                pool.wait_ge(clear, 7)
        pairs = [(wq[:, :, 0:HD], a["L0_ffn_Wq"]), (wk[:, :, 0:HD], a["L0_ffn_Wk"]), (wv[:, :, 0:HD], a["L0_ffn_Wv"]),
                 (bo[:, :], a["L0_ffn_bo"])]
        for s in range(4):
            rows = slice(QUAD * s, QUAD * s + HD)
            pairs += [(bq[rows, :], a["L0_ffn_bq"][s]), (bk[rows, :], a["L0_ffn_bk"][s]), (bv[rows, :], a["L0_ffn_bv"][s]),
                      (wo[rows, :, :], a["L0_ffn_Wo"][s])]
        load(nc, pairs)
        with phase(nc, ["l0a_scaled"]) as (block, _, (scaled,)):
            @block.vector
            def _(dve):
                dve.tensor_scalar(bq[:, :], bq[:, :], SCALE, None, ALU.mult).then_inc(scaled, 1)
        xs = mem.sb("l0a_x", [P, 2, SEQ])
        q = mem.sb("l0a_q", [P, 2, Q, SEQ])
        k = mem.sb("l0a_k", [P, 2, Q, SEQ])
        v = mem.sb("l0a_v", [P, 2, 2, HEADS * QUAD])
        prob = mem.sb("l0a_prob", [P, 3, 2, SEQ])
        turned = mem.sb("l0a_prob_t", [P, 2, 2, SEQ])
        neg_max = mem.sb("l0a_neg_max", [P, 4, 2])
        total = mem.sb("l0a_total", [P, 4, 2])
        z = mem.sb("l0a_z", [P, 2, Q, SEQ])
        ps = [mem.psum(f"l0a_ps{n}", [P, 2, SEQ]) for n in range(3)]
        pt = [mem.psum(f"l0a_pt{n}", [P, 2, SEQ]) for n in range(2)]
        pz = [mem.psum(f"l0a_pz{n}", [P, SEQ]) for n in range(2)]
        px = mem.psum("l0a_px", [P, 512])
        names = ["l0a_" + n for n in ("x_ready", "job_ready", "job_saved", "out_saved", "scores_ready", "max_ready", "exp_ready",
                                      "dve_step", "prob_ready", "turn_ready", "turned_saved", "z_ready", "z_saved")]
        with phase(nc, names, BATCH // NB) as (block, i, sems):
            (x_ready, job_ready, job_saved, out_saved, scores_ready, max_ready, exp_ready, dve_step, prob_ready, turn_ready,
             turned_saved, z_ready, z_saved) = sems

            @block.gpsimd
            def _(pool):
                for b in range(NB):
                    if b >= 2:
                        pool.wait_ge(job_ready, turn_of["qk", b - 2, Q - 1] + 1)
                    pool.tensor_copy(xs[:, b % 2, :], st.xnt[:, bass.ds(i * (NB * SEQ) + b * SEQ, SEQ)]).then_inc(x_ready, 1)

            @block.tensor
            def _(pe):
                def job(what, b, n):
                    m = turn_of[what, b, n]
                    if by_act[m]:
                        pe.wait_ge(job_saved, by_act[m])
                    if by_dve[m]:
                        pe.wait_ge(out_saved, by_dve[m])
                    if what == "out":
                        pe.wait_ge(z_saved, Q * (b + 1))
                        for t in range(2):
                            for g in range(Q):
                                ins = pe.matmul(px[:, t * P:(t + 1) * P], z[:, b % 2, g, t * P:(t + 1) * P], wo[:, g, :],
                                                start=(g == 0), stop=(g == Q - 1))
                    else:
                        pe.wait_ge(x_ready, b + 1)
                        x = xs[:, b % 2, :]
                    if what == "qk":
                        pe.matmul(px[:, 0:SEQ], wq[:, 4 * n:4 * n + 4, :], x, start=True, stop=True)
                        ins = pe.matmul(px[:, SEQ:], wk[:, 4 * n:4 * n + 4, :], x, start=True, stop=True)
                    if what == "v":
                        ins = pe.matmul(px[:, :], x[:, n * P:(n + 1) * P], wv[:, :, :], start=True, stop=True)
                    ins.then_inc(job_ready, 1)

                def scores(m):
                    b, h = m // HEADS, m % HEADS
                    if h % 4 == 0:
                        pe.wait_ge(job_saved, by_act[turn_of["qk", b, h // 4] + 1])
                    if m >= 3:
                        pe.wait_ge(exp_ready, 2 * (m - 2))
                    rows = slice(QUAD * (h % 4), QUAD * (h % 4) + QUAD)
                    for t in range(2):
                        ins = pe.matmul(ps[m % 3][:, t, :], q[rows, b % 2, h // 4, t * P:(t + 1) * P], k[rows, b % 2, h // 4, :],
                                        start=True, stop=True)
                    ins.then_inc(scores_ready, 1)

                def turn(m):
                    pe.wait_ge(prob_ready, 2 * m + 2)
                    if m >= 2:
                        pe.wait_ge(turned_saved, m - 1)
                    for t in range(2):
                        for s in range(2):
                            ins = pe.transpose(pt[m % 2][:, s, t * P:(t + 1) * P], prob[:, m % 3, t, s * P:(s + 1) * P],
                                               c.ident[:, :])
                    ins.then_inc(turn_ready, 1)

                def weigh(m):
                    b, h = m // HEADS, m % HEADS
                    g = m // 4
                    if h == 0:
                        pe.wait_ge(job_saved, by_act[turn_of["v", b, 1] + 1])
                    if h % 4 == 0 and g >= 2:
                        pe.wait_ge(z_saved, g - 1)
                    pe.wait_ge(turned_saved, m + 1)
                    rows = slice(QUAD * (h % 4), QUAD * (h % 4) + QUAD)
                    for s in range(2):
                        ins = pe.matmul(pz[g % 2][rows, :], v[:, b % 2, s, h * QUAD:(h + 1) * QUAD], turned[:, m % 2, s, :],
                                        start=(s == 0), stop=(s == 1))
                    ins.then_inc(z_ready, 1)

                for m in range(max(ALL + 3, last)):
                    if m == 0:
                        for j in jobs[m]:
                            job(*j)
                    if m < ALL:
                        scores(m)
                    if m > 0:
                        for j in jobs.get(m, []):
                            job(*j)
                    if 0 <= m - 2 < ALL:
                        turn(m - 2)
                    if 0 <= m - 3 < ALL:
                        weigh(m - 3)

            @block.scalar
            def _(act):
                def save(what, b, n):
                    act.wait_ge(job_ready, turn_of[what, b, n] + 1)
                    if what == "qk":
                        if b >= 2:
                            act.wait_ge(scores_ready, HEADS * (b - 2) + 4 * n + 4)
                        act.activation(q[:, b % 2, n, :], px[:, 0:SEQ], ACT.Identity, bias=bq[:, n:n + 1], scale=SCALE)
                        act.activation(k[:, b % 2, n, :], px[:, SEQ:], ACT.Identity, bias=bk[:, n:n + 1]).then_inc(job_saved, 1)
                    else:
                        if b >= 2:
                            act.wait_ge(z_ready, HEADS * (b - 1))
                        act.activation(v[:, b % 2, n, :], px[:, :], ACT.Copy).then_inc(job_saved, 1)

                def exp(m):
                    act.wait_ge(max_ready, m + 1)
                    if m >= 3:
                        act.wait_ge(turn_ready, m - 2)
                    for t in range(2):
                        act.activation(prob[:, m % 3, t, :], ps[m % 3][:, t, :], ACT.Exp, bias=neg_max[:, m % 4, t:t + 1],
                                       accum_out=total[:, m % 4, t:t + 1]).then_inc(exp_ready, 1)

                def save_z(g):
                    b = g // Q
                    act.wait_ge(z_ready, 4 * g + 4)
                    if b >= 2 and g % Q == 0:
                        act.wait_ge(job_ready, turn_of["out", b - 2, 0] + 1)
                    act.activation(z[:, b % 2, g % Q, :], pz[g % 2][:, :], ACT.Identity, bias=bv[:, g % Q:g % Q + 1])\
                       .then_inc(z_saved, 1)

                for m in range(max(ALL + 4, last)):
                    now = [j for j in jobs.get(m, []) if j[0] != "out"]
                    if m == 0:
                        for j in now:
                            save(*j)
                    if m < ALL:
                        exp(m)
                    if m > 0:
                        for j in now:
                            save(*j)
                    if m >= 7 and m % 4 == 3 and m // 4 - 1 < ALL // 4:
                        save_z(m // 4 - 1)

            @block.vector
            def _(dve):
                link = Chain(dve, dve_step)
                for m in range(max(ALL + 2, last)):
                    if m < ALL:
                        dve.wait_ge(scores_ready, m + 1)
                        dve.tensor_reduce(neg_max[:, m % 4, :], ps[m % 3][:, :, :], AX.X, ALU.max, negate=True).then_inc(max_ready, 1)
                    if 1 <= m <= ALL:
                        n = m - 1
                        dve.wait_ge(exp_ready, 2 * n + 2)
                        link(dve.reciprocal(total[:, n % 4, :], total[:, n % 4, :]))
                        for t in range(2):
                            dve.tensor_scalar(prob[:, n % 3, t, :], prob[:, n % 3, t, :], total[:, n % 4, t:t + 1], None, ALU.mult)\
                               .then_inc(prob_ready, 1)
                    if 2 <= m < ALL + 2:
                        n = m - 2
                        dve.wait_ge(turn_ready, n + 1)
                        if n >= 2:
                            dve.wait_ge(z_ready, n - 1)
                        dve.tensor_copy(turned[:, n % 2, :, :], pt[n % 2][:, :, :]).then_inc(turned_saved, 1)
                    for what, b, n in jobs.get(m, []):
                        if what == "out":
                            rows = st.g[:, bass.ds(i * (2 * NB) + 2 * b, 2), :]
                            dve.wait_ge(job_ready, turn_of[what, b, n] + 1)
                            ins = dve.tensor_tensor(rows, px[:, 0:2 * P].rearrange("p (a b) -> p a b", a=2),
                                                    bo[:, :].unsqueeze(1).to_broadcast([P, 2, D]), ALU.add)
                            ins.then_inc(out_saved, 1)
                            dve.wait_ge(out_saved, b + 1)
                            dve.tensor_tensor(rows, rows, st.xn[:, bass.ds(i * (2 * NB) + 2 * b, 2), :], ALU.add)


def layer0_ffn(nc, c, st, a):
    E, F = 8, 256
    U = E * F // P
    attention16(nc, c, st, a)
    with ExitStack() as ctx:
        mem = Memory(nc, ctx)
        w1 = mem.sb("l0f_w1", [P, U, P])
        w2 = mem.sb("l0f_w2", [P, U, D])
        b1 = mem.sb("l0f_b1", [P, U])
        b2 = mem.sb("l0f_b2", [E, D])
        gw = mem.sb("l0f_gw", [P, E])
        gb = mem.sb("l0f_gb", [P, E])
        norms = mem.sb("l0f_norms", [P, 4, D])
        w_tok = mem.sb("l0f_w_tok", [P, BLK, E])
        h_tok = mem.sb("l0f_h_tok", [P, BLK, D])
        h_ch = mem.sb("l0f_h_ch", [P, TOK])
        load(nc, [(w1[:, :, :], a["L0_ffn_W1"]), (w2[:, :, :], a["L0_ffn_W2"]), (b1[:, :], a["L0_ffn_b1"]),
                  (b2[:, :], a["L0_ffn_b2"]), (gw[:, :], a["L0_ffn_gW"]), (gb[:, :], a["L0_ffn_gb"]),
                  (norms[:, 0, :], a["L0_ffn_ln1_g"]), (norms[:, 1, :], a["L0_ffn_ln1_b"]),
                  (norms[:, 2, :], a["L0_ffn_ln2_g"]), (norms[:, 3, :], a["L0_ffn_ln2_b"])])
        layer_norm(nc, c, "l0n1", st.g, h_tok, h_ch, norms[:, 0, :], norms[:, 1, :])
        top_two(nc, c, st, "l0r", h_ch, gw, gb, E, w_tok, softmax=True)
        experts(nc, c, st, "l0e", h_ch, w_tok, E, F // P, ACT.Relu, w1, w2, b1=b1, b2=b2, residual=h_tok)
        layer_norm(nc, c, "l0n2", st.g, st.g, None, norms[:, 2, :], norms[:, 3, :])


def layer1_attention(nc, c, st, a):
    INNER, STATES, TAPS = 256, 16, 4
    CH = INNER // P
    PAD = TAPS - 1
    NSEQ = GT // SEQ
    with ExitStack() as ctx:
        mem = Memory(nc, ctx)
        w_in = mem.sb("l1_w_in", [P, 2 * CH, P])
        conv_w = mem.sb("l1_conv_w", [P, CH, TAPS])
        conv_b = mem.sb("l1_conv_b", [P, CH])
        w_b = mem.sb("l1_w_b", [P, CH, STATES])
        w_c = mem.sb("l1_w_c", [STATES, CH, P])
        w_out = mem.sb("l1_w_out", [P, CH, D])
        load(nc, [(w_in[:, :, :], a["L1_attn_w_in"]), (conv_w[:, :, :], a["L1_attn_conv_w"]), (conv_b[:, :], a["L1_attn_conv_b"]),
                  (w_b[:, :, :], a["L1_attn_w_B"]), (w_c[:, :, :], a["L1_attn_w_C"]), (w_out[:, :, :], a["L1_attn_w_out"])])
        padded = mem.sb("l1_padded", [P, CH, NSEQ, PAD + SEQ])
        conv = mem.sb("l1_conv", [P, CH, NSEQ, SEQ])
        zs = mem.sb("l1_zs", [P, CH, GT])
        decay = mem.sb("l1_decay", [STATES, SEQ])
        drive = mem.sb("l1_drive", [STATES, NSEQ, SEQ])
        state = mem.sb("l1_state", [STATES, NSEQ, SEQ])
        yz = mem.sb("l1_yz", [P, CH, GT])
        p_in = [mem.psum(f"l1_p_in{n}", [P, NSEQ, SEQ]) for n in range(2 * CH)]
        p_b = mem.psum("l1_p_b", [STATES, NSEQ, SEQ])
        p_y = [mem.psum(f"l1_p_y{n}", [P, GT]) for n in range(CH)]
        p_o = mem.psum("l1_p_o", [P, GB, D])
        with phase(nc, ["l1_set"]) as (block, _, (l1_set,)):
            @block.gpsimd
            def _(pool):
                pool.memset(padded[:, :, :, :], 0.0).then_inc(l1_set, 1)
                pool.memset(decay[:, :], 0.9).then_inc(l1_set, 1)
                pool.wait_ge(l1_set, 2)
        names = ["l1_" + n for n in ("in_ready", "x_saved", "z_saved", "dve_step", "conv_ready", "xc_ready", "b_ready",
                                     "drive_ready", "state_ready", "y_ready", "yz_ready", "o_ready")]
        with phase(nc, names, GRP) as (block, i, sems):
            (in_ready, x_saved, z_saved, dve_step, conv_ready, xc_ready, b_ready, drive_ready, state_ready, y_ready,
             yz_ready, o_ready) = sems

            @block.tensor
            def _(pe):
                for n in range(2 * CH):
                    pe.matmul(p_in[n][:, :, :], w_in[:, n, :], st.xnt[:, bass.ds(i * GT, GT)], start=True, stop=True)\
                      .then_inc(in_ready, 1)
                for n in range(CH):
                    pe.wait_ge(xc_ready, n + 1)
                    ins = pe.matmul(p_b[:, :, :], w_b[:, n, :], conv[:, n, :, :], start=(n == 0), stop=(n == CH - 1))
                ins.then_inc(b_ready, 1)
                pe.wait_ge(state_ready, NSEQ)
                for n in range(CH):
                    pe.matmul(p_y[n][:, :], w_c[:, n, :], state[:, :, :], start=True, stop=True).then_inc(y_ready, 1)
                pe.wait_ge(yz_ready, CH)
                for j in range(GB):
                    for n in range(CH):
                        ins = pe.matmul(p_o[:, j, :], yz[:, n, j * P:(j + 1) * P], w_out[:, n, :],
                                        start=(n == 0), stop=(n == CH - 1))
                ins.then_inc(o_ready, 1)

            @block.scalar
            def _(act):
                for n in range(CH):
                    act.wait_ge(in_ready, n + 1)
                    act.activation(padded[:, n, :, PAD:], p_in[n][:, :, :], ACT.Copy).then_inc(x_saved, 1)
                for n in range(CH):
                    act.wait_ge(in_ready, CH + n + 1)
                    act.activation(zs[:, n, :].rearrange("p (a b) -> p a b", a=NSEQ), p_in[CH + n][:, :, :], ACT.Silu)\
                       .then_inc(z_saved, 1)
                for n in range(CH):
                    act.wait_ge(conv_ready, n + 1)
                    act.activation(conv[:, n, :, :], conv[:, n, :, :], ACT.Silu, bias=conv_b[:, n:n + 1]).then_inc(xc_ready, 1)
                act.wait_ge(b_ready, 1)
                act.activation(drive[:, :, :], p_b[:, :, :], ACT.Copy, scale=0.1).then_inc(drive_ready, 1)
                act.wait_ge(o_ready, 1)
                act.activation(st.s[:, bass.ds(i * GB, GB), :], p_o[:, :, :], ACT.Copy)

            @block.vector
            def _(dve):
                link = Chain(dve, dve_step)
                for n in range(CH):
                    dve.wait_ge(x_saved, n + 1)
                    out = conv[:, n, :, :]
                    for k in range(TAPS):
                        x = padded[:, n, :, k:k + SEQ]
                        if k == 0:
                            link(dve.tensor_scalar(out, x, conv_w[:, n, k:k + 1], None, ALU.mult))
                        else:
                            ins = dve.scalar_tensor_tensor(out, x, conv_w[:, n, k:k + 1], out, ALU.mult, ALU.add)
                            if k < TAPS - 1:
                                link(ins)
                    ins.then_inc(conv_ready, 1)
                dve.wait_ge(drive_ready, 1)
                for s in range(NSEQ):
                    dve.tensor_tensor_scan(state[:, s, :], decay[:, :], drive[:, s, :], 0.0, ALU.mult, ALU.add)\
                       .then_inc(state_ready, 1)
                for n in range(CH):
                    dve.wait_ge(y_ready, n + 1)
                    dve.wait_ge(z_saved, n + 1)
                    dve.tensor_tensor(yz[:, n, :], p_y[n][:, :], zs[:, n, :], ALU.mult).then_inc(yz_ready, 1)


def layer1_ffn(nc, c, st, a):
    E, H = 8, 256
    with ExitStack() as ctx:
        mem = Memory(nc, ctx)
        w1 = mem.sb("l1f_w1", [P, E * H // P, P])
        w3 = mem.sb("l1f_w3", [P, E * H // P, P])
        w2 = mem.sb("l1f_w2", [P, E * H // P, D])
        gw = mem.sb("l1f_gw", [P, E])
        w_tok = mem.sb("l1f_w_tok", [P, BLK, E])
        load(nc, [(w1[:, :, :], a["L1_ffn_W1"]), (w3[:, :, :], a["L1_ffn_W3"]), (w2[:, :, :], a["L1_ffn_W2"]),
                  (gw[:, :], a["L1_ffn_Wg"])])
        with ExitStack() as inner:
            mem = Memory(nc, inner)
            score = mem.sb("l1f_score", [P, E, BLK])
            chosen = mem.sb("l1f_chosen", [P, E, BLK])
            token_scores(nc, "l1f", st.xnt, gw, E, score)
            choose(nc, c, "l1c", score, chosen, E, TOK // E)
            softmax_of_chosen(nc, c, score, chosen, w_tok, E)
        experts(nc, c, st, "l1e", st.xnt, w_tok, E, H // P, ACT.Silu, w1, w2, w3=w3)


def softmax_of_chosen(nc, c, score, chosen, w_tok, n_exp):
    with ExitStack() as ctx:
        mem = Memory(nc, ctx)
        best = mem.sb("l1s_best", [P, n_exp])
        top = mem.sb("l1s_top", [P, n_exp])
        part = mem.sb("l1s_part", [P, n_exp])
        recip = mem.sb("l1s_recip", [P, n_exp])
        p_sum = mem.psum("l1s_sum", [P, n_exp])
        wide = [P, n_exp, BLK]
        with phase(nc, ["l1s_dve_step", "l1s_best_ready", "l1s_top_ready", "l1s_shifted", "l1s_exp_ready", "l1s_part_ready",
                        "l1s_sum_ready"]) as (block, _, sems):
            dve_step, best_ready, top_ready, shifted, exp_ready, part_ready, sum_ready = sems

            @block.vector
            def _(dve):
                link = Chain(dve, dve_step)
                dve.tensor_reduce(best[:, :], score[:, :, :], AX.X, ALU.max).then_inc(best_ready, 1)
                dve.wait_ge(top_ready, 1)
                dve.tensor_tensor(score[:, :, :], score[:, :, :], top[:, :].unsqueeze(2).to_broadcast(wide), ALU.subtract)\
                   .then_inc(shifted, 1)
                dve.wait_ge(exp_ready, 1)
                link(dve.tensor_tensor(score[:, :, :], score[:, :, :], chosen[:, :, :], ALU.mult))
                dve.tensor_reduce(part[:, :], score[:, :, :], AX.X, ALU.add).then_inc(part_ready, 1)
                dve.wait_ge(sum_ready, 1)
                link(dve.reciprocal(recip[:, :], p_sum[:, :]))
                link(dve.tensor_tensor(w_tok[:, :, :].rearrange("p b e -> p e b"), score[:, :, :],
                                       recip[:, :].unsqueeze(2).to_broadcast(wide), ALU.mult))

            @block.gpsimd
            def _(pool):
                pool.wait_ge(best_ready, 1)
                pool.partition_all_reduce(top[:, :], best[:, :], P, bass.bass_isa.ReduceOp.max).then_inc(top_ready, 1)

            @block.scalar
            def _(act):
                act.wait_ge(shifted, 1)
                act.activation(score[:, :, :], score[:, :, :], ACT.Exp).then_inc(exp_ready, 1)

            @block.tensor
            def _(pe):
                pe.wait_ge(part_ready, 1)
                pe.matmul(p_sum[:, :], c.ones[:, :], part[:, :], start=True, stop=True).then_inc(sum_ready, 1)


WINDOW = 16
BEFORE = (WINDOW - 1) // 2
PITCH = SEQ + WINDOW


def layer2_attention(nc, c, st, a):
    KG = 4
    CHUNKS = WINDOW // KG
    NB = 8
    with ExitStack() as ctx:
        mem = Memory(nc, ctx)
        band = nc.dram_tensor("l2_band", (BATCH * SEQ * PITCH,), F32, kind="Internal").ap()
        w1 = mem.sb("l2_w1", [P, D])
        w2 = mem.sb("l2_w2", [P, D])
        v = mem.sb("l2_v", [P, 1])
        v_diag = mem.sb("l2_v_diag", [P, WINDOW, WINDOW])
        zero = mem.sb("l2_zero", [P, 2, PITCH])
        padded = mem.sb("l2_padded", [P, 2, WINDOW - 1 + SEQ])
        load(nc, [(w1[:, :], a["L2_attn_w1"]), (w2[:, :], a["L2_attn_w2"]), (v[:, :], a["L2_attn_v"])])
        with phase(nc, ["l2_zero_set", "l2_band_cleared", "l2_v_placed"]) as (block, _, (zero_set, band_cleared, v_placed)):
            @block.vector
            def _(dve):
                dve.memset(zero[:, :, :], 0.0).then_inc(zero_set, 1)
                dve.memset(padded[:, :, :], 0.0).then_inc(zero_set, 1)
                dve.memset(v_diag[:, :, :], 0.0).then_inc(zero_set, 1)
                dve.wait_ge(zero_set, 3)
                diag = v_diag[:, :, :].rearrange("p a b -> p (a b)")[:, 0:WINDOW * WINDOW:WINDOW + 1]
                dve.tensor_copy(diag, v[:, 0:1].to_broadcast([P, WINDOW])).then_inc(v_placed, 1)

            @block.sync
            def _(sp):
                sp.wait_ge(zero_set, 3)
                for b in range(BATCH):
                    rows = band[b * SEQ * PITCH:(b + 1) * SEQ * PITCH].rearrange("(t p n) -> p t n", t=2, p=P)
                    sp.dma_start(rows, zero[:, :, :]).then_inc(band_cleared, 16)
                sp.wait_ge(band_cleared, 16 * BATCH)

        with ExitStack() as inner:
            mem = Memory(nc, inner)
            q = mem.sb("l2_q", [P, 2, SEQ])
            th = mem.sb("l2_tanh", [P, 2, WINDOW, SEQ])
            score = mem.sb("l2_score", [WINDOW, 2, SEQ])
            prob = mem.sb("l2_prob", [P, 2 * NB, WINDOW])
            small = mem.sb("l2_small", [P, 2 * NB])
            pp = [mem.psum(f"l2_pp{n}", [P, 2, SEQ]) for n in range(2)]
            ps = [mem.psum(f"l2_ps{n}", [WINDOW, SEQ]) for n in range(2)]
            pw = mem.psum("l2_pw", [P, 2 * NB, WINDOW])
            names = ["l2_" + n for n in ("proj_ready", "pq_saved", "sum_ready", "tanh_ready", "tanh_used",
                                         "score_saved", "score_turned", "dve_step", "shifted", "exp_ready", "weight_ready",
                                         "stored")]
            with phase(nc, names, BATCH // NB) as (block, i, sems):
                (proj_ready, pq_saved, sum_ready, tanh_ready, tanh_used, score_saved, score_turned, dve_step,
                 shifted, exp_ready, weight_ready, stored) = sems

                @block.tensor
                def _(pe):
                    def project(b):
                        if b >= 2:
                            pe.wait_ge(pq_saved, 2 * (b - 1))
                        x = st.xnt[:, bass.ds(i * (NB * SEQ) + b * SEQ, SEQ)]
                        pe.matmul(pp[b % 2][:, 0, :], w2[:, :], x, start=True, stop=True)
                        pe.matmul(pp[b % 2][:, 1, :], w1[:, :], x, start=True, stop=True).then_inc(proj_ready, 1)

                    def turn(b):
                        pe.wait_ge(score_saved, b + 1)
                        for t in range(2):
                            ins = pe.transpose(pw[:, 2 * b + t, :], score[:, b % 2, t * P:(t + 1) * P],
                                               c.ident[0:WINDOW, 0:WINDOW])
                        ins.then_inc(score_turned, 1)

                    project(0)
                    for b in range(NB):
                        if b + 1 < NB:
                            project(b + 1)
                        if b >= 2:
                            pe.wait_ge(score_saved, b - 1)
                        for k in range(WINDOW):
                            if k % KG == 0:
                                pe.wait_ge(tanh_ready, CHUNKS * b + k // KG + 1)
                            ins = pe.matmul(ps[b % 2][:, :], v_diag[:, k, :], th[:, b % 2, k, :], start=(k == 0),
                                            stop=(k == WINDOW - 1))
                            if k % KG == KG - 1:
                                ins.then_inc(tanh_used, 1)
                        if b >= 1:
                            turn(b - 1)
                    turn(NB - 1)

                @block.scalar
                def _(act):
                    def save(b):
                        act.wait_ge(proj_ready, b + 1)
                        if b >= 2:
                            act.wait_ge(sum_ready, CHUNKS * (b - 1))
                        act.activation(padded[:, b % 2, BEFORE:BEFORE + SEQ], pp[b % 2][:, 0, :], ACT.Copy).then_inc(pq_saved, 1)
                        act.activation(q[:, b % 2, :], pp[b % 2][:, 1, :], ACT.Copy).then_inc(pq_saved, 1)

                    save(0)
                    for b in range(NB):
                        for n in range(CHUNKS):
                            act.wait_ge(sum_ready, CHUNKS * b + n + 1)
                            part = th[:, b % 2, n * KG:(n + 1) * KG, :]
                            act.activation(part, part, ACT.Tanh).then_inc(tanh_ready, 1)
                            if n == 1 and b + 1 < NB:
                                save(b + 1)
                    act.wait_ge(shifted, 1)
                    act.activation(prob[:, :, :], prob[:, :, :], ACT.Exp).then_inc(exp_ready, 1)

                @block.vector
                def _(dve):
                    link = Chain(dve, dve_step)

                    def save_scores(b):
                        dve.wait_ge(tanh_used, CHUNKS * (b + 1))
                        if b >= 2:
                            dve.wait_ge(score_turned, b - 1)
                        dve.tensor_copy(score[:, b % 2, :], ps[b % 2][:, :]).then_inc(score_saved, 1)

                    for b in range(NB):
                        dve.wait_ge(pq_saved, 2 * (b + 1))
                        for n in range(CHUNKS):
                            if b >= 2:
                                dve.wait_ge(tanh_used, CHUNKS * (b - 2) + n + 1)
                            one = padded[:, b % 2, n * KG:n * KG + SEQ]
                            windows = bass.AP(one.tensor, one.offset, [one.ap[0], [1, KG], [1, SEQ]])
                            dve.tensor_tensor(th[:, b % 2, n * KG:(n + 1) * KG, :], windows,
                                              q[:, b % 2, :].unsqueeze(1).to_broadcast([P, KG, SEQ]), ALU.add)\
                               .then_inc(sum_ready, 1)
                        if b >= 1:
                            save_scores(b - 1)
                    save_scores(NB - 1)
                    spread = small[:, :].unsqueeze(2).to_broadcast([P, 2 * NB, WINDOW])
                    dve.wait_ge(score_turned, NB)
                    link(dve.tensor_reduce(small[:, :], pw[:, :, :], AX.X, ALU.max))
                    dve.tensor_tensor(prob[:, :, :], pw[:, :, :], spread, ALU.subtract).then_inc(shifted, 1)
                    dve.wait_ge(exp_ready, 1)
                    link(dve.tensor_reduce(small[:, :], prob[:, :, :], AX.X, ALU.add))
                    link(dve.reciprocal(small[:, :], small[:, :]))
                    dve.tensor_tensor(prob[:, :, :], prob[:, :, :], spread, ALU.mult).then_inc(weight_ready, 1)

                @block.sync
                def _(sp):
                    sp.wait_ge(weight_ready, 1)
                    for b in range(NB):
                        rows = band[bass.ds(i * (NB * SEQ * PITCH) + b * (SEQ * PITCH), SEQ * PITCH)]
                        dst = bass.AP(rows.tensor, rows.offset, [[PITCH + 1, P], [P * (PITCH + 1), 2], [1, WINDOW]])
                        sp.dma_start(dst, prob[:, 2 * b:2 * b + 2, :]).then_inc(stored, 16)
                    sp.wait_ge(stored, 16 * NB)

        with ExitStack() as inner:
            mem = Memory(nc, inner)
            rows_sb = mem.sb("l2_rows", [P, 2 * NB, SEQ])
            turned = mem.sb("l2_turned", [P, 2, 4, P])
            pt = [mem.psum(f"l2_pt{n}", [P, 4, P]) for n in range(2)]
            po = [mem.psum(f"l2_po{n}", [P, 2, D]) for n in range(2)]
            PARTS = 4
            names = ["l2_" + n for n in ("loaded0", "loaded1", "loaded2", "loaded3", "turn_ready", "turn_saved", "out_ready",
                                         "out_saved")]
            with phase(nc, names, BATCH // NB) as (block, i, sems):
                loaded, (turn_ready, turn_saved, out_ready, out_saved) = sems[:PARTS], sems[PARTS:]
                PER = NB // PARTS

                @block.sync
                def _(sp):
                    for part in range(PARTS):
                        src = band[bass.ds(i * (NB * SEQ * PITCH) + part * (PER * SEQ * PITCH), PER * SEQ * PITCH)]
                        src = src.rearrange("(n p w) -> p n w", p=P, w=PITCH)
                        sp.dma_start(rows_sb[:, 2 * PER * part:2 * PER * (part + 1), :], src[:, :, BEFORE:BEFORE + SEQ])\
                          .then_inc(loaded[part], 16)

                @block.tensor
                def _(pe):
                    def turn(b):
                        pe.wait_ge(loaded[b // PER], 16)
                        if b >= 2:
                            pe.wait_ge(turn_saved, b - 1)
                        for t in range(2):
                            for s in range(2):
                                ins = pe.transpose(pt[b % 2][:, 2 * t + s, :], rows_sb[:, 2 * b + t, s * P:(s + 1) * P], c.ident[:, :])
                        ins.then_inc(turn_ready, 1)

                    def weigh(b):
                        pe.wait_ge(turn_saved, b + 1)
                        if b >= 2:
                            pe.wait_ge(out_saved, b - 1)
                        for t in range(2):
                            for s in range(2):
                                ins = pe.matmul(po[b % 2][:, t, :], turned[:, b % 2, 2 * t + s, :],
                                                st.xn[:, i * (2 * NB) + 2 * b + s, :], start=(s == 0), stop=(s == 1))
                        ins.then_inc(out_ready, 1)

                    for b in range(NB + 1):
                        if b < NB:
                            turn(b)
                        if b >= 1:
                            weigh(b - 1)

                @block.vector
                def _(dve):
                    for b in range(NB):
                        dve.wait_ge(turn_ready, b + 1)
                        if b >= 2:
                            dve.wait_ge(out_ready, b - 1)
                        dve.tensor_copy(turned[:, b % 2, :, :], pt[b % 2][:, :, :]).then_inc(turn_saved, 1)

                @block.scalar
                def _(act):
                    for b in range(NB):
                        act.wait_ge(out_ready, b + 1)
                        act.activation(st.s[:, bass.ds(i * (2 * NB) + 2 * b, 2), :], po[b % 2][:, :, :], ACT.Copy)\
                           .then_inc(out_saved, 1)


def layer2_ffn(nc, c, st, a):
    E, F = 8, 512
    U = E * F // P
    with ExitStack() as ctx:
        mem = Memory(nc, ctx)
        w1 = mem.sb("l2f_w1", [P, U, P])
        w2 = mem.sb("l2f_w2", [P, U, D])
        b1 = mem.sb("l2f_b1", [P, U])
        b2 = mem.sb("l2f_b2", [E, D])
        cent = mem.sb("l2f_cent", [P, E])
        gain = mem.sb("l2f_gain", [P, D])
        shift = mem.sb("l2f_shift", [P, D])
        w_tok = mem.sb("l2f_w_tok", [P, BLK, E])
        norm_ch = mem.sb("l2f_norm_ch", [P, TOK])
        load(nc, [(w1[:, :, :], a["L2_ffn_w1"]), (w2[:, :, :], a["L2_ffn_w2"]), (b1[:, :], a["L2_ffn_b1"]),
                  (b2[:, :], a["L2_ffn_b2"]), (cent[:, :], a["L2_ffn_centroids"]), (gain[:, :], a["L2_ffn_ln_g"]),
                  (shift[:, :], a["L2_ffn_ln_b"])])
        layer_norm(nc, c, "l2n", st.xn, None, norm_ch, gain[:, :], shift[:, :])
        with ExitStack() as inner:
            mem = Memory(nc, inner)
            score = mem.sb("l2f_score", [P, E, BLK])
            chosen = mem.sb("l2f_chosen", [P, E, BLK])
            token_scores(nc, "l2f", norm_ch, cent, E, score)
            choose(nc, c, "l2c", score, chosen, E, TOK // E, in_turn=True)
            with phase(nc, ["l2f_w_ready"]) as (block, _, (w_ready,)):
                @block.vector
                def _(dve):
                    dve.tensor_copy(w_tok[:, :, :], chosen[:, :, :].rearrange("p e b -> p b e")).then_inc(w_ready, 1)
        experts(nc, c, st, "l2e", norm_ch, w_tok, E, F // P, ACT.Gelu_apprx_tanh, w1, w2, b1=b1, b2=b2, residual=st.xn)


def layer3_attention(nc, c, st, a):
    HEADS, HD = 16, 64
    PAIRS = HEADS // 2
    HALF = HEADS * HD // 2
    NB = 4
    ALL = NB * HEADS
    PLAN = [("qk", n, 2 * n - 4) for n in range(PAIRS)] + [("v", n, 2 * n - 3) for n in range(4)] + [("out", 0, HEADS + 5)]
    jobs = {}
    for b in range(NB):
        for what, n, at in PLAN:
            jobs.setdefault(max(b * HEADS + at, 0), []).append((what, b, n))
    last = max(jobs) + 1
    order = [job for t in sorted(jobs) for job in jobs[t]]
    turn_of = {job: n for n, job in enumerate(order)}
    by_act = [sum(j[0] != "out" for j in order[:n]) for n in range(len(order) + 1)]
    by_dve = [sum(j[0] != "v" for j in order[:n]) for n in range(len(order) + 1)]
    with ExitStack() as ctx:
        mem = Memory(nc, ctx)
        wq = mem.sb("l3_wq", [P, PAIRS, P])
        wk = mem.sb("l3_wk", [P, PAIRS, P])
        wv = mem.sb("l3_wv", [P, HEADS * HD])
        wo = mem.sb("l3_wo", [P, PAIRS, D])
        bq = mem.sb("l3_bq", [P, PAIRS])
        bk = mem.sb("l3_bk", [P, PAIRS])
        bv = mem.sb("l3_bv", [P, PAIRS])
        bo = mem.sb("l3_bo", [P, D])
        load(nc, [(wq[:, :, :], a["L3_attn_W_Q"]), (wk[:, :, :], a["L3_attn_W_K"]), (wv[:, :], a["L3_attn_W_V"]),
                  (wo[:, :, :], a["L3_attn_W_O"]), (bq[:, :], a["L3_attn_b_Q"]), (bk[:, :], a["L3_attn_b_K"]),
                  (bv[:, :], a["L3_attn_b_V"]), (bo[:, :], a["L3_attn_b_O"])])
        bq8 = mem.sb("l3_bq8", [P, PAIRS])
        with phase(nc, ["l3_bias_ready"]) as (block, _, (bias_ready,)):
            @block.vector
            def _(dve):
                dve.tensor_scalar(bq8[:, :], bq[:, :], 1 / 8, None, ALU.mult).then_inc(bias_ready, 1)
        xs = mem.sb("l3_x", [P, 2, SEQ])
        q = mem.sb("l3_q", [P, 2, PAIRS, SEQ])
        k = mem.sb("l3_k", [P, 2, PAIRS, SEQ])
        v = mem.sb("l3_v", [P, 2, 2, HEADS * HD])
        prob = mem.sb("l3_prob", [P, 3, 3 * P])
        turned = mem.sb("l3_prob_t", [P, 2, 3 * P])
        neg_max = mem.sb("l3_neg_max", [P, 4, 2])
        total = mem.sb("l3_total", [P, 4, 2])
        z = mem.sb("l3_z", [P, 2, PAIRS, SEQ])
        ps = [mem.psum(f"l3_ps{n}", [P, 512]) for n in range(3)]
        pt = [mem.psum(f"l3_pt{n}", [P, 512]) for n in range(2)]
        pz = [mem.psum(f"l3_pz{n}", [P, 512]) for n in range(2)]
        px = mem.psum("l3_px", [P, 512])
        names = ["l3_" + n for n in ("x_ready", "job_ready", "job_saved", "k_saved", "scores_ready", "max_ready", "exp_ready",
                                     "dve_step", "prob_ready", "turn_ready", "turned_saved", "z_ready", "z_saved")]
        with phase(nc, names, BATCH // NB) as (block, i, sems):
            (x_ready, job_ready, job_saved, k_saved, scores_ready, max_ready, exp_ready, dve_step, prob_ready, turn_ready,
             turned_saved, z_ready, z_saved) = sems

            @block.gpsimd
            def _(pool):
                for b in range(NB):
                    if b >= 2:
                        pool.wait_ge(job_ready, turn_of["qk", b - 2, PAIRS - 1] + 1)
                    pool.tensor_copy(xs[:, b % 2, :], st.xnt[:, bass.ds(i * (NB * SEQ) + b * SEQ, SEQ)]).then_inc(x_ready, 1)

            @block.tensor
            def _(pe):
                def job(what, b, n):
                    m = turn_of[what, b, n]
                    if by_act[m]:
                        pe.wait_ge(job_saved, by_act[m])
                    if by_dve[m]:
                        pe.wait_ge(k_saved, by_dve[m])
                    if what == "out":
                        pe.wait_ge(z_saved, PAIRS * (b + 1))
                        for t in range(2):
                            for g in range(PAIRS):
                                ins = pe.matmul(px[:, t * P:(t + 1) * P], z[:, b % 2, g, t * P:(t + 1) * P], wo[:, g, :],
                                                start=(g == 0), stop=(g == PAIRS - 1))
                    else:
                        pe.wait_ge(x_ready, b + 1)
                        x = xs[:, b % 2, :]
                    if what == "qk":
                        pe.matmul(px[:, 0:SEQ], wq[:, n, :], x, start=True, stop=True)
                        ins = pe.matmul(px[:, SEQ:], wk[:, n, :], x, start=True, stop=True)
                    if what == "v":
                        t, half = n % 2, n // 2
                        ins = pe.matmul(px[:, :], x[:, t * P:(t + 1) * P], wv[:, half * HALF:(half + 1) * HALF],
                                        start=True, stop=True)
                    ins.then_inc(job_ready, 1)

                def scores(m):
                    b, h = m // HEADS, m % HEADS
                    if h % 2 == 0:
                        done = turn_of["qk", b, h // 2] + 1
                        pe.wait_ge(job_saved, by_act[done])
                        pe.wait_ge(k_saved, by_dve[done])
                    if m >= 3:
                        pe.wait_ge(exp_ready, 2 * (m - 2))
                    rows = slice(HD * (h % 2), HD * (h % 2) + HD)
                    out, qh, kh = ps[m % 3], q[rows, b % 2, h // 2, :], k[rows, b % 2, h // 2, :]
                    pe.matmul(out[:, 0:P], qh[:, 0:P], kh[:, 0:P], start=True, stop=False)
                    pe.matmul(out[:, 0:P], c.ident_bf[:, :], c.future[:, :], start=False, stop=True)
                    pe.matmul(out[:, P:3 * P], qh[:, P:], kh[:, :], start=True, stop=False, skip_group_check=True)
                    pe.matmul(out[:, 2 * P:3 * P], c.ident_bf[:, :], c.future[:, :], start=False, stop=True,
                              skip_group_check=True).then_inc(scores_ready, 1)

                def turn(m):
                    pe.wait_ge(prob_ready, 2 * m + 2)
                    if m >= 2:
                        pe.wait_ge(turned_saved, m - 1)
                    for j in range(3):
                        ins = pe.transpose(pt[m % 2][:, j * P:(j + 1) * P], prob[:, m % 3, j * P:(j + 1) * P], c.ident[:, :])
                    ins.then_inc(turn_ready, 1)

                def weigh(m):
                    b, h = m // HEADS, m % HEADS
                    n, rows = m // 2, slice(HD * (h % 2), HD * (h % 2) + HD)
                    if h % 8 == 0:
                        pe.wait_ge(job_saved, by_act[turn_of["v", b, 2 * (h // 8) + 1] + 1])
                    if h % 2 == 0 and n >= 2:
                        pe.wait_ge(z_saved, n - 1)
                    pe.wait_ge(turned_saved, m + 1)
                    out, cols = pz[n % 2], slice(h * HD, (h + 1) * HD)
                    pe.matmul(out[rows, 0:SEQ], v[:, b % 2, 0, cols], turned[:, m % 2, 0:SEQ], start=True, stop=False,
                              skip_group_check=True)
                    pe.matmul(out[rows, P:SEQ], v[:, b % 2, 1, cols], turned[:, m % 2, SEQ:], start=False, stop=True,
                              skip_group_check=True).then_inc(z_ready, 1)

                for m in range(max(ALL + 3, last)):
                    if m == 0:
                        for j in jobs[m]:
                            job(*j)
                    if m < ALL:
                        scores(m)
                    if m > 0:
                        for j in jobs.get(m, []):
                            job(*j)
                    if 0 <= m - 2 < ALL:
                        turn(m - 2)
                    if 0 <= m - 3 < ALL:
                        weigh(m - 3)

            @block.scalar
            def _(act):
                def save(what, b, n):
                    act.wait_ge(job_ready, turn_of[what, b, n] + 1)
                    if what == "qk":
                        if b >= 2:
                            act.wait_ge(scores_ready, HEADS * (b - 2) + 2 * n + 2)
                        act.activation(q[:, b % 2, n, :], px[:, 0:SEQ], ACT.Identity, bias=bq8[:, n:n + 1], scale=1 / 8)\
                           .then_inc(job_saved, 1)
                    else:
                        t, half = n % 2, n // 2
                        if b >= 2:
                            act.wait_ge(z_ready, HEADS * (b - 1))
                        act.activation(v[:, b % 2, t, half * HALF:(half + 1) * HALF], px[:, :], ACT.Copy).then_inc(job_saved, 1)

                def exp(m):
                    act.wait_ge(max_ready, 2 * m + 2)
                    if m >= 3:
                        act.wait_ge(turn_ready, m - 2)
                    row = prob[:, m % 3, :]
                    act.activation(row[:, 0:P], ps[m % 3][:, 0:P], ACT.Exp, bias=neg_max[:, m % 4, 0:1],
                                   accum_out=total[:, m % 4, 0:1]).then_inc(exp_ready, 1)
                    act.activation(row[:, P:], ps[m % 3][:, P:3 * P], ACT.Exp, bias=neg_max[:, m % 4, 1:2],
                                   accum_out=total[:, m % 4, 1:2]).then_inc(exp_ready, 1)

                def save_z(g):
                    b, n = g // PAIRS, g % PAIRS
                    act.wait_ge(z_ready, 2 * g + 2)
                    if b >= 2 and n == 0:
                        act.wait_ge(job_ready, turn_of["out", b - 2, 0] + 1)
                    act.activation(z[:, b % 2, n, :], pz[g % 2][:, 0:SEQ], ACT.Identity, bias=bv[:, n:n + 1]).then_inc(z_saved, 1)

                for m in range(max(ALL + 4, last)):
                    now = [j for j in jobs.get(m, []) if j[0] != "out"]
                    if m == 0:
                        for j in now:
                            save(*j)
                    if m < ALL:
                        exp(m)
                    if m > 0:
                        for j in now:
                            save(*j)
                    if m >= 5 and m % 2 == 1 and (m - 5) // 2 < ALL // 2:
                        save_z((m - 5) // 2)

            @block.vector
            def _(dve):
                link = Chain(dve, dve_step)

                def save(what, b, n):
                    if what != "v":
                        dve.wait_ge(job_ready, turn_of[what, b, n] + 1)
                    if what == "qk":
                        if b >= 2:
                            dve.wait_ge(scores_ready, HEADS * (b - 2) + 2 * n + 2)
                        dve.wait_ge(job_saved, by_act[turn_of[what, b, n] + 1])
                        dve.tensor_scalar(k[:, b % 2, n, :], px[:, SEQ:], bk[:, n:n + 1], None, ALU.add).then_inc(k_saved, 1)
                    if what == "out":
                        dve.tensor_tensor(st.s[:, bass.ds(i * (2 * NB) + 2 * b, 2), :],
                                          px[:, 0:2 * P].rearrange("p (a b) -> p a b", a=2),
                                          bo[:, :].unsqueeze(1).to_broadcast([P, 2, D]), ALU.add).then_inc(k_saved, 1)

                for m in range(max(ALL + 2, last)):
                    if m == 0:
                        for job in jobs[m]:
                            save(*job)
                    if m < ALL:
                        dve.wait_ge(scores_ready, m + 1)
                        dve.tensor_reduce(neg_max[:, m % 4, 0:1], ps[m % 3][:, 0:P], AX.X, ALU.max, negate=True).then_inc(max_ready, 1)
                        dve.tensor_reduce(neg_max[:, m % 4, 1:2], ps[m % 3][:, P:3 * P], AX.X, ALU.max, negate=True)\
                           .then_inc(max_ready, 1)
                    if 1 <= m <= ALL:
                        n = m - 1
                        dve.wait_ge(exp_ready, 2 * n + 2)
                        link(dve.reciprocal(total[:, n % 4, :], total[:, n % 4, :]))
                        row = prob[:, n % 3, :]
                        dve.tensor_scalar(row[:, 0:P], row[:, 0:P], total[:, n % 4, 0:1], None, ALU.mult).then_inc(prob_ready, 1)
                        dve.tensor_scalar(row[:, P:], row[:, P:], total[:, n % 4, 1:2], None, ALU.mult).then_inc(prob_ready, 1)
                    if 2 <= m < ALL + 2:
                        n = m - 2
                        dve.wait_ge(turn_ready, n + 1)
                        if n >= 2:
                            dve.wait_ge(z_ready, n - 1)
                        dve.tensor_copy(turned[:, n % 2, :], pt[n % 2][:, 0:3 * P]).then_inc(turned_saved, 1)
                    if m > 0:
                        for job in jobs.get(m, []):
                            save(*job)


def layer3_ffn(nc, c, st, a):
    E = 6
    with ExitStack() as ctx:
        mem = Memory(nc, ctx)
        w1 = mem.sb("l3f_w1", [P, E + 1, P])
        w3 = mem.sb("l3f_w3", [P, E + 1, P])
        w2 = mem.sb("l3f_w2", [P, E + 1, D])
        gw = mem.sb("l3f_gw", [P, E])
        gb = mem.sb("l3f_gb", [P, E])
        w_tok = mem.sb("l3f_w_tok", [P, BLK, E + 1])
        load(nc, [(w1[:, 0:E, :], a["L3_ffn_ew1"]), (w3[:, 0:E, :], a["L3_ffn_ew3"]), (w2[:, 0:E, :], a["L3_ffn_ew2"]),
                  (w1[:, E, :], a["L3_ffn_fc1"]), (w3[:, E, :], a["L3_ffn_fc2"]), (w2[:, E, :], a["L3_ffn_fc3"]),
                  (gw[:, :], a["L3_ffn_gate_w"]), (gb[:, :], a["L3_ffn_gate_b"])])
        top_two(nc, c, st, "l3r", st.xnt, gw, gb, E, w_tok, softmax=False)
        with phase(nc, ["shared_weight"]) as (block, _, (shared_weight,)):
            @block.gpsimd
            def _(pool):
                pool.memset(w_tok[:, :, E:E + 1], 1.0).then_inc(shared_weight, 1)
                pool.wait_ge(shared_weight, 1)
        experts(nc, c, st, "l3e", st.xnt, w_tok, E + 1, 1, ACT.Silu, w1, w2, w3=w3)


def gated_stack(nc, a, out):
    with ExitStack() as ctx:
        mem = Memory(nc, ctx)
        c, st = Constants(mem), State(mem)
        constants(nc, c)
        load(nc, [(st.x[:, :, :], a["x"])])
        layers = ((layer0_attention, layer0_ffn), (layer1_attention, layer1_ffn), (layer2_attention, layer2_ffn),
                  (layer3_attention, layer3_ffn))
        for n, (mixer, ffn) in enumerate(layers):
            layer_norm(nc, c, f"norm{n}", st.x, st.xn, st.xnt, combined=st if n else None)
            mixer(nc, c, st, a)
            ffn(nc, c, st, a)
        finish(nc, st, out)



def heads_in(w):
    n, m, d = w.shape
    return w.transpose(1, 0, 2).reshape(m, n * d // 128, 128)
def rows(b, n=128):
    return np.broadcast_to(b, (n,) + b.shape)
def units_t(w):
    e, f, ch = w.shape
    return w.transpose(2, 0, 1).reshape(ch, e * f // 128, 128)
def units(w):
    e, ch, f = w.shape
    return w.transpose(1, 0, 2).reshape(ch, e * f // 128, 128)
def down(w):
    e, f, o = w.shape
    return w.reshape(e * f // 128, 128, o).transpose(1, 0, 2)
def layout(i):
    o = {}
    o["x"] = i["L0_attn_hidden_states"].reshape(32, 128, 128).transpose(1, 0, 2)
    for n in ("Q", "K"):
        o[f"L3_attn_W_{n}"] = heads_in(i[f"L3_attn_W_{n}"])
        o[f"L3_attn_b_{n}"] = i[f"L3_attn_b_{n}"].reshape(8, 128).T
    o["L3_attn_W_V"] = heads_in(i["L3_attn_W_V"]).reshape(128, 1024)
    o["L3_attn_b_V"] = i["L3_attn_b_V"].reshape(8, 128).T
    o["L3_attn_W_O"] = i["L3_attn_W_O"].reshape(8, 128, 128).transpose(1, 0, 2)
    o["L3_attn_b_O"] = rows(i["L3_attn_b_O"])
    o["L3_ffn_ew1"] = units_t(i["L3_ffn_ew1"])
    o["L3_ffn_ew3"] = units_t(i["L3_ffn_ew3"])
    o["L3_ffn_ew2"] = i["L3_ffn_ew2"].transpose(2, 0, 1)
    o["L3_ffn_fc1"] = i["L3_ffn_fc1"].T
    o["L3_ffn_fc2"] = i["L3_ffn_fc2"].T
    o["L3_ffn_fc3"] = i["L3_ffn_fc3"].T
    o["L3_ffn_gate_w"] = i["L3_ffn_gate_w"].T
    o["L3_ffn_gate_b"] = rows(i["L3_ffn_gate_b"])
    for n in ("Wq", "Wk", "Wv", "Wb", "Wmix", "Wo"):
        o[f"L0_attn_{n}"] = i[f"L0_attn_{n}"].T
    o["L0_attn_Wb_wide"] = np.repeat(i["L0_attn_Wb"].T, 32, axis=1)
    for n in ("q", "k", "v"):
        o[f"L0_attn_conv_{n}"] = i[f"L0_attn_conv_{n}"]
    o["L0_attn_norm_w"] = np.broadcast_to(i["L0_attn_norm_w"], (4, 32)).reshape(128, 1)
    for n in ("Wq", "Wk", "Wv"):
        o[f"L0_ffn_{n}"] = i[f"L0_ffn_{n}"].reshape(128, 16, 8)
    for n in ("bq", "bk", "bv"):
        o[f"L0_ffn_{n}"] = i[f"L0_ffn_{n}"].reshape(4, 4, 8).transpose(1, 2, 0)
    o["L0_ffn_Wo"] = i["L0_ffn_Wo"].reshape(4, 4, 8, 128).transpose(1, 2, 0, 3)
    for n in ("bo", "gb", "ln1_g", "ln1_b", "ln2_g", "ln2_b"):
        o[f"L0_ffn_{n}"] = rows(i[f"L0_ffn_{n}"])
    o["L0_ffn_W1"] = units(i["L0_ffn_W1"])
    o["L0_ffn_b1"] = i["L0_ffn_b1"].reshape(16, 128).T
    o["L0_ffn_W2"] = down(i["L0_ffn_W2"])
    o["L0_ffn_b2"], o["L0_ffn_gW"] = i["L0_ffn_b2"], i["L0_ffn_gW"]
    o["L1_attn_w_in"] = i["L1_attn_w_in"].reshape(128, 4, 128)
    o["L1_attn_conv_w"] = i["L1_attn_conv_w"].reshape(2, 128, 4).transpose(1, 0, 2)
    o["L1_attn_conv_b"] = i["L1_attn_conv_b"].reshape(2, 128).T
    o["L1_attn_w_B"] = i["L1_attn_w_B"].reshape(2, 128, 16).transpose(1, 0, 2)
    o["L1_attn_w_C"] = i["L1_attn_w_C"].reshape(16, 2, 128)
    o["L1_attn_w_out"] = i["L1_attn_w_out"].reshape(2, 128, 128).transpose(1, 0, 2)
    o["L1_ffn_W1"] = units_t(i["L1_ffn_W1"])
    o["L1_ffn_W3"] = units_t(i["L1_ffn_W3"])
    o["L1_ffn_W2"] = down(i["L1_ffn_W2"].transpose(0, 2, 1))
    o["L1_ffn_Wg"] = i["L1_ffn_Wg"].T
    o["L2_attn_w1"] = i["L2_attn_w1"]
    o["L2_attn_w2"] = i["L2_attn_w2"]
    o["L2_attn_v"] = i["L2_attn_v"]
    o["L2_ffn_centroids"] = i["L2_ffn_centroids"].T
    o["L2_ffn_ln_g"] = rows(i["L2_ffn_ln_g"])
    o["L2_ffn_ln_b"] = rows(i["L2_ffn_ln_b"])
    o["L2_ffn_w1"] = units(i["L2_ffn_w1"])
    o["L2_ffn_b1"] = i["L2_ffn_b1"].reshape(32, 128).T
    o["L2_ffn_w2"] = down(i["L2_ffn_w2"])
    o["L2_ffn_b2"] = i["L2_ffn_b2"]
    return o


def kernel(**inputs):
    import concourse.bacc as _bacc
    from concourse.bass_utils import run_bass_kernel_spmd as _run

    nc = _bacc.Bacc("TRN2", target_bir_lowering=False, num_devices=1)
    arrays, aps = {}, {}
    for name, array in layout({k: np.asarray(v) for k, v in inputs.items()}).items():
        array = np.ascontiguousarray(array)
        arrays[f"in_{name}_dram"] = array
        aps[name] = nc.dram_tensor(f"in_{name}_dram", array.shape, mybir.dt.from_np(array.dtype), kind="ExternalInput").ap()
    out = nc.dram_tensor("out_0_dram", (BATCH, SEQ, D), F32, kind="ExternalOutput").ap()
    gated_stack(nc, aps, out)
    r = _run(nc, [arrays], core_ids=[0])
    return r.results[0]["out_0_dram"]
```
